# Optimizing a Trainium2 kernel written in Bass

```python
import numpy as np
import jax
import jax.numpy as jnp

def _softmax(x, axis=-1):
    return jax.nn.softmax(x, axis=axis)

def _gelu(x):
    return jax.nn.gelu(x, approximate=True)

def _silu(x):
    return jax.nn.silu(x)

def _sigmoid(x):
    return jax.nn.sigmoid(x)

def _layernorm(x, axis=-1, eps=1e-05):
    m = jnp.mean(x, axis=axis, keepdims=True)
    v = jnp.var(x, axis=axis, keepdims=True)
    return (x - m) / jnp.sqrt(v + eps)

def _scatter_add(tgt, idx, src, axis=0):
    return tgt.at[idx].add(src)

def _segment_sum(src, seg, n):
    return jax.ops.segment_sum(src, seg, n)
kernel_name = 'mk_adaln_d1_jaxref_r8_442876'

def setup_inputs(seed: int=0):
    np.random.seed(seed)
    _w = jnp.asarray

    def _L0_attn_setup():
        import jax, jax.numpy as jnp
        import numpy as np
        B, S, D = (2, 256, 128)
        H = 16
        DH = D // H
        key = jax.random.key(seed)
        ks = jax.random.split(key, 9)
        s = 1.0 / np.sqrt(D)
        inp = {'X': jax.random.normal(ks[0], (B, S, D), dtype=jnp.float32), 'Wq': jax.random.normal(ks[1], (D, D), dtype=jnp.float32) * s, 'bq': jnp.zeros((D,), dtype=jnp.float32), 'Wk': jax.random.normal(ks[2], (D, D), dtype=jnp.float32) * s, 'bk': jnp.zeros((D,), dtype=jnp.float32), 'Wv': jax.random.normal(ks[3], (D, D), dtype=jnp.float32) * s, 'bv': jnp.zeros((D,), dtype=jnp.float32), 'Wo': jax.random.normal(ks[4], (D, D), dtype=jnp.float32) * s, 'bo': jnp.zeros((D,), dtype=jnp.float32)}
        return inp
    _L0_attn_in = _L0_attn_setup()

    def _L0_ffn_setup():
        import jax, jax.numpy as jnp
        import numpy as np
        DIM = 128
        DEPTH = 6
        HEADS = 16
        DIM_HEAD = 64
        WINDOW = 32
        INNER = HEADS * DIM_HEAD
        DIM_INNER = int(DIM * 4 * 2 / 3)
        QK_SCALE = 8.0

        def shift_tokens(t):
            a, s = jnp.split(t, 2, -1)
            s = jnp.pad(s, ((0, 0), (1, 0), (0, 0)))[:, :-1]
            return jnp.concatenate([a, s], -1)

        def l2norm(t):
            return t / jnp.maximum(jnp.linalg.norm(t, axis=-1, keepdims=True), 1e-12)

        def rotate_half(x):
            x1, x2 = jnp.split(x, 2, -1)
            return jnp.concatenate([-x2, x1], -1)

        def rotary_tables(n):
            half = jnp.arange(0, DIM_HEAD, 2, dtype=jnp.float32)
            inv_freq = 1.0 / 10000.0 ** (half / DIM_HEAD)
            t = jnp.arange(n, dtype=jnp.float32)
            freqs = t[:, None] * inv_freq[None, :]
            freqs = jnp.concatenate([freqs, freqs], -1)
            base_scale = (half + 0.4 * DIM_HEAD) / (1.4 * DIM_HEAD)
            power = (t - n // 2) / (WINDOW // 2)
            scale = base_scale[None, :] ** power[:, None]
            scale = jnp.concatenate([scale, scale], -1)
            return (freqs, scale)

        def local_attention(q, k, v):
            b, h, n, d = q.shape
            w = WINDOW
            nw = n // w
            bq = q.reshape(b, h, nw, w, d)
            bk = k.reshape(b, h, nw, w, d)
            bv = v.reshape(b, h, nw, w, d)

            def look(t):
                p = jnp.pad(t, ((0, 0), (0, 0), (1, 0), (0, 0), (0, 0)))
                return jnp.concatenate([p[:, :, :nw], p[:, :, 1:]], axis=3)
            bk2, bv2 = (look(bk), look(bv))
            seq = jnp.arange(n).reshape(nw, w)
            seq_p = jnp.pad(seq, ((1, 0), (0, 0)), constant_values=-1)
            jt = jnp.concatenate([seq_p[:nw], seq_p[1:]], axis=1)
            it = seq[:, :, None]
            jb = jt[:, None, :]
            mask = (it < jb) | (it > jb + w) | (jb == -1)
            sim = jnp.einsum('bhwie,bhwje->bhwij', bq, bk2) * QK_SCALE
            sim = jnp.where(mask, -jnp.finfo(sim.dtype).max, sim)
            attn = jax.nn.softmax(sim, -1)
            out = jnp.einsum('bhwij,bhwje->bhwie', attn, bv2)
            return out.reshape(b, h, n, d)

        def attn_layer(x, Wqkv, qs, ksc, Wo):
            b, n, _ = x.shape
            qkv = x @ Wqkv
            q, k, v = jnp.split(qkv, 3, -1)
            sh = lambda t: t.reshape(b, n, HEADS, DIM_HEAD).transpose(0, 2, 1, 3)
            q, k, v = (sh(q), sh(k), sh(v))
            q = l2norm(q) * qs
            k = l2norm(k) * ksc
            freqs, scale = rotary_tables(n)
            cos, sin = (jnp.cos(freqs), jnp.sin(freqs))
            q = q * cos * scale + rotate_half(q) * sin * scale
            inv = 1.0 / scale
            k = k * cos * inv + rotate_half(k) * sin * inv
            out = local_attention(q, k, v)
            out = out.transpose(0, 2, 1, 3).reshape(b, n, INNER)
            return out @ Wo

        def ffn_layer(x, g, bln, W1, b1, W2, b2):
            mu = x.mean(-1, keepdims=True)
            var = ((x - mu) ** 2).mean(-1, keepdims=True)
            xn = (x - mu) / jnp.sqrt(var + 1e-05) * g + bln
            hg = xn @ W1 + b1
            a, gate = jnp.split(hg, 2, -1)
            return a * jax.nn.gelu(gate, approximate=False) @ W2 + b2
        key = jax.random.key(seed)
        ks = jax.random.split(key, 8)
        B, N = (2, 256)
        init = lambda k, shape: jax.random.normal(k, shape, jnp.float32) * 0.02
        return {'x': jax.random.normal(ks[0], (B, N, DIM), jnp.float32), 'Wqkv': init(ks[1], (DEPTH, DIM, 3 * INNER)), 'q_scale': jnp.ones((DEPTH, DIM_HEAD), jnp.float32), 'k_scale': jnp.ones((DEPTH, DIM_HEAD), jnp.float32), 'Wo': init(ks[2], (DEPTH, INNER, DIM)), 'ln_g': jnp.ones((DEPTH, DIM), jnp.float32), 'ln_b': jnp.zeros((DEPTH, DIM), jnp.float32), 'W1': init(ks[3], (DEPTH, DIM, 2 * DIM_INNER)), 'b1': jnp.zeros((DEPTH, 2 * DIM_INNER), jnp.float32), 'W2': init(ks[4], (DEPTH, DIM_INNER, DIM)), 'b2': jnp.zeros((DEPTH, DIM), jnp.float32)}
    _L0_ffn_in = _L0_ffn_setup()
    _L0_c = _w((lambda *s: np.random.randn(*s).astype(np.float32) * 0.05)(4, 128))
    _L0_wmod = _w((lambda *s: np.random.randn(*s).astype(np.float32) * 0.05)(128, 6 * 128) * 128 ** (-0.5))
    _d = {'L0_attn_X': _L0_attn_in['X'], 'L0_attn_Wq': _L0_attn_in['Wq'], 'L0_attn_bq': _L0_attn_in['bq'], 'L0_attn_Wk': _L0_attn_in['Wk'], 'L0_attn_bk': _L0_attn_in['bk'], 'L0_attn_Wv': _L0_attn_in['Wv'], 'L0_attn_bv': _L0_attn_in['bv'], 'L0_attn_Wo': _L0_attn_in['Wo'], 'L0_attn_bo': _L0_attn_in['bo'], 'L0_ffn_Wqkv': _L0_ffn_in['Wqkv'], 'L0_ffn_q_scale': _L0_ffn_in['q_scale'], 'L0_ffn_k_scale': _L0_ffn_in['k_scale'], 'L0_ffn_Wo': _L0_ffn_in['Wo'], 'L0_ffn_ln_g': _L0_ffn_in['ln_g'], 'L0_ffn_ln_b': _L0_ffn_in['ln_b'], 'L0_ffn_W1': _L0_ffn_in['W1'], 'L0_ffn_b1': _L0_ffn_in['b1'], 'L0_ffn_W2': _L0_ffn_in['W2'], 'L0_ffn_b2': _L0_ffn_in['b2'], 'L0_c': _L0_c, 'L0_wmod': _L0_wmod}
    _x0 = _d['L0_attn_X']
    _d['L0_attn_X'] = jax.random.normal(jax.random.fold_in(jax.random.key(seed), 1), (4, 1024, 128), dtype=_x0.dtype)
    del _x0
    return _d

def reference(L0_attn_X, L0_attn_Wq, L0_attn_bq, L0_attn_Wk, L0_attn_bk, L0_attn_Wv, L0_attn_bv, L0_attn_Wo, L0_attn_bo, L0_ffn_Wqkv, L0_ffn_q_scale, L0_ffn_k_scale, L0_ffn_Wo, L0_ffn_ln_g, L0_ffn_ln_b, L0_ffn_W1, L0_ffn_b1, L0_ffn_W2, L0_ffn_b2, L0_c, L0_wmod):

    def _L0_attn_ref(X, Wq, bq, Wk, bk, Wv, bv, Wo, bo):
        import jax, jax.numpy as jnp
        import numpy as np
        B, S, D = (2, 256, 128)
        H = 16
        DH = D // H
        b, s, _ = X.shape
        Q = X @ Wq.T + bq
        K = X @ Wk.T + bk
        V = X @ Wv.T + bv
        q = Q.reshape(b, s, H, DH).transpose(0, 2, 1, 3)
        k = K.reshape(b, s, H, DH).transpose(0, 2, 1, 3)
        v = V.reshape(b, s, H, DH).transpose(0, 2, 1, 3)
        scores = jnp.einsum('bhqd,bhkd->bhqk', q, k) / jnp.sqrt(jnp.float32(DH))
        attn = jax.nn.softmax(scores, axis=-1)
        out = jnp.einsum('bhqk,bhkd->bhqd', attn, v)
        out = out.transpose(0, 2, 1, 3).reshape(b, s, D)
        return out @ Wo.T + bo

    def _L0_ffn_ref(x, Wqkv, q_scale, k_scale, Wo, ln_g, ln_b, W1, b1, W2, b2):
        import jax, jax.numpy as jnp
        import numpy as np
        DIM = 128
        DEPTH = 6
        HEADS = 16
        DIM_HEAD = 64
        WINDOW = 32
        INNER = HEADS * DIM_HEAD
        DIM_INNER = int(DIM * 4 * 2 / 3)
        QK_SCALE = 8.0

        def shift_tokens(t):
            a, s = jnp.split(t, 2, -1)
            s = jnp.pad(s, ((0, 0), (1, 0), (0, 0)))[:, :-1]
            return jnp.concatenate([a, s], -1)

        def l2norm(t):
            return t / jnp.maximum(jnp.linalg.norm(t, axis=-1, keepdims=True), 1e-12)

        def rotate_half(x):
            x1, x2 = jnp.split(x, 2, -1)
            return jnp.concatenate([-x2, x1], -1)

        def rotary_tables(n):
            half = jnp.arange(0, DIM_HEAD, 2, dtype=jnp.float32)
            inv_freq = 1.0 / 10000.0 ** (half / DIM_HEAD)
            t = jnp.arange(n, dtype=jnp.float32)
            freqs = t[:, None] * inv_freq[None, :]
            freqs = jnp.concatenate([freqs, freqs], -1)
            base_scale = (half + 0.4 * DIM_HEAD) / (1.4 * DIM_HEAD)
            power = (t - n // 2) / (WINDOW // 2)
            scale = base_scale[None, :] ** power[:, None]
            scale = jnp.concatenate([scale, scale], -1)
            return (freqs, scale)

        def local_attention(q, k, v):
            b, h, n, d = q.shape
            w = WINDOW
            nw = n // w
            bq = q.reshape(b, h, nw, w, d)
            bk = k.reshape(b, h, nw, w, d)
            bv = v.reshape(b, h, nw, w, d)

            def look(t):
                p = jnp.pad(t, ((0, 0), (0, 0), (1, 0), (0, 0), (0, 0)))
                return jnp.concatenate([p[:, :, :nw], p[:, :, 1:]], axis=3)
            bk2, bv2 = (look(bk), look(bv))
            seq = jnp.arange(n).reshape(nw, w)
            seq_p = jnp.pad(seq, ((1, 0), (0, 0)), constant_values=-1)
            jt = jnp.concatenate([seq_p[:nw], seq_p[1:]], axis=1)
            it = seq[:, :, None]
            jb = jt[:, None, :]
            mask = (it < jb) | (it > jb + w) | (jb == -1)
            sim = jnp.einsum('bhwie,bhwje->bhwij', bq, bk2) * QK_SCALE
            sim = jnp.where(mask, -jnp.finfo(sim.dtype).max, sim)
            attn = jax.nn.softmax(sim, -1)
            out = jnp.einsum('bhwij,bhwje->bhwie', attn, bv2)
            return out.reshape(b, h, n, d)

        def attn_layer(x, Wqkv, qs, ksc, Wo):
            b, n, _ = x.shape
            qkv = x @ Wqkv
            q, k, v = jnp.split(qkv, 3, -1)
            sh = lambda t: t.reshape(b, n, HEADS, DIM_HEAD).transpose(0, 2, 1, 3)
            q, k, v = (sh(q), sh(k), sh(v))
            q = l2norm(q) * qs
            k = l2norm(k) * ksc
            freqs, scale = rotary_tables(n)
            cos, sin = (jnp.cos(freqs), jnp.sin(freqs))
            q = q * cos * scale + rotate_half(q) * sin * scale
            inv = 1.0 / scale
            k = k * cos * inv + rotate_half(k) * sin * inv
            out = local_attention(q, k, v)
            out = out.transpose(0, 2, 1, 3).reshape(b, n, INNER)
            return out @ Wo

        def ffn_layer(x, g, bln, W1, b1, W2, b2):
            mu = x.mean(-1, keepdims=True)
            var = ((x - mu) ** 2).mean(-1, keepdims=True)
            xn = (x - mu) / jnp.sqrt(var + 1e-05) * g + bln
            hg = xn @ W1 + b1
            a, gate = jnp.split(hg, 2, -1)
            return a * jax.nn.gelu(gate, approximate=False) @ W2 + b2
        for i in range(DEPTH):
            x = attn_layer(shift_tokens(x), Wqkv[i], q_scale[i], k_scale[i], Wo[i]) + x
            x = ffn_layer(shift_tokens(x), ln_g[i], ln_b[i], W1[i], b1[i], W2[i], b2[i]) + x
        return x
    x = L0_attn_X
    mod = (_silu(L0_c) @ L0_wmod).reshape(L0_c.shape[0], 6, 1, -1)
    sa, ca, ga, sb, cb, gb = (mod[:, 0], mod[:, 1], mod[:, 2], mod[:, 3], mod[:, 4], mod[:, 5])
    ga = (2 * (ga >= 0) - 1) * jnp.maximum(jnp.abs(ga), 0.25)
    gb = (2 * (gb >= 0) - 1) * jnp.maximum(jnp.abs(gb), 0.25)
    h = _layernorm(x, axis=-1) * (1 + ca) + sa
    x = x + ga * _L0_attn_ref(h, L0_attn_Wq, L0_attn_bq, L0_attn_Wk, L0_attn_bk, L0_attn_Wv, L0_attn_bv, L0_attn_Wo, L0_attn_bo)
    h = _layernorm(x, axis=-1) * (1 + cb) + sb
    x = x + gb * _L0_ffn_ref(h, L0_ffn_Wqkv, L0_ffn_q_scale, L0_ffn_k_scale, L0_ffn_Wo, L0_ffn_ln_g, L0_ffn_ln_b, L0_ffn_W1, L0_ffn_b1, L0_ffn_W2, L0_ffn_b2)
    return x

_drawn_inputs = setup_inputs


def setup_inputs(seed=0):
    import zlib

    import numpy as np

    out = dict(_drawn_inputs(seed))
    spreads = {'L0_attn_bq': (0.0, 0.8),
     'L0_attn_bk': (0.0, 2.0),
     'L0_attn_bv': (0.0, 0.345),
     'L0_attn_bo': (0.0, 0.327),
     'L0_ffn_q_scale': (1.0, 0.6),
     'L0_ffn_k_scale': (1.0, 0.6),
     'L0_ffn_ln_g': (1.0, 0.6),
     'L0_ffn_ln_b': (0.0, 0.8),
     'L0_ffn_b1': (0.0, 0.8),
     'L0_ffn_b2': (0.0, 0.645)}
    factors = {'L0_ffn_W1': 7.386, 'L0_ffn_W2': 7.251}
    for name, (base, spread) in spreads.items():
        noise = np.random.default_rng([zlib.crc32(name.encode()), seed]).standard_normal(out[name].shape)
        drawn = base * np.exp(spread * noise) if base else spread * noise
        out[name] = jnp.asarray(drawn.astype(out[name].dtype))
    for name, factor in factors.items():
        out[name] = (out[name] * factor).astype(out[name].dtype)
    return out
```

```python
from contextlib import ExitStack

import numpy as np
import concourse.bass as bass
from concourse import mybir

F32 = mybir.dt.float32
BF16 = mybir.dt.bfloat16
ALU = mybir.AluOpType
ACT = mybir.ActivationFunctionType
AX = mybir.AxisListType

P = 128
B, S, D = 4, 1024, 128
NT = S // P
H, DH = 16, 8
NL = 6
LH, LD = 16, 64
INNER = LH * LD
WIN = 32
FF = int(D * 4 * 2 / 3)
LN_EPS = 1e-5
MASKED = -1e30

QB = 64
KB = QB + WIN
CH = [(c * P, min(P, FF - c * P)) for c in range((FF + P - 1) // P)]

NPART = 3
NPROD = NPART * NPART * DH
MROW = 96
KROWS = MROW + 2
GH = 4
NG = B * H // GH
VW = 32


class Count:

    def __init__(self, sem, per=1):
        self.sem, self.per = sem, per

    def at(self, n, k=None):
        k = self.per if k is None else k
        if isinstance(n, tuple):
            base, off = n
            return base * self.per + (self.per * off + k)
        return self.per * n + k

    def wait(self, engine, n, k=None):
        engine.wait_ge(self.sem, self.at(n, k))


def build(nc, ins, out):
    pe, act, dve, pool, sp = nc.tensor, nc.scalar, nc.vector, nc.gpsimd, nc.sync
    whole = ExitStack()

    def sb(ctx, name, shape, dt=F32):
        return ctx.enter_context(nc.sbuf_tensor(name, shape, dt))

    def ps(ctx, name, shape, dt=F32):
        return ctx.enter_context(nc.psum_tensor(name, shape, dt))

    def count(ctx, name, per=1):
        return Count(ctx.enter_context(nc.semaphore(name)), per)

    X = sb(whole, "X", [P, B, NT, D])
    ident = sb(whole, "ident", [P, P])
    ident_b = sb(whole, "ident_b", [P, P], BF16)
    ones = sb(whole, "ones", [P, P])
    gate_b = sb(whole, "gate_b", [P, B, D])
    spare = sb(whole, "spare", [P, 1])
    x_mid = nc.dram_tensor("x_mid", [P, B, NT, D], F32, kind="Internal").ap()
    parts_d = [nc.dram_tensor(f"parts_{n}", [B, NPART, P, S], BF16, kind="Internal").ap() for n in "qk"]
    x_dram = ins["X"].rearrange("b (t p) c -> p b t c", p=P)
    out_dram = out.rearrange("b (t p) c -> p b t c", p=P)

    first = ExitStack()
    mod = sb(first, "mod", [P, 6, B, D])
    VA = sb(first, "VA", [P, B, NT, H, DH + 1])
    AO = sb(first, "AO", [P, B, NT, D])
    woT = sb(first, "woT", [P, D])
    rows = sb(first, "rows", [1, 2, D])

    with ExitStack() as c:
        cT = sb(c, "cT", [P, B])
        wmod = sb(c, "wmod", [P, 6 * D])
        sig = sb(c, "sig", [P, 3, B])
        modT = sb(c, "modT", [P, 6, B])
        tmp = sb(c, "tmp", [P, 2, 2, B])
        diag = sb(c, "diag", [P, 6, B, D])
        p_mod = ps(c, "p_mod", [P, 6, B])
        p_bc = ps(c, "p_bc", [P, 6, B, D])
        s_in = count(c, "s_in", 16)
        s_cst = count(c, "s_cst")
        s_v = count(c, "s_v")
        s_e = count(c, "s_e")
        s_m = count(c, "s_m")
        s_dg = count(c, "s_dg")
        s_bc = count(c, "s_bc")
        s_mc = count(c, "s_mc")
        for dst, src in ((cT[:, :], ins["cT"]), (wmod[:, :], ins["wmod"]), (X[:, :, :, :], x_dram),
                         (woT[:, :], ins["woT"]), (rows[:, 0, :], ins["bv"]), (rows[:, 1, :], ins["bo"])):
            sp.dma_start(dst, src).then_inc(s_in.sem, 16)
        pool.memset(ident[:, :], 0.0).then_inc(s_cst.sem, 1)
        pool.memset(ones[:, :], 1.0).then_inc(s_cst.sem, 1)
        pool.memset(VA[:, :, :, :, DH:DH + 1], 1.0).then_inc(s_cst.sem, 1)
        pool.wait_ge(s_cst.sem, 3)
        pool.affine_select(out=ident[:, :], in_=ident[:, :], compare_op=ALU.not_equal, fill=1.0,
                           base=0, pattern=[[-1, P]], channel_multiplier=1).then_inc(s_cst.sem, 1)
        act.wait_ge(s_in.sem, 16 * 6)
        act.activation(sig[:, 0, :], cT[:, :], ACT.Exp, scale=-1.0).then_inc(s_e.sem, 1)
        n_v = 0

        def step(ins_):
            nonlocal n_v
            n_v += 1
            ins_.then_inc(s_v.sem, 1)
            dve.wait_ge(s_v.sem, n_v)

        dve.wait_ge(s_cst.sem, 4)
        step(dve.tensor_copy(ident_b[:, :], ident[:, :]))
        dve.wait_ge(s_e.sem, 1)
        step(dve.tensor_scalar_add(sig[:, 1, :], sig[:, 0, :], 1.0))
        step(dve.reciprocal(sig[:, 2, :], sig[:, 1, :]))
        step(dve.tensor_tensor(out=sig[:, 0, :], in0=cT[:, :], in1=sig[:, 2, :], op=ALU.mult))
        pe.wait_ge(s_v.sem, n_v)
        pe.wait_ge(s_in.sem, 16 * 6)
        for j in range(6):
            mm = pe.matmul(p_mod[:, j, :], wmod[:, j * D:(j + 1) * D], sig[:, 0, :], start=True, stop=True)
        mm.then_inc(s_m.sem, 1)
        dve.wait_ge(s_m.sem, 1)
        step(dve.tensor_copy(modT[:, :, :], p_mod[:, :, :]))
        scales, gates = modT[:, 1:5:3, :], modT[:, 2:6:3, :]
        step(dve.tensor_scalar_add(scales, scales, 1.0))
        step(dve.tensor_scalar(tmp[:, 0, :, :], gates, -1.0, None, ALU.mult))
        step(dve.tensor_tensor(out=tmp[:, 0, :, :], in0=gates, in1=tmp[:, 0, :, :], op=ALU.max))
        step(dve.tensor_scalar_max(tmp[:, 0, :, :], tmp[:, 0, :, :], 0.25))
        step(dve.tensor_scalar(tmp[:, 1, :, :], gates, 0.0, 2.0, ALU.is_ge, ALU.mult))
        step(dve.tensor_scalar_add(tmp[:, 1, :, :], tmp[:, 1, :, :], -1.0))
        step(dve.tensor_tensor(out=gates, in0=tmp[:, 0, :, :], in1=tmp[:, 1, :, :], op=ALU.mult))
        for j in range(6):
            for b in range(B):
                dg = dve.tensor_scalar(diag[:, j, b, :], ident[:, :], modT[:, j, b:b + 1], None, ALU.mult)
            dg.then_inc(s_dg.sem, 1)
            s_dg.wait(pe, j)
            pe.matmul(p_bc[:, j, :, :], ones[:, :], diag[:, j, :, :], start=True, stop=True).then_inc(s_bc.sem, 1)
            s_bc.wait(act, j)
            act.activation(mod[:, j, :, :], p_bc[:, j, :, :], ACT.Copy).then_inc(s_mc.sem, 1)
        dve.wait_ge(s_mc.sem, 6)
        dve.tensor_copy(gate_b[:, :, :], mod[:, 5, :, :])
        nc.all_engine_barrier()

    CT = 4
    NC = B * NT // CT
    with ExitStack() as c:
        wT = [sb(c, f"w{n}T", [P, D]) for n in "qkv"]
        bias = sb(c, "bias_qk", [P, 2])
        stats = sb(c, "stats", [P, 2, CT, 6])
        mv = sb(c, "mv", [P, 2, CT, 2])
        power = sb(c, "power", [P, CT])
        rstd = sb(c, "rstd", [P, 2, CT])
        hn = sb(c, "hn", [P, 2, CT, D])
        hT = sb(c, "hT", [P, 2, CT * P])
        full = sb(c, "full", [P, 2, 2, CT * P])
        rest = sb(c, "rest", [P, 2, CT * P])
        parts = sb(c, "parts", [P, 2, 2, NPART, CT * P], BF16)
        p_t = ps(c, "p_t", [P, 2, CT * P])
        p_qk = ps(c, "p_qk", [P, 2, 2, CT * P])
        p_v = ps(c, "p_v", [P, 2, CT, D])
        s_w = count(c, "s_w", 16)
        s_pw = count(c, "s_pw")
        s_ln = count(c, "s_ln", 6)
        s_rs = count(c, "s_rs")
        s_t = count(c, "s_t")
        s_hT = count(c, "s_hT")
        s_qk = count(c, "s_qk", 2)
        s_vp = count(c, "s_vp")
        s_full = count(c, "s_full", 2)
        s_va = count(c, "s_va")
        s_sp = count(c, "s_sp", 10)
        s_pd = [[count(c, f"s_pd{u}{n}", 16) for n in "qk"] for u in range(2)]
        for dst, src in ((wT[0][:, :], ins["wqT"]), (wT[1][:, :], ins["wkT"]), (wT[2][:, :], ins["wvT"]),
                         (bias[:, 0:1], ins["bq"]), (bias[:, 1:2], ins["bk"])):
            sp.dma_start(dst, src).then_inc(s_w.sem, 16)
        pool.memset(power[:, :], -0.5).then_inc(s_pw.sem, 1)
        pool.wait_ge(s_pw.sem, 1)
        pe.wait_ge(s_w.sem, 16 * 5)
        act.wait_ge(s_w.sem, 16 * 5)

        def layernorm(n, b, u, fresh):
            for j in range(CT):
                i = dve.bn_stats(stats[:, u, j, :], X[:, b, CT * u + j, :])
            i.then_inc(s_ln.sem, 1)
            s_ln.wait(dve, n, 1)
            dve.memset(spare[:, :], 0.0)
            for j in range(CT):
                i = dve.bn_aggr(mv[:, u, j, :], stats[:, u, j, :])
            i.then_inc(s_ln.sem, 1)
            s_ln.wait(dve, n, 2)
            dve.tensor_scalar_add(mv[:, u, :, 1:2], mv[:, u, :, 1:2], LN_EPS).then_inc(s_ln.sem, 1)
            s_ln.wait(pool, n, 3)
            pool.tensor_tensor(out=rstd[:, u, :], in0=mv[:, u, :, 1], in1=power[:, :], op=ALU.pow)\
                .then_inc(s_rs.sem, 1)
            s_rs.wait(dve, n)
            if not fresh:
                s_t.wait(dve, (n[0], n[1] - 2))
            for j in range(CT):
                i = dve.tensor_scalar(hn[:, u, j, :], X[:, b, CT * u + j, :], mv[:, u, j, 0:1],
                                      rstd[:, u, j:j + 1], ALU.subtract, ALU.mult)
            i.then_inc(s_ln.sem, 1)
            for m, op in ((1, ALU.mult), (0, ALU.add)):
                s_ln.wait(dve, n, 5 - m)
                dve.tensor_tensor(out=hn[:, u, :, :], in0=hn[:, u, :, :],
                                  in1=mod[:, m, b, :].unsqueeze(1).broadcast_to([P, CT, D]),
                                  op=op).then_inc(s_ln.sem, 1)

        def chunk(n, b, u, fresh):
            layernorm(n, b, u, fresh)
            s_ln.wait(pe, n, 6)
            if not fresh:
                s_hT.wait(pe, (n[0], n[1] - 2))
            for j in range(CT):
                mm = pe.transpose(p_t[:, u, j * P:(j + 1) * P], hn[:, u, j, :], ident[:, :])
            mm.then_inc(s_t.sem, 1)
            s_t.wait(act, n)
            if not fresh:
                s_vp.wait(act, (n[0], n[1] - 2))
            act.activation(hT[:, u, :], p_t[:, u, :], ACT.Copy).then_inc(s_hT.sem, 1)
            s_hT.wait(pe, n)
            for i in range(2):
                if not fresh:
                    s_full.wait(pe, (n[0], n[1] - 2), i + 1)
                pe.matmul(p_qk[:, u, i, :], wT[i][:, :], hT[:, u, :], start=True, stop=True).then_inc(s_qk.sem, 1)
            if not fresh:
                s_va.wait(pe, (n[0], n[1] - 2))
            for j in range(CT):
                pe.matmul(p_v[:, u, j, :], hT[:, u, j * P:(j + 1) * P], wT[2][:, :], start=True, stop=False)
                mm = pe.matmul(p_v[:, u, j, :], ones[0:1, :], rows[:, 0, :], start=False, stop=True)
            mm.then_inc(s_vp.sem, 1)
            for i in range(2):
                s_qk.wait(act, n, i + 1)
                if not fresh:
                    s_sp.wait(act, (n[0], n[1] - 2))
                act.activation(full[:, u, i, :], p_qk[:, u, i, :], ACT.Identity,
                               bias=bias[:, i:i + 1]).then_inc(s_full.sem, 1)
            s_vp.wait(act, n)
            act.activation(VA[:, b, CT * u:CT * u + CT, :, 0:DH],
                           p_v[:, u, :, :].rearrange("p t (h d) -> p t h d", d=DH),
                           ACT.Copy).then_inc(s_va.sem, 1)
            for i in range(2):
                s_full.wait(dve, n, i + 1)
                if not fresh:
                    s_pd[u][i].wait(dve, (b, -1))
                k = 5 * i
                dve.tensor_copy(parts[:, u, i, 0, :], full[:, u, i, :]).then_inc(s_sp.sem, 1)
                s_sp.wait(dve, n, k + 1)
                dve.tensor_tensor(out=rest[:, i, :], in0=full[:, u, i, :], in1=parts[:, u, i, 0, :],
                                  op=ALU.subtract).then_inc(s_sp.sem, 1)
                s_sp.wait(dve, n, k + 2)
                dve.tensor_copy(parts[:, u, i, 1, :], rest[:, i, :]).then_inc(s_sp.sem, 1)
                s_sp.wait(dve, n, k + 3)
                dve.tensor_tensor(out=parts[:, u, i, 2, :], in0=rest[:, i, :], in1=parts[:, u, i, 1, :],
                                  op=ALU.subtract).then_inc(s_sp.sem, 2)
                s_sp.wait(sp, n, k + 5)
                sp.dma_start(parts_d[i][b, :, :, u * CT * P:(u + 1) * CT * P].rearrange("j p n -> p j n"),
                             parts[:, u, i, :, :]).then_inc(s_pd[u][i].sem, 16)

        for u in range(2):
            chunk(u, 0, u, True)
        with nc.Fori(1, B) as b:
            for u in range(2):
                chunk((b * 2, u), b, u, False)
        for u in range(2):
            for i in range(2):
                s_pd[u][i].wait(sp, B - 1)
        nc.all_engine_barrier()

    with ExitStack() as c:
        QA = sb(c, "QA", [KROWS, 2, 2, GH, 512], BF16)
        KA = sb(c, "KA", [KROWS, 2, GH, S], BF16)
        VG = sb(c, "VG", [P, 2, NT, GH, VW])
        E = sb(c, "E", [P, 4, GH, 512])
        negmax = sb(c, "negmax", [P, 2, GH, 4])
        nm = sb(c, "nm", [GH * 4, 2, P])
        nmb = sb(c, "nmb", [GH * 4, 2, 2, P], BF16)
        OE = sb(c, "OE", [P, 2, 512])
        rsum = sb(c, "rsum", [P, 2, 4, GH])
        p_max = ps(c, "p_max", [P, 2, S])
        p_s = ps(c, "p_s", [P, 2, 512])
        p_o = ps(c, "p_o", [P, 2, 512])
        HU = 16
        s_z = count(c, "s_z")
        s_ld = count(c, "s_ld", 16 * 3 * NPART * NPART)
        s_vg = count(c, "s_vg")
        s_mx = count(c, "s_mx", 2 * HU + 2)
        s_mr = count(c, "s_mr", 2 * HU + 2)
        s_mb = count(c, "s_mb", 4)
        s_md = count(c, "s_md", 64)
        s_st = count(c, "s_st", 64)
        s_ex = count(c, "s_ex", 64)
        s_pv = count(c, "s_pv", 16)
        s_oe = count(c, "s_oe", 2)
        s_ot = count(c, "s_ot", 2)
        s_rc = count(c, "s_rc", 2)
        s_ao = count(c, "s_ao", 2)

        pool.memset(QA[:, :, :, :, :], 0.0).then_inc(s_z.sem, 1)
        pool.memset(VG[:, :, :, :, :], 0.0).then_inc(s_z.sem, 1)
        dve.memset(KA[:, :, :, :], 0.0).then_inc(s_z.sem, 1)
        dve.wait_ge(s_z.sem, 3)
        dve.memset(KA[MROW:KROWS, :, :, :], 1.0).then_inc(s_z.sem, 1)
        sp.wait_ge(s_z.sem, 4)
        pool.wait_ge(s_z.sem, 4)
        pe.wait_ge(s_z.sem, 4)

        def add(n, d):
            return (n[0], n[1] + d) if isinstance(n, tuple) else n + d

        def heads(hg):
            return slice(hg * GH, hg * GH + GH) if isinstance(hg, int) else bass.ds(hg * GH, GH)

        def load(n, b, hg, p, reuse):
            if reuse:
                s_st.wait(sp, add(n, -2))
            for i in range(NPART):
                for j in range(NPART):
                    r = (i * NPART + j) * DH
                    q = parts_d[0][b, i].rearrange("(h d) n -> d h n", d=DH)
                    k = parts_d[1][b, j].rearrange("(h d) n -> d h n", d=DH)
                    for qh in range(2):
                        sp.dma_start(QA[r:r + DH, p, qh, :, :], q[:, heads(hg), qh * 512:(qh + 1) * 512])\
                            .then_inc(s_ld.sem, 16)
                    sp.dma_start(KA[r:r + DH, p, :, :], k[:, heads(hg), :]).then_inc(s_ld.sem, 16)

        def values(n, b, hg, p, reuse):
            if reuse:
                s_pv.wait(pool, add(n, -2))
            pool.tensor_copy(VG[:, p, :, :, 0:DH + 1], VA[:, b, :, heads(hg), :]).then_inc(s_vg.sem, 1)

        unit_log = {}

        def max_unit(n, p, qh, i, reuse):
            k = qh * (HU + 1) + i
            c_, qt = divmod(i, 4)
            if reuse or k >= 2:
                s_mr.wait(pe, n if k >= 2 else add(n, -1), k - 1 if k >= 2 else 2 * HU + 2 + k - 1)
            if i == 0 and qh == 0:
                s_ld.wait(pe, n)
            slot = k % 2
            for j in range(2):
                mm = pe.matmul(p_max[:, slot, j * 512:(j + 1) * 512], QA[0:NPROD, p, qh, c_, qt * P:(qt + 1) * P],
                               KA[0:NPROD, p, c_, j * 512:(j + 1) * 512], start=True, stop=True)
            mm.then_inc(s_mx.sem, 1)
            s_mx.wait(dve, n, k + 1)
            dve.tensor_reduce(negmax[:, qh, c_, qt:qt + 1], p_max[:, slot, :], axis=AX.X, op=ALU.max,
                              negate=True).then_inc(s_mr.sem, 1)

        def max_rows(n, p, qh, reuse):
            k = qh * (HU + 1) + HU
            slot = k % 2
            s_mr.wait(pe, n, k)
            pe.transpose(p_max[0:GH * 4, slot, 0:P], negmax[:, qh, :, :].rearrange("p c q -> p (c q)"),
                         ident[:, :]).then_inc(s_mx.sem, 1)
            s_mx.wait(dve, n, k + 1)
            dve.tensor_copy(nm[:, qh, :], p_max[0:GH * 4, slot, 0:P]).then_inc(s_mr.sem, 1)
            s_mr.wait(dve, n, k + 1)
            if reuse:
                s_md.wait(dve, add(n, -1), 32 * (qh + 1))
            dve.tensor_copy(nmb[:, qh, 0, :], nm[:, qh, :]).then_inc(s_mb.sem, 1)
            s_mb.wait(dve, n, 2 * qh + 1)
            dve.tensor_tensor(out=nmb[:, qh, 1, :], in0=nm[:, qh, :], in1=nmb[:, qh, 0, :],
                              op=ALU.subtract).then_inc(s_mb.sem, 1)
            s_mb.wait(sp, n, 2 * qh + 2)
            for j in range(2):
                sp.dma_start(QA[MROW + j:MROW + j + 1, p, qh, :, :],
                             nmb[:, qh, j, :]).then_inc(s_md.sem, 16)

        def score(n, p, s, c_, reuse):
            qh, kb = divmod(s, 8)
            i = 4 * s + c_
            if i >= 2:
                s_ex.wait(pe, n, i - 1)
            elif reuse:
                s_ex.wait(pe, add(n, -1), 64 + i - 1)
            if kb == 0 and c_ == 0:
                s_md.wait(pe, n, 32 * (qh + 1))
            pe.matmul(p_s[:, i % 2, :], KA[:, p, c_, kb * P:(kb + 1) * P], QA[:, p, qh, c_, :],
                      start=True, stop=True).then_inc(s_st.sem, 1)
            s_st.wait(act, n, i + 1)
            if c_ == 0 and (s >= 4 or reuse):
                s_pv.wait(act, n if s >= 4 else add(n, -1), s - 3 if s >= 4 else s + 13)
            act.activation(E[:, s % 4, c_, :], p_s[:, i % 2, :], ACT.Exp, scale=DH ** -0.5)\
                .then_inc(s_ex.sem, 1)

        def weigh(n, p, s, reuse):
            qh, kb = divmod(s, 8)
            s_ex.wait(pe, n, 4 * s + 4)
            if s == 0:
                s_vg.wait(pe, n)
            if kb == 0 and reuse:
                s_ao.wait(pe, add(n, -1), qh + 1)
            for c_ in range(GH):
                mm = pe.matmul(p_o[c_ * VW:(c_ + 1) * VW, qh, :], VG[:, p, kb, c_, :], E[:, s % 4, c_, :],
                               start=(kb == 0), stop=(kb == 7), skip_group_check=True)
            mm.then_inc(s_pv.sem, 1)

        def result(n, b, hg, qh, reuse):
            s_pv.wait(dve, n, 8 * (qh + 1))
            if reuse:
                s_ot.wait(dve, add(n, -1), qh + 1)
            dve.tensor_copy(OE[:, qh, :], p_o[:, qh, :]).then_inc(s_oe.sem, 1)
            s_oe.wait(pe, n, qh + 1)
            for qt in range(4):
                mm = pe.transpose(p_o[:, qh, qt * P:(qt + 1) * P], OE[:, qh, qt * P:(qt + 1) * P], ident[:, :])
            mm.then_inc(s_ot.sem, 1)
            s_ot.wait(dve, n, qh + 1)
            o = p_o[:, qh, :].rearrange("p (q c w) -> p q c w", q=4, w=VW)
            dve.reciprocal(rsum[:, qh, :, :], o[:, :, :, DH]).then_inc(s_rc.sem, 1)
            s_rc.wait(dve, n, qh + 1)
            a = AO[:, b, 4 * qh:4 * qh + 4, :].rearrange("p q (g c d) -> p q g c d", g=H // GH, d=DH)
            a = a[:, :, hg, :, :]
            dve.tensor_tensor(out=a, in0=o[:, :, :, 0:DH],
                              in1=rsum[:, qh, :, :].unsqueeze(3).broadcast_to([P, 4, GH, DH]),
                              op=ALU.mult).then_inc(s_ao.sem, 1)

        def group(n, p, at, nxt, prev, reuse):
            for s in range(16):
                if s == 0 and nxt:
                    load(add(n, 1), *nxt, 1 - p, reuse)
                    values(add(n, 1), *nxt, 1 - p, reuse)
                score(n, p, s, 0, reuse)
                score(n, p, s, 1, reuse)
                if s > 0:
                    weigh(n, p, s - 1, reuse)
                elif prev:
                    weigh(add(n, -1), 1 - p, 15, True)
                if s == 2 and prev:
                    result(add(n, -1), *prev, 1, True)
                if s == 10:
                    result(n, *at, 0, reuse)
                score(n, p, s, 2, reuse)
                units = []
                if s < 6:
                    lo, hi = HU * s // 6, HU * (s + 1) // 6
                    units = [(n, p, 1, i, reuse or True) for i in range(lo, hi)]
                elif s < 14 and nxt:
                    units = [(add(n, 1), 1 - p, 0, i, True) for i in range(2 * (s - 6), 2 * (s - 6) + 2)]
                for u in units[:1]:
                    max_unit(*u)
                score(n, p, s, 3, reuse)
                for u in units[1:]:
                    max_unit(*u)
                if s == 5:
                    max_rows(n, p, 1, reuse)
                if s == 13 and nxt:
                    max_rows(add(n, 1), 1 - p, 0, True)

        load(0, 0, 0, 0, False)
        values(0, 0, 0, 0, False)
        for i in range(HU):
            max_unit(0, 0, 0, i, False)
        max_rows(0, 0, 0, False)
        HG = H // GH
        where = [(g // HG, g % HG) for g in range(NG)]
        group(0, 0, where[0], where[1], None, False)
        group(1, 1, where[1], where[2], where[0], True)
        with nc.Fori(1, NG // 2 - 1) as it:
            b0, hp = it // 2, it % 2
            g0 = (it * 2, 0)
            nb, nh = (it + 1) // 2, (it + 1) % 2
            pb, ph = (it - 1) // 2, (it - 1) % 2
            group(g0, 0, (b0, hp * 2), (b0, hp * 2 + 1), (pb, ph * 2 + 1), True)
            group((it * 2, 1), 1, (b0, hp * 2 + 1), (nb, nh * 2), (b0, hp * 2), True)
        group(NG - 2, 0, where[-2], where[-1], where[-3], True)
        group(NG - 1, 1, where[-1], None, where[-2], True)
        weigh(NG - 1, 1, 15, True)
        result(NG - 1, *where[-1], 1, True)
        nc.all_engine_barrier()

    with ExitStack() as c:
        ao = sb(c, "ao", [P, B, D])
        aoT = sb(c, "aoT", [P, B, P])
        gated = sb(c, "gated", [P, B, D])
        stats = sb(c, "stats2", [P, B, 6])
        mv = sb(c, "mv2", [P, B, 2])
        power = sb(c, "power2", [P, B])
        rstd = sb(c, "rstd2", [P, B])
        p_t = ps(c, "p_t2", [P, B, P])
        p_w = ps(c, "p_w2", [P, B, D])
        s_pw = count(c, "s_pw2")
        s_c = count(c, "s_c")
        s_t = count(c, "s_t2")
        s_tc = count(c, "s_tc")
        s_w = count(c, "s_w2")
        s_d = count(c, "s_d", 8)
        s_r = count(c, "s_r2")
        s_xm = count(c, "s_xm", 16)
        pool.memset(power[:, :], -0.5).then_inc(s_pw.sem, 1)
        pool.wait_ge(s_pw.sem, 1)
        with nc.Fori(0, NT) as t:
            n = (t, 0)
            dve.tensor_scalar_mul(ao[:, :, :], AO[:, :, t, :], 1.0).then_inc(s_c.sem, 1)
            s_c.wait(pe, n)
            for b in range(B):
                mm = pe.transpose(p_t[:, b, :], ao[:, b, :], ident[:, :])
            mm.then_inc(s_t.sem, 1)
            s_t.wait(act, n)
            act.activation(aoT[:, :, :], p_t[:, :, :], ACT.Copy).then_inc(s_tc.sem, 1)
            s_tc.wait(pe, n)
            for b in range(B):
                pe.matmul(p_w[:, b, :], aoT[:, b, :], woT[:, :], start=True, stop=False)
                mm = pe.matmul(p_w[:, b, :], ones[0:1, :], rows[:, 1, :], start=False, stop=True)
            mm.then_inc(s_w.sem, 1)
            s_w.wait(dve, n)
            dve.tensor_tensor(out=gated[:, :, :], in0=p_w[:, :, :], in1=mod[:, 2, :, :], op=ALU.mult)\
                .then_inc(s_d.sem, 1)
            s_d.wait(dve, n, 1)
            dve.tensor_tensor(out=gated[:, :, :], in0=gated[:, :, :], in1=X[:, :, t, :], op=ALU.add)\
                .then_inc(s_d.sem, 1)
            s_d.wait(dve, n, 2)
            sp.wait_ge(s_d.sem, s_d.at(n, 2))
            sp.dma_start(x_mid[:, :, t, :], gated[:, :, :]).then_inc(s_xm.sem, 16)
            for b in range(B):
                i = dve.bn_stats(stats[:, b, :], gated[:, b, :])
            i.then_inc(s_d.sem, 1)
            s_d.wait(dve, n, 3)
            dve.memset(spare[:, :], 0.0)
            for b in range(B):
                i = dve.bn_aggr(mv[:, b, :], stats[:, b, :])
            i.then_inc(s_d.sem, 1)
            s_d.wait(dve, n, 4)
            dve.tensor_scalar_add(mv[:, :, 1:2], mv[:, :, 1:2], LN_EPS).then_inc(s_d.sem, 1)
            s_d.wait(pool, n, 5)
            pool.tensor_tensor(out=rstd[:, :], in0=mv[:, :, 1], in1=power[:, :], op=ALU.pow)\
                .then_inc(s_r.sem, 1)
            s_r.wait(dve, n)
            for b in range(B):
                i = dve.tensor_scalar(X[:, b, t, :], gated[:, b, :], mv[:, b, 0:1], rstd[:, b:b + 1],
                                      ALU.subtract, ALU.mult)
            i.then_inc(s_d.sem, 1)
            s_d.wait(dve, n, 6)
            dve.tensor_tensor(out=X[:, :, t, :], in0=X[:, :, t, :], in1=mod[:, 4, :, :], op=ALU.mult)\
                .then_inc(s_d.sem, 1)
            s_d.wait(dve, n, 7)
            s_xm.wait(dve, n)
            dve.tensor_tensor(out=X[:, :, t, :], in0=X[:, :, t, :], in1=mod[:, 3, :, :], op=ALU.add)\
                .then_inc(s_d.sem, 1)
            s_d.wait(dve, n, 8)
        nc.all_engine_barrier()
    first.close()

    layers(nc, ins, X, ident, ident_b, ones, spare, sb, ps, count)

    with ExitStack() as c:
        XM = sb(c, "XM", [P, B, NT, D])
        s_l = count(c, "s_l", 16)
        s_f = count(c, "s_f", 2)
        s_out = count(c, "s_out", 16)
        for b in range(B):
            sp.dma_start(XM[:, b, :, :], x_mid[:, b, :, :]).then_inc(s_l.sem, 16)
        for b in range(B):
            dve.tensor_tensor(out=X[:, b, :, :], in0=X[:, b, :, :],
                              in1=gate_b[:, b, :].unsqueeze(1).broadcast_to([P, NT, D]),
                              op=ALU.mult).then_inc(s_f.sem, 1)
            dve.wait_ge(s_f.sem, 2 * b + 1)
            dve.wait_ge(s_l.sem, 16 * B)
            dve.tensor_tensor(out=X[:, b, :, :], in0=X[:, b, :, :], in1=XM[:, b, :, :],
                              op=ALU.add).then_inc(s_f.sem, 1)
            s_f.wait(sp, b)
            sp.dma_start(out_dram[:, b, :, :], X[:, b, :, :]).then_inc(s_out.sem, 16)
        sp.wait_ge(s_out.sem, 16 * B)
    whole.close()


def layers(nc, ins, X, ident, ident_b, ones, spare, sb, ps, count):
    pe, act, dve, pool, sp = nc.tensor, nc.scalar, nc.vector, nc.gpsimd, nc.sync
    c = ExitStack()
    Wqkv = sb(c, "Wqkv", [P, 3 * INNER])
    Wo = sb(c, "Wo", [P, LH // 2, D])
    W1 = sb(c, "W1", [P, 2 * FF])
    W2 = sb(c, "W2", [P, len(CH), D])
    b1 = sb(c, "b1", [P, 2, len(CH)])
    b2 = sb(c, "b2", [1, D])
    ln = sb(c, "ln", [P, 2])
    qks = sb(c, "qks", [P, 2, LD])
    rope = sb(c, "rope", [P, 2, NT, 2, LD])
    tab = sb(c, "tab", [P, 2, NT, 2, LD])
    mask = sb(c, "mask", [P, NT, 4 * KB], BF16)
    power = sb(c, "power3", [P, 2 * LH])
    xin = sb(c, "xin", [P, B, D])
    XS = sb(c, "XS", [P, B, WIN + P + 1])
    QK = sb(c, "QK", [P, 2, 2 * INNER])
    SQ = sb(c, "SQ", [P, 2 * INNER])
    T1 = sb(c, "T1", [P, 2, 2 * INNER])
    T2 = sb(c, "T2", [P, 2 * INNER])
    ss = sb(c, "ss", [P, 2, 2 * LH])
    rn = sb(c, "rn", [P, 2, 2 * LH])
    qT = sb(c, "qT", [P, 2, LH // 2, P])
    kT = sb(c, "kT", [P, B, LH // 2, WIN + P])
    E = sb(c, "Ew", [P, 2, LH, KB])
    mx = sb(c, "mx", [P, 2, LH])
    sm = sb(c, "sm", [P, 2, 2, LH])
    V = sb(c, "V", [KB, 2, 2, INNER])
    ET = sb(c, "ET", [KB, LH, P])
    OT = sb(c, "OT", [P, 2, LH // 2, P])
    x1 = sb(c, "x1", [P, B, D])
    FS = sb(c, "FS", [P, B, P + 1])
    fx = sb(c, "fx", [P, B, D])
    fst = sb(c, "fst", [P, B, 6])
    fmv = sb(c, "fmv", [P, B, 2])
    frs = sb(c, "frs", [P, B])
    fn = sb(c, "fn", [P, B, D])
    fnT = sb(c, "fnT", [P, B * P])
    G = sb(c, "G", [P, B * P])
    HH = sb(c, "HH", [P, len(CH), B * P])
    NR = 4
    R = ps(c, "R", [P, NR, 512])
    PS = ps(c, "PS", [P, 4, 512])

    names = dict(xi=1, xT=1, hal=1, xs=2, qk=4, qke=4, sq=1, t1=1, t2=1, ss=2, pw=1, ad=1, no=1,
                 tq=4, kh=1, te=4, s=2, mx=2, sub=2, ex=2, sum=1, rc=1, pn=1, vp=4, ve=4, pt=4, pe=4,
                 pv=2, oe=2, wo=1, x1=2, f1=1, fc=1, f1e=2, f2=1, f2e=1, fst=3, frs=1, fn=1, f3=1, f3e=1,
                 ff=6, g=3, hh=3, f5=1, fx=1)
    s = {k: count(c, "l_" + k, per) for k, per in names.items()}
    s_w = count(c, "l_w", 16 * 13)
    s_c = count(c, "l_c", 16)
    s_tab = count(c, "l_tab", 4)
    s_z = count(c, "l_z", 3)
    s_one = count(c, "l_one")

    sp.dma_start(rope[:, :, :, :, :], ins["rope"]).then_inc(s_c.sem, 16)
    sp.dma_start(mask[:, :, :], ins["mask"]).then_inc(s_c.sem, 16)
    pool.memset(power[:, :], -0.5).then_inc(s_one.sem, 1)
    pool.wait_ge(s_one.sem, 1)
    for e in (pe, dve):
        e.wait_ge(s_c.sem, 32)

    class At:

        def __init__(self, tile, step, t, first):
            self.tile, self.step, self.t, self.first = tile, step, t, first

    waited = {}

    def wait_once(e, name, base, d, k):
        k = s[name].per if k is None else k
        if waited.get((e.engine, name), (-99, 0)) >= (d, k):
            return
        waited[e.engine, name] = (d, k)
        s[name].wait(e, (base, d), k)

    def wait(e, name, at, d, k=None):
        if not (at.first and d < 0):
            wait_once(e, name, at.tile, d, k)

    def waitf(e, name, at, k=None, d=-1):
        wait_once(e, name, at.step, d, k)

    def time_of(at, d):
        return at.t + d // B

    def inc(i, name, n=1):
        return i.then_inc(s[name].sem, n)

    class Ring:

        def __init__(self):
            self.n, self.last = 0, [None] * NR

        def take(self, at):
            r = self.n % NR
            self.n += 1
            if self.last[r]:
                kind, name, d, k = self.last[r]
                if kind == "tile":
                    wait(pe, name, at, d, k)
                else:
                    waitf(pe, name, at, k, d)
            self.last[r] = None
            return r

        def read(self, r, name, d, k, kind="tile"):
            self.last[r] = (kind, name, d, k)

        def next_body(self):
            self.last = [x and (x[0], x[1], x[2] - (B if x[0] == "tile" else 1), x[3]) for x in self.last]

    ring = Ring()

    def input_T(at, d):
        b, t = d % B, time_of(at, d)
        wait(dve, "xT", at, d - B)
        inc(dve.tensor_scalar_mul(xin[:, b, :], X[:, b, t, :], 1.0), "xi")
        r = ring.take(at)
        wait(pe, "xi", at, d)
        inc(pe.transpose(R[:, r, 0:P], xin[:, b, :], ident[:, :]), "xT")
        wait(act, "vp", at, d - B)
        inc(act.activation(XS[:, b, 0:WIN + 1], XS[:, b, P:P + WIN + 1], ACT.Copy), "hal")
        wait(act, "xT", at, d)
        wait(act, "hal", at, d)
        hc = D // 2
        inc(act.activation(XS[0:hc, b, WIN:WIN + P], R[0:hc, r, 0:P], ACT.Copy), "xs")
        inc(act.activation(XS[hc:D, b, WIN + 1:WIN + 1 + P], R[hc:D, r, 0:P], ACT.Copy), "xs")
        ring.read(r, "xs", d, 2)

    def project_qk(at, d):
        b, p = d % B, d % 2
        wait(pe, "xs", at, d)
        for j in range(4):
            r = ring.take(at)
            inc(pe.matmul(R[:, r, :], XS[:, b, WIN:WIN + P], Wqkv[:, j * 512:(j + 1) * 512],
                          start=True, stop=True), "qk")
            wait(act, "qk", at, d, j + 1)
            if j == 0:
                wait(act, "t2", at, d - 2)
            inc(act.activation(QK[:, p, j * 512:(j + 1) * 512], R[:, r, :], ACT.Copy), "qke")
            ring.read(r, "qke", d, j + 1)

    def rotate(at, d):
        p, t = d % 2, time_of(at, d)
        wait(act, "qke", at, d)
        wait(act, "ss", at, d - 1, 1)
        inc(act.activation(SQ[:, :], QK[:, p, :], ACT.Square), "sq")
        q = QK[:, p, :].rearrange("p (i h e) -> p i h e", i=2, e=LD)
        t1 = T1[:, p, :].rearrange("p (i h e) -> p i h e", i=2, e=LD)
        t2 = T2[:, :].rearrange("p (i h e) -> p i h e", i=2, e=LD)
        tb = tab[:, :, t, :, :]
        wait(dve, "qke", at, d)
        wait(dve, "tq", at, d - 2)
        inc(dve.tensor_tensor(out=t1, in0=q, in1=tb[:, 0].unsqueeze(2).broadcast_to([P, 2, LH, LD]),
                              op=ALU.mult), "t1")
        wait(dve, "ad", at, d - 1)
        hf = LD // 2
        for j in range(2):
            i = dve.tensor_tensor(out=t2[:, :, :, j * hf:(j + 1) * hf], in0=q[:, :, :, (1 - j) * hf:(2 - j) * hf],
                                  in1=tb[:, 1, :, j * hf:(j + 1) * hf].unsqueeze(2).broadcast_to([P, 2, LH, hf]),
                                  op=ALU.mult)
        inc(i, "t2")
        wait(pool, "t2", at, d)
        wait(pool, "t1", at, d)
        inc(pool.tensor_tensor(out=T1[:, p, :], in0=T1[:, p, :], in1=T2[:, :], op=ALU.add), "ad")
        wait(dve, "sq", at, d)
        wait(dve, "pw", at, d - 2)
        inc(dve.reduce_sum(ss[:, p, :], SQ[:, :].rearrange("p (h e) -> p h e", e=LD), axis=AX.X), "ss")
        wait(dve, "ss", at, d, 1)
        inc(dve.tensor_scalar_max(ss[:, p, :], ss[:, p, :], 1e-24), "ss")
        wait(pool, "ss", at, d, 2)
        wait(pool, "no", at, d - 2)
        inc(pool.tensor_tensor(out=rn[:, p, :], in0=ss[:, p, :], in1=power[:, :], op=ALU.pow), "pw")

    def normalise(at, d):
        p = d % 2
        wait(dve, "ad", at, d)
        wait(dve, "pw", at, d)
        t1 = T1[:, p, :].rearrange("p (h e) -> p h e", e=LD)
        inc(dve.tensor_tensor(out=t1, in0=t1, in1=rn[:, p, :].unsqueeze(2).broadcast_to([P, 2 * LH, LD]),
                              op=ALU.mult), "no")

    def transpose_qk(at, d):
        b, p = d % B, d % 2
        wait(pe, "no", at, d)
        for j in range(4):
            r = ring.take(at)
            for i in range(4):
                mm = pe.transpose(R[:, r, i * P:(i + 1) * P], T1[:, p, (4 * j + i) * P:(4 * j + i + 1) * P], ident[:, :])
            inc(mm, "tq")
            wait(act, "tq", at, d, j + 1)
            src = R[:, r, :].rearrange("p (i n) -> p i n", i=4)
            if j < 2:
                inc(act.activation(qT[:, p, 4 * j:4 * j + 4, :], src, ACT.Copy), "te")
            else:
                if j == 2:
                    inc(act.activation(kT[:, b, :, 0:WIN], kT[:, b, :, P:P + WIN], ACT.Copy), "kh")
                    wait(act, "kh", at, d)
                inc(act.activation(kT[:, b, 4 * j - 8:4 * j - 4, WIN:WIN + P], src, ACT.Copy), "te")
            ring.read(r, "te", d, j + 1)

    def scores(at, d):
        b, p, t = d % B, d % 2, time_of(at, d)
        wait(pe, "te", at, d)
        for hf in range(2):
            wait(pe, "sub", at, d - 1, hf + 1)
            for par in range(2):
                bank = 2 * hf + par
                pe.matmul(PS[:, bank, 0:4 * KB], ident_b[:, :], mask[:, t, :], start=True, stop=False,
                          skip_group_check=True)
                o = par * LD
                for g in range(2):
                    for j in range(4):
                        pair = 4 * hf + j
                        mm = pe.matmul(PS[g * QB:(g + 1) * QB, bank, j * KB:(j + 1) * KB],
                                       qT[o:o + LD, p, pair, g * QB:(g + 1) * QB],
                                       kT[o:o + LD, b, pair, g * QB:g * QB + KB],
                                       start=False, stop=True, skip_group_check=True)
            inc(mm, "s")
            view = PS[:, 2 * hf:2 * hf + 2, 0:4 * KB].rearrange("p a (j k) -> p a j k", k=KB)
            m = mx[:, p, 8 * hf:8 * hf + 8].rearrange("p (a j) -> p a j", a=2)
            e = E[:, p, 8 * hf:8 * hf + 8, :].rearrange("p (a j) k -> p a j k", a=2)
            wait(dve, "s", at, d, hf + 1)
            inc(dve.reduce_max(m, view, axis=AX.X), "mx")
            wait(dve, "mx", at, d, hf + 1)
            if hf == 0:
                wait(dve, "pt", at, d - 2)
            inc(dve.tensor_tensor(out=e, in0=view, in1=m.unsqueeze(3).broadcast_to([P, 2, 4, KB]),
                                  op=ALU.subtract), "sub")
            wait(act, "sub", at, d, hf + 1)
            ee = E[:, p, 8 * hf:8 * hf + 8, :]
            inc(act.activation(ee, ee, ACT.Exp), "ex")
        wait(dve, "ex", at, d)
        inc(dve.reduce_sum(sm[:, p, 0, :], E[:, p, :, :], axis=AX.X), "sum")
        wait(dve, "sum", at, d)
        wait(dve, "pn", at, d - 2)
        inc(dve.reciprocal(sm[:, p, 1, :], sm[:, p, 0, :]), "rc")
        wait(pool, "rc", at, d)
        inc(pool.tensor_tensor(out=E[:, p, :, :], in0=E[:, p, :, :],
                               in1=sm[:, p, 1, :].unsqueeze(2).broadcast_to([P, LH, KB]), op=ALU.mult), "pn")

    def project_v(at, d):
        b, p = d % B, d % 2
        for j in range(4):
            g, half = divmod(j, 2)
            r = ring.take(at)
            inc(pe.matmul(R[0:KB, r, :], XS[:, b, g * QB:g * QB + KB],
                          Wqkv[:, 2 * INNER + half * 512:2 * INNER + (half + 1) * 512], start=True, stop=True), "vp")
            wait(act, "vp", at, d, j + 1)
            inc(act.activation(V[:, p, g, half * 512:(half + 1) * 512], R[0:KB, r, :], ACT.Copy), "ve")
            ring.read(r, "ve", d, j + 1)

    def attend(at, d):
        b, p, t = d % B, d % 2, time_of(at, d)
        wait(pe, "pn", at, d)
        for j in range(4):
            r = ring.take(at)
            for i in range(4):
                mm = pe.transpose(R[0:KB, r, i * P:(i + 1) * P], E[:, p, 4 * j + i, :], ident[:, :])
            inc(mm, "pt")
            wait(act, "pt", at, d, j + 1)
            inc(act.activation(ET[:, 4 * j:4 * j + 4, :], R[0:KB, r, :].rearrange("p (i n) -> p i n", i=4),
                               ACT.Copy), "pe")
            ring.read(r, "pe", d, j + 1)
        wait(pe, "ve", at, d)
        for hf in range(2):
            wait(pe, "pe", at, d, 2 * hf + 2)
            r = ring.take(at)
            for j in range(4):
                pair = 4 * hf + j
                for g in range(2):
                    for par in range(2):
                        mm = pe.matmul(R[par * LD:(par + 1) * LD, r, j * P + g * QB:j * P + (g + 1) * QB],
                                       V[:, p, g, (2 * pair + par) * LD:(2 * pair + par + 1) * LD],
                                       ET[:, 8 * hf + 4 * par + j, g * QB:(g + 1) * QB], start=True, stop=True,
                                       skip_group_check=True)
            inc(mm, "pv")
            wait(act, "pv", at, d, hf + 1)
            inc(act.activation(OT[:, p, 4 * hf:4 * hf + 4, :], R[:, r, :].rearrange("p (j n) -> p j n", j=4),
                               ACT.Copy), "oe")
            ring.read(r, "oe", d, hf + 1)
        wait(pe, "oe", at, d)
        r = ring.take(at)
        for pair in range(LH // 2):
            mm = pe.matmul(R[:, r, 0:D], OT[:, p, pair, :], Wo[:, pair, :], start=(pair == 0),
                           stop=(pair == LH // 2 - 1))
        inc(mm, "wo")
        wait(dve, "wo", at, d)
        inc(dve.tensor_tensor(out=x1[:, b, :], in0=R[:, r, 0:D], in1=X[:, b, t, :], op=ALU.add), "x1")
        ring.read(r, "x1", d, 1)
        wait(dve, "x1", at, d, 1)
        inc(dve.tensor_scalar_mul(X[:, b, t, :], x1[:, b, :], 1.0), "x1")

    def ff_shift(at):
        r = ring.take(at)
        wait(pe, "x1", at, -1, 2) if not at.first else None
        for b in range(B):
            mm = pe.transpose(R[:, r, b * P:(b + 1) * P], x1[:, b, :], ident[:, :])
        inc(mm, "f1")
        hc = D // 2
        waitf(act, "f1", at)
        inc(act.activation(FS[hc:D, :, 0:1], FS[hc:D, :, P:P + 1], ACT.Copy), "fc")
        waitf(act, "fc", at)
        src = R[:, r, :].rearrange("p (b n) -> p b n", b=B)
        inc(act.activation(FS[0:hc, :, 0:P], src[0:hc], ACT.Copy), "f1e")
        inc(act.activation(FS[hc:D, :, 1:P + 1], src[hc:D], ACT.Copy), "f1e")
        ring.read(r, "f1e", -1, 2, "step")

    def ff_stats(at):
        waitf(pe, "f1e", at)
        r = ring.take(at)
        for b in range(B):
            mm = pe.transpose(R[:, r, b * P:(b + 1) * P], FS[:, b, 0:P], ident[:, :])
        inc(mm, "f2")
        waitf(dve, "f2", at)
        inc(dve.tensor_copy(fx[:, :, :], R[:, r, :].rearrange("p (b n) -> p b n", b=B)), "f2e")
        ring.read(r, "f2e", -1, 1, "step")
        waitf(dve, "f2e", at)
        for b in range(B):
            i = dve.bn_stats(fst[:, b, :], fx[:, b, :])
        inc(i, "fst")
        waitf(dve, "fst", at, 1)
        dve.memset(spare[:, :], 0.0)
        for b in range(B):
            i = dve.bn_aggr(fmv[:, b, :], fst[:, b, :])
        inc(i, "fst")
        waitf(dve, "fst", at, 2)
        inc(dve.tensor_scalar_add(fmv[:, :, 1:2], fmv[:, :, 1:2], LN_EPS), "fst")
        waitf(pool, "fst", at, 3)
        inc(pool.tensor_tensor(out=frs[:, :], in0=fmv[:, :, 1], in1=power[:, 0:B], op=ALU.pow), "frs")

    def ff_norm(at):
        waitf(dve, "frs", at)
        for b in range(B):
            i = dve.tensor_scalar(fn[:, b, :], fx[:, b, :], fmv[:, b, 0:1], frs[:, b:b + 1],
                                  ALU.subtract, ALU.mult)
        inc(i, "fn")
        waitf(pe, "fn", at)
        r = ring.take(at)
        for b in range(B):
            mm = pe.transpose(R[:, r, b * P:(b + 1) * P], fn[:, b, :], ident[:, :])
        inc(mm, "f3")
        waitf(act, "f3", at)
        inc(act.activation(fnT[:, :], R[:, r, :], ACT.Identity, bias=ln[:, 1:2], scale=ln[:, 0:1]), "f3e")
        ring.read(r, "f3e", -1, 1, "step")

    def ff_up(at):
        waitf(pe, "f3e", at)
        for i, (lo, w) in enumerate(CH):
            rg = ring.take(at)
            inc(pe.matmul(R[0:w, rg, :], W1[:, FF + lo:FF + lo + w], fnT[:, :], start=True, stop=True), "ff")
            ra = ring.take(at)
            inc(pe.matmul(R[0:w, ra, :], W1[:, lo:lo + w], fnT[:, :], start=True, stop=True), "ff")
            waitf(act, "ff", at, 2 * i + 1)
            if i > 0:
                waitf(act, "hh", at, i)
            inc(act.activation(G[0:w, :], R[0:w, rg, :], ACT.Gelu, bias=b1[0:w, 1, i:i + 1]), "g")
            ring.read(rg, "g", -1, i + 1, "step")
            waitf(dve, "ff", at, 2 * i + 2)
            waitf(dve, "g", at, i + 1)
            inc(dve.scalar_tensor_tensor(HH[0:w, i, :], R[0:w, ra, :], b1[0:w, 0, i:i + 1], G[0:w, :],
                                         ALU.add, ALU.mult), "hh")
            ring.read(ra, "hh", -1, i + 1, "step")

    def ff_down(at):
        waitf(pe, "hh", at)
        r = ring.take(at)
        for b in range(B):
            for i, (lo, w) in enumerate(CH):
                pe.matmul(R[:, r, b * P:(b + 1) * P], HH[0:w, i, b * P:(b + 1) * P], W2[0:w, i, :],
                          start=(i == 0), stop=False)
            mm = pe.matmul(R[:, r, b * P:(b + 1) * P], ones[0:1, :], b2[:, :], start=False, stop=True)
        inc(mm, "f5")
        waitf(dve, "f5", at)
        xt = X[:, :, at.t - 1, :]
        inc(dve.tensor_tensor(out=xt, in0=xt, in1=R[:, r, :].rearrange("p (b n) -> p b n", b=B),
                              op=ALU.add), "fx")
        ring.read(r, "fx", -1, 1, "step")
        ring.n += 2

    def body(at, n_new=B, ff=True, n_old=B):
        waited.clear()
        for d in range(n_old):
            new = d < n_new
            if new:
                input_T(at, d)
            else:
                ring.n += 1
            back1 = (d - 1 >= 0 or not at.first) and d - 1 < n_new
            back2 = (d - 2 >= 0 or not at.first) and d - 2 < n_new
            if back1:
                transpose_qk(at, d - 1)
            else:
                ring.n += 4
            if new:
                project_qk(at, d)
                rotate(at, d)
            else:
                ring.n += 4
            if ff and d == 2:
                ff_shift(at)
            if ff and d == 3:
                ff_norm(at)
            if back2:
                project_v(at, d - 2)
            else:
                ring.n += 4
            if ff and d == 3:
                ff_up(at)
            if back1:
                scores(at, d - 1)
            if ff and d == 2:
                ff_stats(at)
            if ff and d == 3:
                ff_down(at)
            if back2:
                attend(at, d - 2)
            else:
                ring.n += 7
            if new:
                normalise(at, d)

    with nc.Fori(0, NL) as l:
        nw = 0
        for dst, src in (
            (Wqkv[:, :], ins["Wqkv"][l]),
            (qks[:, 0, :], ins["q_scale"][l].partition_broadcast(P)),
            (qks[:, 1, :], ins["k_scale"][l].partition_broadcast(P)),
            (Wo[:, :, :], ins["Wo"][l].rearrange("(a p) n -> p a n", p=P)),
            (W1[:, :], ins["W1"][l]),
            (W2[:, 0:2, :], ins["W2"][l, 0:2 * P].rearrange("(a p) n -> p a n", p=P)),
            (W2[0:FF - 2 * P, 2, :], ins["W2"][l, 2 * P:FF]),
            *((b1[0:w, :, i], ins["b1"][l].rearrange("(i f) -> f i", i=2)[lo:lo + w]) for i, (lo, w) in enumerate(CH)),
            (b2[:, :], ins["b2"][l].unsqueeze(0)),
            (ln[:, 0:1], ins["ln_g"][l].unsqueeze(1)),
            (ln[:, 1:2], ins["ln_b"][l].unsqueeze(1)),
        ):
            with nc.allow_non_contiguous_dma("small columns"):
                sp.dma_start(dst, src).then_inc(s_w.sem, 16)
            nw += 1
        assert 16 * nw == s_w.per
        pool.memset(XS[:, :, :], 0.0).then_inc(s_z.sem, 1)
        pool.memset(kT[:, :, :, P:P + WIN], 0.0).then_inc(s_z.sem, 1)
        pool.memset(FS[:, :, :], 0.0).then_inc(s_z.sem, 1)
        for e in (dve, pe, act):
            s_w.wait(e, (l, 0))
        s_z.wait(act, (l, 0))
        hf = LD // 2
        for i in range(2):
            dve.tensor_tensor(out=tab[:, 0, :, i, :], in0=rope[:, 0, :, i, :],
                              in1=qks[:, i, :].unsqueeze(1).broadcast_to([P, NT, LD]),
                              op=ALU.mult).then_inc(s_tab.sem, 1)
            for j in range(2):
                k = dve.tensor_tensor(out=tab[:, 1, :, i, j * hf:(j + 1) * hf],
                                      in0=rope[:, 1, :, i, j * hf:(j + 1) * hf],
                                      in1=qks[:, i, (1 - j) * hf:(2 - j) * hf].unsqueeze(1).broadcast_to([P, NT, hf]),
                                      op=ALU.mult)
            k.then_inc(s_tab.sem, 1)
        s_tab.wait(dve, (l, 0))

        tile0, step0 = l * (NT * B), l * NT
        ring.n, ring.last = 0, [None] * NR
        body(At(tile0, step0, 0, True), ff=False)
        ring.next_body()
        start = (ring.n % NR, list(ring.last))
        with nc.Fori(1, NT) as t:
            body(At(tile0 + t * B, step0 + t, t, False))
            ring.next_body()
            assert start == (ring.n % NR, ring.last), (start, ring.n % NR, ring.last)
        end = At(tile0 + NT * B, step0 + NT, NT, False)
        body(end, n_new=0, ff=False, n_old=2)
        waited.clear()
        for f in (ff_shift, ff_stats, ff_norm, ff_up, ff_down):
            f(end)
        nc.all_engine_barrier()
    c.close()


def tables():
    f32 = np.float32
    half = np.arange(0, LD, 2, dtype=f32)
    inv = (f32(1.0) / np.power(f32(10000.0), half / f32(LD))).astype(f32)
    t = np.arange(S, dtype=f32)
    fr = (t[:, None] * inv[None, :]).astype(f32)
    fr = np.concatenate([fr, fr], -1)
    base = ((half + f32(0.4 * LD)) / f32(1.4 * LD)).astype(f32)
    power = ((t - S // 2) / (WIN // 2)).astype(f32)
    sc = np.power(base[None, :], power[:, None]).astype(f32)
    sc = np.concatenate([sc, sc], -1)
    cos, sin = np.cos(fr).astype(f32), np.sin(fr).astype(f32)
    sign = np.where(np.arange(LD) < LD // 2, f32(-1), f32(1))
    q_k = []
    for scale in (sc * f32(8.0), (f32(1.0) / sc).astype(f32)):
        q_k.append(np.stack([cos * scale, sin * sign * scale]))
    r = np.stack(q_k, 2)
    rope = np.ascontiguousarray(r.reshape(2, NT, P, 2, LD).transpose(2, 0, 1, 3, 4)).astype(f32)
    q = np.arange(P)
    k = np.arange(KB)
    i = q[:, None] % QB
    ok = (k[None, :] >= i) & (k[None, :] <= i + WIN)
    m = np.zeros((P, NT, 4, KB), f32)
    m[~np.broadcast_to(ok[:, None, None, :], m.shape)] = MASKED
    pad = (q[:, None] < QB) & (k[None, :] < WIN)
    m[:, 0][np.broadcast_to(pad[:, None, :], (P, 4, KB))] = MASKED
    return rope, m.reshape(P, NT, 4 * KB)


def kernel(**inputs):
    import concourse.bacc as bacc
    from concourse.bass_utils import run_bass_kernel_spmd

    a = {k: np.asarray(v) for k, v in inputs.items()}
    rope, mask = tables()
    arrays = {
        "X": a["L0_attn_X"], "wqT": a["L0_attn_Wq"].T, "wkT": a["L0_attn_Wk"].T, "wvT": a["L0_attn_Wv"].T,
        "woT": a["L0_attn_Wo"].T, "bq": a["L0_attn_bq"].reshape(D, 1), "bk": a["L0_attn_bk"].reshape(D, 1),
        "bv": a["L0_attn_bv"].reshape(1, D), "bo": a["L0_attn_bo"].reshape(1, D),
        "Wqkv": a["L0_ffn_Wqkv"], "q_scale": a["L0_ffn_q_scale"], "k_scale": a["L0_ffn_k_scale"],
        "Wo": a["L0_ffn_Wo"], "ln_g": a["L0_ffn_ln_g"], "ln_b": a["L0_ffn_ln_b"], "W1": a["L0_ffn_W1"],
        "b1": a["L0_ffn_b1"], "W2": a["L0_ffn_W2"], "b2": a["L0_ffn_b2"], "cT": a["L0_c"].T,
        "wmod": a["L0_wmod"], "rope": rope, "mask": mask.astype(mybir.dt.np(BF16)),
    }
    arrays = {k: np.ascontiguousarray(v) for k, v in arrays.items()}
    nc = bacc.Bacc("TRN2", target_bir_lowering=False, num_devices=1)
    ins = {k: nc.dram_tensor(f"in_{k}", v.shape, mybir.dt.from_np(v.dtype), kind="ExternalInput").ap()
           for k, v in arrays.items()}
    out = nc.dram_tensor("out", (B, S, D), F32, kind="ExternalOutput").ap()
    build(nc, ins, out)
    r = run_bass_kernel_spmd(nc, [{f"in_{k}": v for k, v in arrays.items()}], core_ids=[0])
    return r.results[0]["out"]
```

```python
from contextlib import ExitStack

import numpy as np
import concourse.bass as bass
from concourse import mybir

F32 = mybir.dt.float32
BF16 = mybir.dt.bfloat16
ALU = mybir.AluOpType
ACT = mybir.ActivationFunctionType
AX = mybir.AxisListType

P = 128
B, S, D = 4, 1024, 128
NT = S // P
H, DH = 16, 8
NL = 6
LH, LD = 16, 64
INNER = LH * LD
WIN = 32
FF = int(D * 4 * 2 / 3)
LN_EPS = 1e-5
MASKED = -1e30

QB = 64
KB = QB + WIN
CH = [(c * P, min(P, FF - c * P)) for c in range((FF + P - 1) // P)]

NPART = 3
NPROD = NPART * NPART * DH
MROW = 96
KROWS = MROW + 2
GH = 4
NG = B * H // GH
VW = 32


class Count:

    def __init__(self, sem, per=1):
        self.sem, self.per = sem, per

    def at(self, n, k=None):
        k = self.per if k is None else k
        if isinstance(n, tuple):
            base, off = n
            return base * self.per + (self.per * off + k)
        return self.per * n + k

    def wait(self, engine, n, k=None):
        engine.wait_ge(self.sem, self.at(n, k))


def build(nc, ins, out):
    pe, act, dve, pool, sp = nc.tensor, nc.scalar, nc.vector, nc.gpsimd, nc.sync
    whole = ExitStack()

    def sb(ctx, name, shape, dt=F32):
        return ctx.enter_context(nc.sbuf_tensor(name, shape, dt))

    def ps(ctx, name, shape, dt=F32):
        return ctx.enter_context(nc.psum_tensor(name, shape, dt))

    def count(ctx, name, per=1):
        return Count(ctx.enter_context(nc.semaphore(name)), per)

    X = sb(whole, "X", [P, B, NT, D])
    ident = sb(whole, "ident", [P, P])
    ident_b = sb(whole, "ident_b", [P, P], BF16)
    ones = sb(whole, "ones", [P, P])
    gate_b = sb(whole, "gate_b", [P, B, D])
    spare = sb(whole, "spare", [P, 1])
    x_mid = nc.dram_tensor("x_mid", [P, B, NT, D], F32, kind="Internal").ap()
    parts_d = [nc.dram_tensor(f"parts_{n}", [B, NPART, P, S], BF16, kind="Internal").ap() for n in "qk"]
    x_dram = ins["X"].rearrange("b (t p) c -> p b t c", p=P)
    out_dram = out.rearrange("b (t p) c -> p b t c", p=P)

    first = ExitStack()
    mod = sb(first, "mod", [P, 6, B, D])
    VA = sb(first, "VA", [P, B, NT, H, DH + 1])
    AO = sb(first, "AO", [P, B, NT, D])
    woT = sb(first, "woT", [P, D])
    rows = sb(first, "rows", [1, 2, D])

    with ExitStack() as c:
        cT = sb(c, "cT", [P, B])
        wmod = sb(c, "wmod", [P, 6 * D])
        sig = sb(c, "sig", [P, 3, B])
        modT = sb(c, "modT", [P, 6, B])
        tmp = sb(c, "tmp", [P, 2, 2, B])
        diag = sb(c, "diag", [P, 6, B, D])
        p_mod = ps(c, "p_mod", [P, 6, B])
        p_bc = ps(c, "p_bc", [P, 6, B, D])
        s_in = count(c, "s_in", 16)
        s_cst = count(c, "s_cst")
        s_v = count(c, "s_v")
        s_e = count(c, "s_e")
        s_m = count(c, "s_m")
        s_dg = count(c, "s_dg")
        s_bc = count(c, "s_bc")
        s_mc = count(c, "s_mc")
        for dst, src in ((cT[:, :], ins["cT"]), (wmod[:, :], ins["wmod"]), (X[:, :, :, :], x_dram),
                         (woT[:, :], ins["woT"]), (rows[:, 0, :], ins["bv"]), (rows[:, 1, :], ins["bo"])):
            sp.dma_start(dst, src).then_inc(s_in.sem, 16)
        pool.memset(ident[:, :], 0.0).then_inc(s_cst.sem, 1)
        pool.memset(ones[:, :], 1.0).then_inc(s_cst.sem, 1)
        pool.memset(VA[:, :, :, :, DH:DH + 1], 1.0).then_inc(s_cst.sem, 1)
        pool.wait_ge(s_cst.sem, 3)
        pool.affine_select(out=ident[:, :], in_=ident[:, :], compare_op=ALU.not_equal, fill=1.0,
                           base=0, pattern=[[-1, P]], channel_multiplier=1).then_inc(s_cst.sem, 1)
        act.wait_ge(s_in.sem, 16 * 6)
        act.activation(sig[:, 0, :], cT[:, :], ACT.Exp, scale=-1.0).then_inc(s_e.sem, 1)
        n_v = 0

        def step(ins_):
            nonlocal n_v
            n_v += 1
            ins_.then_inc(s_v.sem, 1)
            dve.wait_ge(s_v.sem, n_v)

        dve.wait_ge(s_cst.sem, 4)
        step(dve.tensor_copy(ident_b[:, :], ident[:, :]))
        dve.wait_ge(s_e.sem, 1)
        step(dve.tensor_scalar_add(sig[:, 1, :], sig[:, 0, :], 1.0))
        step(dve.reciprocal(sig[:, 2, :], sig[:, 1, :]))
        step(dve.tensor_tensor(out=sig[:, 0, :], in0=cT[:, :], in1=sig[:, 2, :], op=ALU.mult))
        pe.wait_ge(s_v.sem, n_v)
        pe.wait_ge(s_in.sem, 16 * 6)
        for j in range(6):
            mm = pe.matmul(p_mod[:, j, :], wmod[:, j * D:(j + 1) * D], sig[:, 0, :], start=True, stop=True)
        mm.then_inc(s_m.sem, 1)
        dve.wait_ge(s_m.sem, 1)
        step(dve.tensor_copy(modT[:, :, :], p_mod[:, :, :]))
        scales, gates = modT[:, 1:5:3, :], modT[:, 2:6:3, :]
        step(dve.tensor_scalar_add(scales, scales, 1.0))
        step(dve.tensor_scalar(tmp[:, 0, :, :], gates, -1.0, None, ALU.mult))
        step(dve.tensor_tensor(out=tmp[:, 0, :, :], in0=gates, in1=tmp[:, 0, :, :], op=ALU.max))
        step(dve.tensor_scalar_max(tmp[:, 0, :, :], tmp[:, 0, :, :], 0.25))
        step(dve.tensor_scalar(tmp[:, 1, :, :], gates, 0.0, 2.0, ALU.is_ge, ALU.mult))
        step(dve.tensor_scalar_add(tmp[:, 1, :, :], tmp[:, 1, :, :], -1.0))
        step(dve.tensor_tensor(out=gates, in0=tmp[:, 0, :, :], in1=tmp[:, 1, :, :], op=ALU.mult))
        for j in range(6):
            for b in range(B):
                dg = dve.tensor_scalar(diag[:, j, b, :], ident[:, :], modT[:, j, b:b + 1], None, ALU.mult)
            dg.then_inc(s_dg.sem, 1)
            s_dg.wait(pe, j)
            pe.matmul(p_bc[:, j, :, :], ones[:, :], diag[:, j, :, :], start=True, stop=True).then_inc(s_bc.sem, 1)
            s_bc.wait(act, j)
            act.activation(mod[:, j, :, :], p_bc[:, j, :, :], ACT.Copy).then_inc(s_mc.sem, 1)
        dve.wait_ge(s_mc.sem, 6)
        dve.tensor_copy(gate_b[:, :, :], mod[:, 5, :, :])
        nc.all_engine_barrier()

    CT = 4
    NC = B * NT // CT
    with ExitStack() as c:
        wT = [sb(c, f"w{n}T", [P, D]) for n in "qkv"]
        bias = sb(c, "bias_qk", [P, 2])
        stats = sb(c, "stats", [P, 2, CT, 6])
        mv = sb(c, "mv", [P, 2, CT, 2])
        power = sb(c, "power", [P, CT])
        rstd = sb(c, "rstd", [P, 2, CT])
        hn = sb(c, "hn", [P, 2, CT, D])
        hT = sb(c, "hT", [P, 2, CT * P])
        full = sb(c, "full", [P, 2, 2, CT * P])
        rest = sb(c, "rest", [P, 2, CT * P])
        parts = sb(c, "parts", [P, 2, 2, NPART, CT * P], BF16)
        p_t = ps(c, "p_t", [P, 2, CT * P])
        p_qk = ps(c, "p_qk", [P, 2, 2, CT * P])
        p_v = ps(c, "p_v", [P, 2, CT, D])
        s_w = count(c, "s_w", 16)
        s_pw = count(c, "s_pw")
        s_ln = count(c, "s_ln", 6)
        s_rs = count(c, "s_rs")
        s_t = count(c, "s_t")
        s_hT = count(c, "s_hT")
        s_qk = count(c, "s_qk", 2)
        s_vp = count(c, "s_vp")
        s_full = count(c, "s_full", 2)
        s_va = count(c, "s_va")
        s_sp = count(c, "s_sp", 10)
        s_pd = [[count(c, f"s_pd{u}{n}", 16) for n in "qk"] for u in range(2)]
        for dst, src in ((wT[0][:, :], ins["wqT"]), (wT[1][:, :], ins["wkT"]), (wT[2][:, :], ins["wvT"]),
                         (bias[:, 0:1], ins["bq"]), (bias[:, 1:2], ins["bk"])):
            sp.dma_start(dst, src).then_inc(s_w.sem, 16)
        pool.memset(power[:, :], -0.5).then_inc(s_pw.sem, 1)
        pool.wait_ge(s_pw.sem, 1)
        pe.wait_ge(s_w.sem, 16 * 5)
        act.wait_ge(s_w.sem, 16 * 5)

        def layernorm(n, b, u, fresh):
            for j in range(CT):
                i = dve.bn_stats(stats[:, u, j, :], X[:, b, CT * u + j, :])
            i.then_inc(s_ln.sem, 1)
            s_ln.wait(dve, n, 1)
            dve.memset(spare[:, :], 0.0)
            for j in range(CT):
                i = dve.bn_aggr(mv[:, u, j, :], stats[:, u, j, :])
            i.then_inc(s_ln.sem, 1)
            s_ln.wait(dve, n, 2)
            dve.tensor_scalar_add(mv[:, u, :, 1:2], mv[:, u, :, 1:2], LN_EPS).then_inc(s_ln.sem, 1)
            s_ln.wait(pool, n, 3)
            pool.tensor_tensor(out=rstd[:, u, :], in0=mv[:, u, :, 1], in1=power[:, :], op=ALU.pow)\
                .then_inc(s_rs.sem, 1)
            s_rs.wait(dve, n)
            if not fresh:
                s_t.wait(dve, (n[0], n[1] - 2))
            for j in range(CT):
                i = dve.tensor_scalar(hn[:, u, j, :], X[:, b, CT * u + j, :], mv[:, u, j, 0:1],
                                      rstd[:, u, j:j + 1], ALU.subtract, ALU.mult)
            i.then_inc(s_ln.sem, 1)
            for m, op in ((1, ALU.mult), (0, ALU.add)):
                s_ln.wait(dve, n, 5 - m)
                dve.tensor_tensor(out=hn[:, u, :, :], in0=hn[:, u, :, :],
                                  in1=mod[:, m, b, :].unsqueeze(1).broadcast_to([P, CT, D]),
                                  op=op).then_inc(s_ln.sem, 1)

        def chunk(n, b, u, fresh):
            layernorm(n, b, u, fresh)
            s_ln.wait(pe, n, 6)
            if not fresh:
                s_hT.wait(pe, (n[0], n[1] - 2))
            for j in range(CT):
                mm = pe.transpose(p_t[:, u, j * P:(j + 1) * P], hn[:, u, j, :], ident[:, :])
            mm.then_inc(s_t.sem, 1)
            s_t.wait(act, n)
            if not fresh:
                s_vp.wait(act, (n[0], n[1] - 2))
            act.activation(hT[:, u, :], p_t[:, u, :], ACT.Copy).then_inc(s_hT.sem, 1)
            s_hT.wait(pe, n)
            for i in range(2):
                if not fresh:
                    s_full.wait(pe, (n[0], n[1] - 2), i + 1)
                pe.matmul(p_qk[:, u, i, :], wT[i][:, :], hT[:, u, :], start=True, stop=True).then_inc(s_qk.sem, 1)
            if not fresh:
                s_va.wait(pe, (n[0], n[1] - 2))
            for j in range(CT):
                pe.matmul(p_v[:, u, j, :], hT[:, u, j * P:(j + 1) * P], wT[2][:, :], start=True, stop=False)
                mm = pe.matmul(p_v[:, u, j, :], ones[0:1, :], rows[:, 0, :], start=False, stop=True)
            mm.then_inc(s_vp.sem, 1)
            for i in range(2):
                s_qk.wait(act, n, i + 1)
                if not fresh:
                    s_sp.wait(act, (n[0], n[1] - 2))
                act.activation(full[:, u, i, :], p_qk[:, u, i, :], ACT.Identity,
                               bias=bias[:, i:i + 1]).then_inc(s_full.sem, 1)
            s_vp.wait(act, n)
            act.activation(VA[:, b, CT * u:CT * u + CT, :, 0:DH],
                           p_v[:, u, :, :].rearrange("p t (h d) -> p t h d", d=DH),
                           ACT.Copy).then_inc(s_va.sem, 1)
            for i in range(2):
                s_full.wait(dve, n, i + 1)
                if not fresh:
                    s_pd[u][i].wait(dve, (b, -1))
                k = 5 * i
                dve.tensor_copy(parts[:, u, i, 0, :], full[:, u, i, :]).then_inc(s_sp.sem, 1)
                s_sp.wait(dve, n, k + 1)
                dve.tensor_tensor(out=rest[:, i, :], in0=full[:, u, i, :], in1=parts[:, u, i, 0, :],
                                  op=ALU.subtract).then_inc(s_sp.sem, 1)
                s_sp.wait(dve, n, k + 2)
                dve.tensor_copy(parts[:, u, i, 1, :], rest[:, i, :]).then_inc(s_sp.sem, 1)
                s_sp.wait(dve, n, k + 3)
                dve.tensor_tensor(out=parts[:, u, i, 2, :], in0=rest[:, i, :], in1=parts[:, u, i, 1, :],
                                  op=ALU.subtract).then_inc(s_sp.sem, 2)
                s_sp.wait(sp, n, k + 5)
                sp.dma_start(parts_d[i][b, :, :, u * CT * P:(u + 1) * CT * P].rearrange("j p n -> p j n"),
                             parts[:, u, i, :, :]).then_inc(s_pd[u][i].sem, 16)

        for u in range(2):
            chunk(u, 0, u, True)
        with nc.Fori(1, B) as b:
            for u in range(2):
                chunk((b * 2, u), b, u, False)
        for u in range(2):
            for i in range(2):
                s_pd[u][i].wait(sp, B - 1)
        nc.all_engine_barrier()

    with ExitStack() as c:
        QA = sb(c, "QA", [KROWS, 2, 2, GH, 512], BF16)
        KA = sb(c, "KA", [KROWS, 2, GH, S], BF16)
        VG = sb(c, "VG", [P, 2, NT, GH, VW])
        E = sb(c, "E", [P, 4, GH, 512])
        negmax = sb(c, "negmax", [P, 2, GH, 4])
        nm = sb(c, "nm", [GH * 4, 2, P])
        nmb = sb(c, "nmb", [GH * 4, 2, 2, P], BF16)
        OE = sb(c, "OE", [P, 2, 512])
        rsum = sb(c, "rsum", [P, 2, 4, GH])
        p_max = ps(c, "p_max", [P, 2, S])
        p_s = ps(c, "p_s", [P, 2, 512])
        p_o = ps(c, "p_o", [P, 2, 512])
        HU = 16
        s_z = count(c, "s_z")
        s_ld = count(c, "s_ld", 16 * 3 * NPART * NPART)
        s_vg = count(c, "s_vg")
        s_mx = count(c, "s_mx", 2 * HU + 2)
        s_mr = count(c, "s_mr", 2 * HU + 2)
        s_mb = count(c, "s_mb", 4)
        s_md = count(c, "s_md", 64)
        s_st = count(c, "s_st", 64)
        s_ex = count(c, "s_ex", 64)
        s_pv = count(c, "s_pv", 16)
        s_oe = count(c, "s_oe", 2)
        s_ot = count(c, "s_ot", 2)
        s_rc = count(c, "s_rc", 2)
        s_ao = count(c, "s_ao", 2)

        pool.memset(QA[:, :, :, :, :], 0.0).then_inc(s_z.sem, 1)
        pool.memset(VG[:, :, :, :, :], 0.0).then_inc(s_z.sem, 1)
        dve.memset(KA[:, :, :, :], 0.0).then_inc(s_z.sem, 1)
        dve.wait_ge(s_z.sem, 3)
        dve.memset(KA[MROW:KROWS, :, :, :], 1.0).then_inc(s_z.sem, 1)
        sp.wait_ge(s_z.sem, 4)
        pool.wait_ge(s_z.sem, 4)
        pe.wait_ge(s_z.sem, 4)

        def add(n, d):
            return (n[0], n[1] + d) if isinstance(n, tuple) else n + d

        def heads(hg):
            return slice(hg * GH, hg * GH + GH) if isinstance(hg, int) else bass.ds(hg * GH, GH)

        def load(n, b, hg, p, reuse):
            if reuse:
                s_st.wait(sp, add(n, -2))
            for i in range(NPART):
                for j in range(NPART):
                    r = (i * NPART + j) * DH
                    q = parts_d[0][b, i].rearrange("(h d) n -> d h n", d=DH)
                    k = parts_d[1][b, j].rearrange("(h d) n -> d h n", d=DH)
                    for qh in range(2):
                        sp.dma_start(QA[r:r + DH, p, qh, :, :], q[:, heads(hg), qh * 512:(qh + 1) * 512])\
                            .then_inc(s_ld.sem, 16)
                    sp.dma_start(KA[r:r + DH, p, :, :], k[:, heads(hg), :]).then_inc(s_ld.sem, 16)

        def values(n, b, hg, p, reuse):
            if reuse:
                s_pv.wait(pool, add(n, -2))
            pool.tensor_copy(VG[:, p, :, :, 0:DH + 1], VA[:, b, :, heads(hg), :]).then_inc(s_vg.sem, 1)

        unit_log = {}

        def max_unit(n, p, qh, i, reuse):
            k = qh * (HU + 1) + i
            c_, qt = divmod(i, 4)
            if reuse or k >= 2:
                s_mr.wait(pe, n if k >= 2 else add(n, -1), k - 1 if k >= 2 else 2 * HU + 2 + k - 1)
            if i == 0 and qh == 0:
                s_ld.wait(pe, n)
            slot = k % 2
            for j in range(2):
                mm = pe.matmul(p_max[:, slot, j * 512:(j + 1) * 512], QA[0:NPROD, p, qh, c_, qt * P:(qt + 1) * P],
                               KA[0:NPROD, p, c_, j * 512:(j + 1) * 512], start=True, stop=True)
            mm.then_inc(s_mx.sem, 1)
            s_mx.wait(dve, n, k + 1)
            dve.tensor_reduce(negmax[:, qh, c_, qt:qt + 1], p_max[:, slot, :], axis=AX.X, op=ALU.max,
                              negate=True).then_inc(s_mr.sem, 1)

        def max_rows(n, p, qh, reuse):
            k = qh * (HU + 1) + HU
            slot = k % 2
            s_mr.wait(pe, n, k)
            pe.transpose(p_max[0:GH * 4, slot, 0:P], negmax[:, qh, :, :].rearrange("p c q -> p (c q)"),
                         ident[:, :]).then_inc(s_mx.sem, 1)
            s_mx.wait(dve, n, k + 1)
            dve.tensor_copy(nm[:, qh, :], p_max[0:GH * 4, slot, 0:P]).then_inc(s_mr.sem, 1)
            s_mr.wait(dve, n, k + 1)
            if reuse:
                s_md.wait(dve, add(n, -1), 32 * (qh + 1))
            dve.tensor_copy(nmb[:, qh, 0, :], nm[:, qh, :]).then_inc(s_mb.sem, 1)
            s_mb.wait(dve, n, 2 * qh + 1)
            dve.tensor_tensor(out=nmb[:, qh, 1, :], in0=nm[:, qh, :], in1=nmb[:, qh, 0, :],
                              op=ALU.subtract).then_inc(s_mb.sem, 1)
            s_mb.wait(sp, n, 2 * qh + 2)
            for j in range(2):
                sp.dma_start(QA[MROW + j:MROW + j + 1, p, qh, :, :],
                             nmb[:, qh, j, :]).then_inc(s_md.sem, 16)

        def score(n, p, s, c_, reuse):
            qh, kb = divmod(s, 8)
            i = 4 * s + c_
            if i >= 2:
                s_ex.wait(pe, n, i - 1)
            elif reuse:
                s_ex.wait(pe, add(n, -1), 64 + i - 1)
            if kb == 0 and c_ == 0:
                s_md.wait(pe, n, 32 * (qh + 1))
            pe.matmul(p_s[:, i % 2, :], KA[:, p, c_, kb * P:(kb + 1) * P], QA[:, p, qh, c_, :],
                      start=True, stop=True).then_inc(s_st.sem, 1)
            s_st.wait(act, n, i + 1)
            if c_ == 0 and (s >= 4 or reuse):
                s_pv.wait(act, n if s >= 4 else add(n, -1), s - 3 if s >= 4 else s + 13)
            act.activation(E[:, s % 4, c_, :], p_s[:, i % 2, :], ACT.Exp, scale=DH ** -0.5)\
                .then_inc(s_ex.sem, 1)

        def weigh(n, p, s, reuse):
            qh, kb = divmod(s, 8)
            s_ex.wait(pe, n, 4 * s + 4)
            if s == 0:
                s_vg.wait(pe, n)
            if kb == 0 and reuse:
                s_ao.wait(pe, add(n, -1), qh + 1)
            for c_ in range(GH):
                mm = pe.matmul(p_o[c_ * VW:(c_ + 1) * VW, qh, :], VG[:, p, kb, c_, :], E[:, s % 4, c_, :],
                               start=(kb == 0), stop=(kb == 7), skip_group_check=True)
            mm.then_inc(s_pv.sem, 1)

        def result(n, b, hg, qh, reuse):
            s_pv.wait(dve, n, 8 * (qh + 1))
            if reuse:
                s_ot.wait(dve, add(n, -1), qh + 1)
            dve.tensor_copy(OE[:, qh, :], p_o[:, qh, :]).then_inc(s_oe.sem, 1)
            s_oe.wait(pe, n, qh + 1)
            for qt in range(4):
                mm = pe.transpose(p_o[:, qh, qt * P:(qt + 1) * P], OE[:, qh, qt * P:(qt + 1) * P], ident[:, :])
            mm.then_inc(s_ot.sem, 1)
            s_ot.wait(dve, n, qh + 1)
            o = p_o[:, qh, :].rearrange("p (q c w) -> p q c w", q=4, w=VW)
            dve.reciprocal(rsum[:, qh, :, :], o[:, :, :, DH]).then_inc(s_rc.sem, 1)
            s_rc.wait(dve, n, qh + 1)
            a = AO[:, b, 4 * qh:4 * qh + 4, :].rearrange("p q (g c d) -> p q g c d", g=H // GH, d=DH)
            a = a[:, :, hg, :, :]
            dve.tensor_tensor(out=a, in0=o[:, :, :, 0:DH],
                              in1=rsum[:, qh, :, :].unsqueeze(3).broadcast_to([P, 4, GH, DH]),
                              op=ALU.mult).then_inc(s_ao.sem, 1)

        def group(n, p, at, nxt, prev, reuse):
            for s in range(16):
                if s == 0 and nxt:
                    load(add(n, 1), *nxt, 1 - p, reuse)
                    values(add(n, 1), *nxt, 1 - p, reuse)
                score(n, p, s, 0, reuse)
                score(n, p, s, 1, reuse)
                if s > 0:
                    weigh(n, p, s - 1, reuse)
                elif prev:
                    weigh(add(n, -1), 1 - p, 15, True)
                if s == 2 and prev:
                    result(add(n, -1), *prev, 1, True)
                if s == 10:
                    result(n, *at, 0, reuse)
                score(n, p, s, 2, reuse)
                units = []
                if s < 6:
                    lo, hi = HU * s // 6, HU * (s + 1) // 6
                    units = [(n, p, 1, i, reuse or True) for i in range(lo, hi)]
                elif s < 14 and nxt:
                    units = [(add(n, 1), 1 - p, 0, i, True) for i in range(2 * (s - 6), 2 * (s - 6) + 2)]
                for u in units[:1]:
                    max_unit(*u)
                score(n, p, s, 3, reuse)
                for u in units[1:]:
                    max_unit(*u)
                if s == 5:
                    max_rows(n, p, 1, reuse)
                if s == 13 and nxt:
                    max_rows(add(n, 1), 1 - p, 0, True)

        load(0, 0, 0, 0, False)
        values(0, 0, 0, 0, False)
        for i in range(HU):
            max_unit(0, 0, 0, i, False)
        max_rows(0, 0, 0, False)
        HG = H // GH
        where = [(g // HG, g % HG) for g in range(NG)]
        group(0, 0, where[0], where[1], None, False)
        group(1, 1, where[1], where[2], where[0], True)
        with nc.Fori(1, NG // 2 - 1) as it:
            b0, hp = it // 2, it % 2
            g0 = (it * 2, 0)
            nb, nh = (it + 1) // 2, (it + 1) % 2
            pb, ph = (it - 1) // 2, (it - 1) % 2
            group(g0, 0, (b0, hp * 2), (b0, hp * 2 + 1), (pb, ph * 2 + 1), True)
            group((it * 2, 1), 1, (b0, hp * 2 + 1), (nb, nh * 2), (b0, hp * 2), True)
        group(NG - 2, 0, where[-2], where[-1], where[-3], True)
        group(NG - 1, 1, where[-1], None, where[-2], True)
        weigh(NG - 1, 1, 15, True)
        result(NG - 1, *where[-1], 1, True)
        nc.all_engine_barrier()

    with ExitStack() as c:
        ao = sb(c, "ao", [P, B, D])
        aoT = sb(c, "aoT", [P, B, P])
        gated = sb(c, "gated", [P, B, D])
        stats = sb(c, "stats2", [P, B, 6])
        mv = sb(c, "mv2", [P, B, 2])
        power = sb(c, "power2", [P, B])
        rstd = sb(c, "rstd2", [P, B])
        p_t = ps(c, "p_t2", [P, B, P])
        p_w = ps(c, "p_w2", [P, B, D])
        s_pw = count(c, "s_pw2")
        s_c = count(c, "s_c")
        s_t = count(c, "s_t2")
        s_tc = count(c, "s_tc")
        s_w = count(c, "s_w2")
        s_d = count(c, "s_d", 8)
        s_r = count(c, "s_r2")
        s_xm = count(c, "s_xm", 16)
        pool.memset(power[:, :], -0.5).then_inc(s_pw.sem, 1)
        pool.wait_ge(s_pw.sem, 1)
        with nc.Fori(0, NT) as t:
            n = (t, 0)
            dve.tensor_scalar_mul(ao[:, :, :], AO[:, :, t, :], 1.0).then_inc(s_c.sem, 1)
            s_c.wait(pe, n)
            for b in range(B):
                mm = pe.transpose(p_t[:, b, :], ao[:, b, :], ident[:, :])
            mm.then_inc(s_t.sem, 1)
            s_t.wait(act, n)
            act.activation(aoT[:, :, :], p_t[:, :, :], ACT.Copy).then_inc(s_tc.sem, 1)
            s_tc.wait(pe, n)
            for b in range(B):
                pe.matmul(p_w[:, b, :], aoT[:, b, :], woT[:, :], start=True, stop=False)
                mm = pe.matmul(p_w[:, b, :], ones[0:1, :], rows[:, 1, :], start=False, stop=True)
            mm.then_inc(s_w.sem, 1)
            s_w.wait(dve, n)
            dve.tensor_tensor(out=gated[:, :, :], in0=p_w[:, :, :], in1=mod[:, 2, :, :], op=ALU.mult)\
                .then_inc(s_d.sem, 1)
            s_d.wait(dve, n, 1)
            dve.tensor_tensor(out=gated[:, :, :], in0=gated[:, :, :], in1=X[:, :, t, :], op=ALU.add)\
                .then_inc(s_d.sem, 1)
            s_d.wait(dve, n, 2)
            sp.wait_ge(s_d.sem, s_d.at(n, 2))
            sp.dma_start(x_mid[:, :, t, :], gated[:, :, :]).then_inc(s_xm.sem, 16)
            for b in range(B):
                i = dve.bn_stats(stats[:, b, :], gated[:, b, :])
            i.then_inc(s_d.sem, 1)
            s_d.wait(dve, n, 3)
            dve.memset(spare[:, :], 0.0)
            for b in range(B):
                i = dve.bn_aggr(mv[:, b, :], stats[:, b, :])
            i.then_inc(s_d.sem, 1)
            s_d.wait(dve, n, 4)
            dve.tensor_scalar_add(mv[:, :, 1:2], mv[:, :, 1:2], LN_EPS).then_inc(s_d.sem, 1)
            s_d.wait(pool, n, 5)
            pool.tensor_tensor(out=rstd[:, :], in0=mv[:, :, 1], in1=power[:, :], op=ALU.pow)\
                .then_inc(s_r.sem, 1)
            s_r.wait(dve, n)
            for b in range(B):
                i = dve.tensor_scalar(X[:, b, t, :], gated[:, b, :], mv[:, b, 0:1], rstd[:, b:b + 1],
                                      ALU.subtract, ALU.mult)
            i.then_inc(s_d.sem, 1)
            s_d.wait(dve, n, 6)
            dve.tensor_tensor(out=X[:, :, t, :], in0=X[:, :, t, :], in1=mod[:, 4, :, :], op=ALU.mult)\
                .then_inc(s_d.sem, 1)
            s_d.wait(dve, n, 7)
            s_xm.wait(dve, n)
            dve.tensor_tensor(out=X[:, :, t, :], in0=X[:, :, t, :], in1=mod[:, 3, :, :], op=ALU.add)\
                .then_inc(s_d.sem, 1)
            s_d.wait(dve, n, 8)
        nc.all_engine_barrier()
    first.close()

    layers(nc, ins, X, ident, ident_b, ones, spare, sb, ps, count)

    with ExitStack() as c:
        XM = sb(c, "XM", [P, B, NT, D])
        s_l = count(c, "s_l", 16)
        s_f = count(c, "s_f", 2)
        s_out = count(c, "s_out", 16)
        for b in range(B):
            sp.dma_start(XM[:, b, :, :], x_mid[:, b, :, :]).then_inc(s_l.sem, 16)
        for b in range(B):
            dve.tensor_tensor(out=X[:, b, :, :], in0=X[:, b, :, :],
                              in1=gate_b[:, b, :].unsqueeze(1).broadcast_to([P, NT, D]),
                              op=ALU.mult).then_inc(s_f.sem, 1)
            dve.wait_ge(s_f.sem, 2 * b + 1)
            dve.wait_ge(s_l.sem, 16 * B)
            dve.tensor_tensor(out=X[:, b, :, :], in0=X[:, b, :, :], in1=XM[:, b, :, :],
                              op=ALU.add).then_inc(s_f.sem, 1)
            s_f.wait(sp, b)
            sp.dma_start(out_dram[:, b, :, :], X[:, b, :, :]).then_inc(s_out.sem, 16)
        sp.wait_ge(s_out.sem, 16 * B)
    whole.close()


def layers(nc, ins, X, ident, ident_b, ones, spare, sb, ps, count):
    pe, act, dve, pool, sp = nc.tensor, nc.scalar, nc.vector, nc.gpsimd, nc.sync
    c = ExitStack()
    Wqkv = sb(c, "Wqkv", [P, 2, 3 * INNER])
    Wo = sb(c, "Wo", [P, 2, LH // 2, D])
    qks = sb(c, "qks", [P, 2, 2, 2, LD])
    W1 = sb(c, "W1", [P, 2 * FF])
    W2 = sb(c, "W2", [P, len(CH), D])
    b1 = sb(c, "b1", [P, 2, len(CH)])
    b2 = sb(c, "b2", [1, D])
    ln = sb(c, "ln", [P, 2])
    rope = sb(c, "rope", [P, NT, 2, 2, LD])
    tab = sb(c, "tab", [P, 2, 2, LD])
    mask = sb(c, "mask", [P, NT, 4 * KB], BF16)
    power = sb(c, "power3", [P, 2 * LH])
    begun = sb(c, "begun", [P, NT])
    xin = sb(c, "xin", [P, B, D])
    XS = sb(c, "XS", [P, B, WIN + P + 1])
    QK = sb(c, "QK", [P, 2 * INNER])
    SQ = sb(c, "SQ", [P, 2 * INNER])
    T1 = sb(c, "T1", [P, 2, 2 * INNER])
    T2 = sb(c, "T2", [P, 2 * INNER])
    ss = sb(c, "ss", [P, 2, 2 * LH])
    rn = sb(c, "rn", [P, 2, 2 * LH])
    qT = sb(c, "qT", [P, 2, LH // 2, P])
    kT = sb(c, "kT", [P, B, LH // 2, WIN + P])
    E = sb(c, "Ew", [P, 2, LH, KB])
    mx = sb(c, "mx", [P, 2, LH])
    sm = sb(c, "sm", [P, 2, 2, LH])
    V = sb(c, "V", [KB, 2, INNER])
    ET = sb(c, "ET", [KB, LH, P])
    OT = sb(c, "OT", [P, LH // 2, P])
    x1 = sb(c, "x1", [P, B, D])
    FS = sb(c, "FS", [P, B, P + 1])
    fx = sb(c, "fx", [P, B, D])
    fst = sb(c, "fst", [P, B, 6])
    fmv = sb(c, "fmv", [P, B, 2])
    frs = sb(c, "frs", [P, B])
    fn = sb(c, "fn", [P, B, D])
    fnT = sb(c, "fnT", [P, B * P])
    G = sb(c, "G", [P, 2, B * P])
    HH = sb(c, "HH", [P, len(CH), B * P])
    NR = 4
    R = ps(c, "R", [P, NR, 512])
    PS = ps(c, "PS", [P, 4, 512])

    names = dict(xi=1, tab=1, xT=1, hal=1, xs=2, qk=4, qke=4, sq=1, t1=1, t2=1, ss=2, pw=1, ad=1, no=1,
                 tq=4, kh=1, te=4, s=2, mx=2, sub=2, ex=2, sum=1, rc=1, pn=1, vp=4, ve=4, pt=4, pe=4,
                 pv=2, oe=2, wo=1, x1=2, f1=1, fc=1, f1e=2, f2=1, f2e=1, fst=3, frs=1, fn=1, f3=1, f3e=1,
                 ff=6, g=3, hh=3, f5=1, fx=1)
    s = {k: count(c, "l_" + k, per) for k, per in names.items()}
    s_wa = count(c, "l_wa", 16 * 7)
    s_wf = count(c, "l_wf", 16 * 9)
    s_c = count(c, "l_c", 16 * 2)
    s_one = count(c, "l_one")

    def load_attention(l, par):
        hf = LD // 2
        for dst, src in (
            (Wqkv[:, par, :], ins["Wqkv"][l]),
            (qks[:, par, 0, 0, :], ins["q_scale"][l].partition_broadcast(P)),
            (qks[:, par, 0, 1, :], ins["k_scale"][l].partition_broadcast(P)),
            (qks[:, par, 1, :, 0:hf], ins["qk_scale"][l, :, hf:LD].partition_broadcast(P)),
            (qks[:, par, 1, :, hf:LD], ins["qk_scale"][l, :, 0:hf].partition_broadcast(P)),
            (Wo[:, par, 0:4, :], ins["Wo"][l, 0:4 * P].rearrange("(a p) n -> p a n", p=P)),
            (Wo[:, par, 4:8, :], ins["Wo"][l, 4 * P:8 * P].rearrange("(a p) n -> p a n", p=P)),
        ):
            sp.dma_start(dst, src).then_inc(s_wa.sem, 16)

    def load_ff(l):
        for dst, src in (
            (W1[:, :], ins["W1"][l]),
            (W2[:, 0:2, :], ins["W2"][l, 0:2 * P].rearrange("(a p) n -> p a n", p=P)),
            (W2[0:FF - 2 * P, 2, :], ins["W2"][l, 2 * P:FF]),
            *((b1[0:w, :, i], ins["b1"][l].rearrange("(i f) -> f i", i=2)[lo:lo + w]) for i, (lo, w) in enumerate(CH)),
            (b2[:, :], ins["b2"][l].unsqueeze(0)),
            (ln[:, 0:1], ins["ln_g"][l].unsqueeze(1)),
            (ln[:, 1:2], ins["ln_b"][l].unsqueeze(1)),
        ):
            with nc.allow_non_contiguous_dma("small columns"):
                sp.dma_start(dst, src).then_inc(s_wf.sem, 16)

    class At:

        def __init__(self, u, first=False):
            self.u, self.first = u, first
            self.tile = u * B
            self.t, self.t_prev, self.t_next = u % NT, (u + NT - 1) % NT, (u + 1) % NT
            self.layer, self.par = u // NT, u // NT % 2
            self.par_prev = ((u + NT - 1) // NT + 1) % 2

        def time(self, d):
            return self.t if d >= 0 else self.t_prev

        def parity(self, d):
            return self.par if d >= 0 else self.par_prev

    waited = {}

    def wait_once(e, name, base, d, k):
        k = s[name].per if k is None else k
        if waited.get((e.engine, name), (-99, 0)) >= (d, k):
            return
        waited[e.engine, name] = (d, k)
        s[name].wait(e, (base, d), k)

    def wait(e, name, at, d, k=None):
        if not (at.first and d < 0):
            wait_once(e, name, at.tile, d, k)

    def waitf(e, name, at, k=None, d=-1):
        wait_once(e, name, at.u, d, k)

    def inc(i, name, n=1):
        return i.then_inc(s[name].sem, n)

    class Ring:

        def __init__(self):
            self.n, self.last = 0, [None] * NR

        def take(self, at):
            r = self.n % NR
            self.n += 1
            if self.last[r]:
                kind, name, d, k = self.last[r]
                if kind == "tile":
                    wait(pe, name, at, d, k)
                else:
                    waitf(pe, name, at, k, d)
            self.last[r] = None
            return r

        def read(self, r, name, d, k, kind="tile"):
            self.last[r] = (kind, name, d, k)

        def next_step(self):
            self.last = [x and (x[0], x[1], x[2] - (B if x[0] == "tile" else 1), x[3]) for x in self.last]

    ring = Ring()
    hc = D // 2

    def read_input(at, t, prev):
        if prev is not None:
            wait(dve, "xT", at, prev)
        inc(dve.tensor_scalar_mul(xin[:, :, :], X[:, :, t, :], 1.0), "xi")

    def step_start(at):
        s_wa.wait(pe, (at.layer, 0))
        s_wa.wait(dve, (at.layer, 0))
        wait(dve, "t2", at, -1)
        inc(dve.tensor_tensor(out=tab[:, :, :, :], in0=rope[:, at.t, :, :, :], in1=qks[:, at.par, :, :, :],
                              op=ALU.mult), "tab")

    def input_T(at, d):
        b = d % B
        r = ring.take(at)
        waitf(pe, "xi", at, d=0)
        inc(pe.transpose(R[:, r, 0:P], xin[:, b, :], ident[:, :]), "xT")
        wait(dve, "vp", at, d - B)
        inc(dve.tensor_scalar(XS[:, b, 0:WIN + 1], XS[:, b, P:P + WIN + 1], begun[:, bass.ds(at.t, 1)], None,
                              ALU.mult), "hal")
        wait(act, "hal", at, d)
        wait(act, "xT", at, d)
        inc(act.activation(XS[0:hc, b, WIN:WIN + P], R[0:hc, r, 0:P], ACT.Copy), "xs")
        inc(act.activation(XS[hc:D, b, WIN + 1:WIN + 1 + P], R[hc:D, r, 0:P], ACT.Copy), "xs")
        ring.read(r, "xs", d, 2)

    def project_qk(at, d, js):
        b = d % B
        wait(pe, "xs", at, d)
        for j in js:
            r = ring.take(at)
            inc(pe.matmul(R[:, r, :], XS[:, b, WIN:WIN + P], Wqkv[:, at.par, j * 512:(j + 1) * 512],
                          start=True, stop=True), "qk")
            wait(act, "qk", at, d, j + 1)
            if j == 0:
                wait(act, "t2", at, d - 1)
            inc(act.activation(QK[:, j * 512:(j + 1) * 512], R[:, r, :], ACT.Copy), "qke")
            ring.read(r, "qke", d, j + 1)

    def view_qk(a):
        return a.rearrange("p (i h e) -> p i h e", i=2, e=LD)

    def square(at, d):
        wait(act, "qke", at, d)
        wait(act, "ss", at, d - 1, 1)
        inc(act.activation(SQ[:, :], QK[:, :], ACT.Square), "sq")

    def rotate_cos(at, d):
        wait(dve, "qke", at, d)
        wait(dve, "tq", at, d - 2)
        waitf(dve, "tab", at, d=0)
        inc(dve.tensor_tensor(out=view_qk(T1[:, d % 2, :]), in0=view_qk(QK[:, :]),
                              in1=tab[:, 0].unsqueeze(2).broadcast_to([P, 2, LH, LD]), op=ALU.mult), "t1")

    def rotate_sin(at, d):
        p, hf = d % 2, LD // 2
        q, t2 = view_qk(QK[:, :]), view_qk(T2[:, :])
        wait(dve, "ad", at, d - 1)
        for j in range(2):
            i = dve.tensor_tensor(out=t2[:, :, :, j * hf:(j + 1) * hf], in0=q[:, :, :, (1 - j) * hf:(2 - j) * hf],
                                  in1=tab[:, 1, :, j * hf:(j + 1) * hf].unsqueeze(2).broadcast_to([P, 2, LH, hf]),
                                  op=ALU.mult)
        inc(i, "t2")
        wait(pool, "t2", at, d)
        inc(pool.tensor_tensor(out=T1[:, p, :], in0=T1[:, p, :], in1=T2[:, :], op=ALU.add), "ad")

    def norms(at, d):
        p = d % 2
        wait(dve, "sq", at, d)
        inc(dve.reduce_sum(ss[:, p, :], SQ[:, :].rearrange("p (h e) -> p h e", e=LD), axis=AX.X), "ss")
        wait(dve, "ss", at, d, 1)
        inc(dve.tensor_scalar_max(ss[:, p, :], ss[:, p, :], 1e-24), "ss")
        wait(pool, "ss", at, d, 2)
        inc(pool.tensor_tensor(out=rn[:, p, :], in0=ss[:, p, :], in1=power[:, :], op=ALU.pow), "pw")

    def normalise(at, d):
        p = d % 2
        wait(dve, "ad", at, d)
        wait(dve, "pw", at, d)
        t1 = T1[:, p, :].rearrange("p (h e) -> p h e", e=LD)
        inc(dve.tensor_tensor(out=t1, in0=t1, in1=rn[:, p, :].unsqueeze(2).broadcast_to([P, 2 * LH, LD]),
                              op=ALU.mult), "no")

    def halo_k(at, d):
        b = d % B
        wait(dve, "s", at, d - 1)
        inc(dve.tensor_scalar(kT[:, b, :, 0:WIN], kT[:, b, :, P:P + WIN], begun[:, bass.ds(at.time(d), 1)], None,
                              ALU.mult), "kh")

    def transpose_qk(at, d):
        b, p = d % B, d % 2
        wait(pe, "no", at, d)
        for j in range(4):
            r = ring.take(at)
            for i in range(4):
                mm = pe.transpose(R[:, r, i * P:(i + 1) * P], T1[:, p, (4 * j + i) * P:(4 * j + i + 1) * P], ident[:, :])
            inc(mm, "tq")
            wait(act, "tq", at, d, j + 1)
            src = R[:, r, :].rearrange("p (i n) -> p i n", i=4)
            if j < 2:
                inc(act.activation(qT[:, p, 4 * j:4 * j + 4, :], src, ACT.Copy), "te")
            else:
                wait(act, "kh", at, d)
                inc(act.activation(kT[:, b, 4 * j - 8:4 * j - 4, WIN:WIN + P], src, ACT.Copy), "te")
            ring.read(r, "te", d, j + 1)

    def scores(at, d, hf):
        b, p = d % B, d % 2
        wait(pe, "te", at, d)
        wait(pe, "kh", at, d)
        wait(pe, "sub", at, d - 1, hf + 1)
        for par in range(2):
            bank, o = 2 * hf + par, par * LD
            pe.matmul(PS[:, bank, 0:4 * KB], ident_b[:, :], mask[:, at.time(d), :], start=True, stop=False,
                      skip_group_check=True)
            for g in range(2):
                for j in range(4):
                    pair = 4 * hf + j
                    mm = pe.matmul(PS[g * QB:(g + 1) * QB, bank, j * KB:(j + 1) * KB],
                                   qT[o:o + LD, p, pair, g * QB:(g + 1) * QB],
                                   kT[o:o + LD, b, pair, g * QB:g * QB + KB],
                                   start=False, stop=True, skip_group_check=True)
        inc(mm, "s")
        view = PS[:, 2 * hf:2 * hf + 2, 0:4 * KB].rearrange("p a (j k) -> p a j k", k=KB)
        m = mx[:, p, 8 * hf:8 * hf + 8].rearrange("p (a j) -> p a j", a=2)
        e = E[:, p, 8 * hf:8 * hf + 8, :].rearrange("p (a j) k -> p a j k", a=2)
        wait(dve, "s", at, d, hf + 1)
        inc(dve.reduce_max(m, view, axis=AX.X), "mx")
        wait(dve, "mx", at, d, hf + 1)
        if hf == 0:
            wait(dve, "pt", at, d - 2)
        inc(dve.tensor_tensor(out=e, in0=view, in1=m.unsqueeze(3).broadcast_to([P, 2, 4, KB]),
                              op=ALU.subtract), "sub")

    def exponentials(at, d, hf):
        wait(act, "sub", at, d, hf + 1)
        e = E[:, d % 2, 8 * hf:8 * hf + 8, :]
        inc(act.activation(e, e, ACT.Exp), "ex")

    def divide(at, d):
        p = d % 2
        wait(dve, "ex", at, d)
        inc(dve.reduce_sum(sm[:, p, 0, :], E[:, p, :, :], axis=AX.X), "sum")
        wait(dve, "sum", at, d)
        wait(dve, "pn", at, d - 2)
        inc(dve.reciprocal(sm[:, p, 1, :], sm[:, p, 0, :]), "rc")
        wait(pool, "rc", at, d)
        inc(pool.tensor_tensor(out=E[:, p, :, :], in0=E[:, p, :, :],
                               in1=sm[:, p, 1, :].unsqueeze(2).broadcast_to([P, LH, KB]), op=ALU.mult), "pn")

    def project_v(at, d):
        b = d % B
        for j in range(4):
            g, half = divmod(j, 2)
            r = ring.take(at)
            inc(pe.matmul(R[0:KB, r, :], XS[:, b, g * QB:g * QB + KB],
                          Wqkv[:, at.parity(d), 2 * INNER + half * 512:2 * INNER + (half + 1) * 512],
                          start=True, stop=True), "vp")
            wait(act, "vp", at, d, j + 1)
            inc(act.activation(V[:, g, half * 512:(half + 1) * 512], R[0:KB, r, :], ACT.Copy), "ve")
            ring.read(r, "ve", d, j + 1)

    def transpose_e(at, d):
        p = d % 2
        wait(pe, "pn", at, d)
        for j in range(4):
            r = ring.take(at)
            for i in range(4):
                mm = pe.transpose(R[0:KB, r, i * P:(i + 1) * P], E[:, p, 4 * j + i, :], ident[:, :])
            inc(mm, "pt")
            wait(act, "pt", at, d, j + 1)
            inc(act.activation(ET[:, 4 * j:4 * j + 4, :], R[0:KB, r, :].rearrange("p (i n) -> p i n", i=4),
                               ACT.Copy), "pe")
            ring.read(r, "pe", d, j + 1)

    def attend(at, d):
        b = d % B
        wait(pe, "ve", at, d)
        for hf in range(2):
            wait(pe, "pe", at, d, 2 * hf + 2)
            r = ring.take(at)
            for j in range(4):
                pair = 4 * hf + j
                for g in range(2):
                    for par in range(2):
                        mm = pe.matmul(R[par * LD:(par + 1) * LD, r, j * P + g * QB:j * P + (g + 1) * QB],
                                       V[:, g, (2 * pair + par) * LD:(2 * pair + par + 1) * LD],
                                       ET[:, 8 * hf + 4 * par + j, g * QB:(g + 1) * QB], start=True, stop=True,
                                       skip_group_check=True)
            inc(mm, "pv")
            wait(act, "pv", at, d, hf + 1)
            inc(act.activation(OT[:, 4 * hf:4 * hf + 4, :], R[:, r, :].rearrange("p (j n) -> p j n", j=4),
                               ACT.Copy), "oe")
            ring.read(r, "oe", d, hf + 1)
        r = ring.take(at)
        for pair in range(LH // 2):
            wait(pe, "oe", at, d, pair // 4 + 1)
            mm = pe.matmul(R[:, r, 0:D], OT[:, pair, :], Wo[:, at.parity(d), pair, :], start=(pair == 0),
                           stop=(pair == LH // 2 - 1))
        inc(mm, "wo")
        wait(dve, "wo", at, d)
        t = at.time(d)
        inc(dve.tensor_tensor(out=x1[:, b, :], in0=R[:, r, 0:D], in1=X[:, b, t, :], op=ALU.add), "x1")
        ring.read(r, "x1", d, 1)
        wait(dve, "x1", at, d, 1)
        inc(dve.tensor_scalar_mul(X[:, b, t, :], x1[:, b, :], 1.0), "x1")

    def ff_shift(at):
        r = ring.take(at)
        wait(pe, "x1", at, -1, 2)
        for b in range(B):
            mm = pe.transpose(R[:, r, b * P:(b + 1) * P], x1[:, b, :], ident[:, :])
        inc(mm, "f1")
        waitf(dve, "f1", at)
        inc(dve.tensor_scalar(FS[hc:D, :, 0:1], FS[hc:D, :, P:P + 1], begun[hc:D, bass.ds(at.t_prev, 1)], None,
                              ALU.mult), "fc")
        waitf(act, "fc", at)
        waitf(act, "f1", at)
        src = R[:, r, :].rearrange("p (b n) -> p b n", b=B)
        inc(act.activation(FS[0:hc, :, 0:P], src[0:hc], ACT.Copy), "f1e")
        inc(act.activation(FS[hc:D, :, 1:P + 1], src[hc:D], ACT.Copy), "f1e")
        ring.read(r, "f1e", -1, 2, "step")

    def ff_stats(at):
        waitf(pe, "f1e", at)
        waitf(pe, "fc", at)
        r = ring.take(at)
        for b in range(B):
            mm = pe.transpose(R[:, r, b * P:(b + 1) * P], FS[:, b, 0:P], ident[:, :])
        inc(mm, "f2")
        waitf(dve, "f2", at)
        inc(dve.tensor_copy(fx[:, :, :], R[:, r, :].rearrange("p (b n) -> p b n", b=B)), "f2e")
        ring.read(r, "f2e", -1, 1, "step")
        waitf(dve, "f2e", at)
        for b in range(B):
            i = dve.bn_stats(fst[:, b, :], fx[:, b, :])
        inc(i, "fst")
        waitf(dve, "fst", at, 1)
        dve.memset(spare[:, :], 0.0)
        for b in range(B):
            i = dve.bn_aggr(fmv[:, b, :], fst[:, b, :])
        inc(i, "fst")
        waitf(dve, "fst", at, 2)
        inc(dve.tensor_scalar_add(fmv[:, :, 1:2], fmv[:, :, 1:2], LN_EPS), "fst")
        waitf(pool, "fst", at, 3)
        inc(pool.tensor_tensor(out=frs[:, :], in0=fmv[:, :, 1], in1=power[:, 0:B], op=ALU.pow), "frs")

    def ff_norm(at):
        waitf(dve, "frs", at)
        for b in range(B):
            i = dve.tensor_scalar(fn[:, b, :], fx[:, b, :], fmv[:, b, 0:1], frs[:, b:b + 1],
                                  ALU.subtract, ALU.mult)
        inc(i, "fn")
        waitf(pe, "fn", at)
        r = ring.take(at)
        for b in range(B):
            mm = pe.transpose(R[:, r, b * P:(b + 1) * P], fn[:, b, :], ident[:, :])
        inc(mm, "f3")
        waitf(act, "f3", at)
        inc(act.activation(fnT[:, :], R[:, r, :], ACT.Identity, bias=ln[:, 1:2], scale=ln[:, 0:1]), "f3e")
        ring.read(r, "f3e", -1, 1, "step")

    def ff_up(at):
        waitf(pe, "f3e", at)
        for i, (lo, w) in enumerate(CH):
            rg = ring.take(at)
            inc(pe.matmul(R[0:w, rg, :], W1[:, FF + lo:FF + lo + w], fnT[:, :], start=True, stop=True), "ff")
            ra = ring.take(at)
            inc(pe.matmul(R[0:w, ra, :], W1[:, lo:lo + w], fnT[:, :], start=True, stop=True), "ff")
            waitf(act, "ff", at, 2 * i + 1)
            if i > 1:
                waitf(act, "hh", at, i - 1)
            inc(act.activation(G[0:w, i % 2, :], R[0:w, rg, :], ACT.Gelu, bias=b1[0:w, 1, i:i + 1]), "g")
            ring.read(rg, "g", -1, i + 1, "step")
            waitf(dve, "ff", at, 2 * i + 2)
            waitf(dve, "g", at, i + 1)
            inc(dve.scalar_tensor_tensor(HH[0:w, i, :], R[0:w, ra, :], b1[0:w, 0, i:i + 1], G[0:w, i % 2, :],
                                         ALU.add, ALU.mult), "hh")
            ring.read(ra, "hh", -1, i + 1, "step")

    def ff_down(at):
        waitf(pe, "hh", at)
        r = ring.take(at)
        for b in range(B):
            for i, (lo, w) in enumerate(CH):
                pe.matmul(R[:, r, b * P:(b + 1) * P], HH[0:w, i, b * P:(b + 1) * P], W2[0:w, i, :],
                          start=(i == 0), stop=False)
            mm = pe.matmul(R[:, r, b * P:(b + 1) * P], ones[0:1, :], b2[:, :], start=False, stop=True)
        inc(mm, "f5")
        waitf(dve, "f5", at)
        xt = X[:, :, at.t_prev, :]
        inc(dve.tensor_tensor(out=xt, in0=xt, in1=R[:, r, :].rearrange("p (b n) -> p b n", b=B),
                              op=ALU.add), "fx")
        ring.read(r, "fx", -1, 1, "step")
        ring.n += 2

    def step(at, new=True, slots=B, ff=True):
        waited.clear()
        if new:
            step_start(at)
        for d in range(slots):
            mid = (d >= 2 or not at.first) and (new or d < 2)
            old = (d >= 3 or not at.first) and (new or d < 3)
            f = ff and d == 3

            def feed_forward(part, banks=1):
                if f:
                    part(at)
                elif d == 3:
                    ring.n += banks

            if new:
                input_T(at, d)
                if d == B - 1:
                    read_input(at, at.t_next, d)
            else:
                ring.n += 1
            if mid:
                halo_k(at, d - 2)
                transpose_qk(at, d - 2)
            else:
                ring.n += 4
            if f:
                if isinstance(at.u, int):
                    s_wf.wait(pe, (at.u - 1) // NT)
                    s_wf.wait(act, (at.u - 1) // NT)
                    s_wf.wait(dve, (at.u - 1) // NT)
                else:
                    for e in (pe, act, dve):
                        s_wf.wait(e, ((at.u + (NT - 1)) // NT, -1))
            feed_forward(ff_shift)
            if old:
                project_v(at, d - 3)
            else:
                ring.n += 4
            feed_forward(ff_stats)
            if mid:
                scores(at, d - 2, 0)
                scores(at, d - 2, 1)
                exponentials(at, d - 2, 0)
                exponentials(at, d - 2, 1)
            feed_forward(ff_norm)
            if new and (d > 0 or not at.first) or not new and d == 0:
                normalise(at, d - 1)
            if mid:
                divide(at, d - 2)
            if new:
                project_qk(at, d, (0, 1, 2, 3))
                square(at, d)
                rotate_cos(at, d)
            else:
                ring.n += 4
            feed_forward(ff_up, 6)
            if new:
                rotate_sin(at, d)
                norms(at, d)
            if old:
                transpose_e(at, d - 3)
            else:
                ring.n += 4
            feed_forward(ff_down, 3)
            if old:
                attend(at, d - 3)
            else:
                ring.n += 3
        ring.next_step()

    sp.dma_start(rope[:, :, :, :, :], ins["rope"]).then_inc(s_c.sem, 16)
    sp.dma_start(mask[:, :, :], ins["mask"]).then_inc(s_c.sem, 16)
    load_attention(0, 0)
    load_ff(0)
    s_wa.wait(sp, 0)
    load_attention(1, 1)
    pool.memset(power[:, :], -0.5).then_inc(s_one.sem, 1)
    pool.memset(XS[:, :, :], 0.0).then_inc(s_one.sem, 1)
    pool.memset(kT[:, :, :, P:P + WIN], 0.0).then_inc(s_one.sem, 1)
    pool.memset(FS[:, :, :], 0.0).then_inc(s_one.sem, 1)
    pool.memset(begun[:, 0:1], 0.0).then_inc(s_one.sem, 1)
    pool.memset(begun[:, 1:NT], 1.0).then_inc(s_one.sem, 1)
    for e in (pool, dve, act, pe):
        e.wait_ge(s_one.sem, 6)
    for e in (pe, dve):
        s_c.wait(e, 0)

    steps = NL * NT
    read_input(At(0, True), 0, None)
    step(At(0, True), ff=False)
    start = (ring.n % NR, list(ring.last))
    with nc.Fori(1, steps, engines=[e.engine for e in (pe, act, dve, pool)]) as u:
        step(At(u))
        assert start == (ring.n % NR, ring.last), (start, ring.n % NR, ring.last)
    end = At(steps)
    step(end, new=False, slots=3, ff=False)
    ring.last = [x and (x[0], x[1], x[2] + (B if x[0] == "tile" else 1), x[3]) for x in ring.last]
    for e in (pe, act, dve):
        s_wf.wait(e, NL - 1)
    for f in (ff_shift, ff_stats, ff_norm, ff_up, ff_down):
        f(end)

    def reload_ff(l):
        wait_at = (l * NT, -1)
        if isinstance(l, int):
            sp.wait_ge(s["f5"].sem, s["f5"].at(l * NT - 1))
        else:
            s["f5"].wait(sp, wait_at)
        load_ff(l)

    with nc.Fori(1, NL - 1, engines=[sp.engine]) as l:
        reload_ff(l)
        s["wo"].wait(sp, (l * (NT * B), -1))
        s_wa.wait(sp, (l, 0))
        load_attention(l + 1, (l + 1) % 2)
    reload_ff(NL - 1)
    nc.all_engine_barrier()
    c.close()


def tables():
    f32 = np.float32
    half = np.arange(0, LD, 2, dtype=f32)
    inv = (f32(1.0) / np.power(f32(10000.0), half / f32(LD))).astype(f32)
    t = np.arange(S, dtype=f32)
    fr = (t[:, None] * inv[None, :]).astype(f32)
    fr = np.concatenate([fr, fr], -1)
    base = ((half + f32(0.4 * LD)) / f32(1.4 * LD)).astype(f32)
    power = ((t - S // 2) / (WIN // 2)).astype(f32)
    sc = np.power(base[None, :], power[:, None]).astype(f32)
    sc = np.concatenate([sc, sc], -1)
    cos, sin = np.cos(fr).astype(f32), np.sin(fr).astype(f32)
    sign = np.where(np.arange(LD) < LD // 2, f32(-1), f32(1))
    q_k = []
    for scale in (sc * f32(8.0), (f32(1.0) / sc).astype(f32)):
        q_k.append(np.stack([cos * scale, sin * sign * scale]))
    r = np.stack(q_k, 2)
    rope = np.ascontiguousarray(r.reshape(2, NT, P, 2, LD).transpose(2, 1, 0, 3, 4)).astype(f32)
    q = np.arange(P)
    k = np.arange(KB)
    i = q[:, None] % QB
    ok = (k[None, :] >= i) & (k[None, :] <= i + WIN)
    m = np.zeros((P, NT, 4, KB), f32)
    m[~np.broadcast_to(ok[:, None, None, :], m.shape)] = MASKED
    pad = (q[:, None] < QB) & (k[None, :] < WIN)
    m[:, 0][np.broadcast_to(pad[:, None, :], (P, 4, KB))] = MASKED
    return rope, m.reshape(P, NT, 4 * KB)


def kernel(**inputs):
    import concourse.bacc as bacc
    from concourse.bass_utils import run_bass_kernel_spmd

    a = {k: np.asarray(v) for k, v in inputs.items()}
    rope, mask = tables()
    arrays = {
        "X": a["L0_attn_X"], "wqT": a["L0_attn_Wq"].T, "wkT": a["L0_attn_Wk"].T, "wvT": a["L0_attn_Wv"].T,
        "woT": a["L0_attn_Wo"].T, "bq": a["L0_attn_bq"].reshape(D, 1), "bk": a["L0_attn_bk"].reshape(D, 1),
        "bv": a["L0_attn_bv"].reshape(1, D), "bo": a["L0_attn_bo"].reshape(1, D),
        "Wqkv": a["L0_ffn_Wqkv"], "q_scale": a["L0_ffn_q_scale"], "k_scale": a["L0_ffn_k_scale"],
        "qk_scale": np.stack([a["L0_ffn_q_scale"], a["L0_ffn_k_scale"]], 1),
        "Wo": a["L0_ffn_Wo"], "ln_g": a["L0_ffn_ln_g"], "ln_b": a["L0_ffn_ln_b"], "W1": a["L0_ffn_W1"],
        "b1": a["L0_ffn_b1"], "W2": a["L0_ffn_W2"], "b2": a["L0_ffn_b2"], "cT": a["L0_c"].T,
        "wmod": a["L0_wmod"], "rope": rope, "mask": mask.astype(mybir.dt.np(BF16)),
    }
    arrays = {k: np.ascontiguousarray(v) for k, v in arrays.items()}
    nc = bacc.Bacc("TRN2", target_bir_lowering=False, num_devices=1)
    ins = {k: nc.dram_tensor(f"in_{k}", v.shape, mybir.dt.from_np(v.dtype), kind="ExternalInput").ap()
           for k, v in arrays.items()}
    out = nc.dram_tensor("out", (B, S, D), F32, kind="ExternalOutput").ap()
    build(nc, ins, out)
    r = run_bass_kernel_spmd(nc, [{f"in_{k}": v for k, v in arrays.items()}], core_ids=[0])
    return r.results[0]["out"]
```

```python
from contextlib import ExitStack

import numpy as np
import concourse.bass as bass
from concourse import mybir

F32 = mybir.dt.float32
BF16 = mybir.dt.bfloat16
F32R = mybir.dt.float32r
ALU = mybir.AluOpType
ACT = mybir.ActivationFunctionType
AX = mybir.AxisListType

P = 128
B, S, D = 4, 1024, 128
NT = S // P
H, DH = 16, 8
NL = 6
LH, LD = 16, 64
INNER = LH * LD
WIN = 32
FF = int(D * 4 * 2 / 3)
LN_EPS = 1e-5
MASKED = -1e30

QB = 64
KB = QB + WIN
CH = [(c * P, min(P, FF - c * P)) for c in range((FF + P - 1) // P)]

LASTW = CH[-1][1]

NPART = 3
NPROD = NPART * NPART * DH
MROW = 96
KROWS = MROW + 2
GH = 4
NG = B * H // GH
VW = 32


class Count:

    def __init__(self, sem, per=1):
        self.sem, self.per = sem, per

    def at(self, n, k=None):
        k = self.per if k is None else k
        if isinstance(n, tuple):
            base, off = n
            return base * self.per + (self.per * off + k)
        return self.per * n + k

    def wait(self, engine, n, k=None):
        engine.wait_ge(self.sem, self.at(n, k))


def build(nc, ins, out):
    pe, act, dve, pool, sp = nc.tensor, nc.scalar, nc.vector, nc.gpsimd, nc.sync
    whole = ExitStack()

    def sb(ctx, name, shape, dt=F32):
        return ctx.enter_context(nc.sbuf_tensor(name, shape, dt))

    def ps(ctx, name, shape, dt=F32):
        return ctx.enter_context(nc.psum_tensor(name, shape, dt))

    def count(ctx, name, per=1):
        return Count(ctx.enter_context(nc.semaphore(name)), per)

    X = sb(whole, "X", [P, B, NT, D])
    ident = sb(whole, "ident", [P, P])
    ident_b = sb(whole, "ident_b", [P, P], BF16)
    ones = sb(whole, "ones", [P, P])
    gate_b = sb(whole, "gate_b", [P, B, D])
    spare = sb(whole, "spare", [P, 1])
    x_mid = nc.dram_tensor("x_mid", [P, B, NT, D], F32, kind="Internal").ap()
    parts_d = [nc.dram_tensor(f"parts_{n}", [B, NPART, P, S], BF16, kind="Internal").ap() for n in "qk"]
    x_dram = ins["X"].rearrange("b (t p) c -> p b t c", p=P)
    out_dram = out.rearrange("b (t p) c -> p b t c", p=P)

    first = ExitStack()
    mod = sb(first, "mod", [P, 6, B, D])
    VA = sb(first, "VA", [P, B, NT, H, DH + 1])
    AO = sb(first, "AO", [P, B, NT, D])
    woT = sb(first, "woT", [P, D])
    rows = sb(first, "rows", [1, 2, D])
    QA = sb(first, "QA", [KROWS, 2, 2, GH, 512], BF16)
    KA = sb(first, "KA", [KROWS, 2, GH, S], BF16)
    VG = sb(first, "VG", [P, 2, NT, GH, VW])
    s_z = count(first, "s_z")

    with ExitStack() as c:
        cT = sb(c, "cT", [P, B])
        wmod = sb(c, "wmod", [P, 6 * D])
        sig = sb(c, "sig", [P, 3, B])
        modT = sb(c, "modT", [P, 6, B])
        tmp = sb(c, "tmp", [P, 2, 2, B])
        diag = sb(c, "diag", [P, 6, B, D])
        p_mod = ps(c, "p_mod", [P, 6, B])
        p_bc = ps(c, "p_bc", [P, 6, B, D])
        s_in = count(c, "s_in", 16)
        s_cst = count(c, "s_cst")
        s_v = count(c, "s_v")
        s_e = count(c, "s_e")
        s_m = count(c, "s_m")
        s_dg = count(c, "s_dg")
        s_bc = count(c, "s_bc")
        s_mc = count(c, "s_mc")
        for dst, src in ((cT[:, :], ins["cT"]), (wmod[:, :], ins["wmod"]), (X[:, :, :, :], x_dram),
                         (woT[:, :], ins["woT"]), (rows[:, 0, :], ins["bv"]), (rows[:, 1, :], ins["bo"])):
            sp.dma_start(dst, src).then_inc(s_in.sem, 16)
        pool.memset(ident[:, :], 0.0).then_inc(s_cst.sem, 1)
        pool.memset(ones[:, :], 1.0).then_inc(s_cst.sem, 1)
        pool.memset(VA[:, :, :, :, DH:DH + 1], 1.0).then_inc(s_cst.sem, 1)
        pool.wait_ge(s_cst.sem, 3)
        pool.affine_select(out=ident[:, :], in_=ident[:, :], compare_op=ALU.not_equal, fill=1.0,
                           base=0, pattern=[[-1, P]], channel_multiplier=1).then_inc(s_cst.sem, 1)
        pool.memset(QA[:, :, :, :, :], 0.0).then_inc(s_z.sem, 1)
        pool.memset(VG[:, :, :, :, :], 0.0).then_inc(s_z.sem, 1)
        pool.memset(KA[0:MROW, :, :, :], 0.0).then_inc(s_z.sem, 1)
        pool.wait_ge(s_z.sem, 3)
        pool.memset(KA[MROW:KROWS, :, :, :], 1.0).then_inc(s_z.sem, 1)
        act.wait_ge(s_in.sem, 16 * 6)
        act.activation(sig[:, 0, :], cT[:, :], ACT.Exp, scale=-1.0).then_inc(s_e.sem, 1)
        n_v = 0

        def step(ins_):
            nonlocal n_v
            n_v += 1
            ins_.then_inc(s_v.sem, 1)
            dve.wait_ge(s_v.sem, n_v)

        dve.wait_ge(s_cst.sem, 4)
        step(dve.tensor_copy(ident_b[:, :], ident[:, :]))
        dve.wait_ge(s_e.sem, 1)
        step(dve.tensor_scalar_add(sig[:, 1, :], sig[:, 0, :], 1.0))
        step(dve.reciprocal(sig[:, 2, :], sig[:, 1, :]))
        step(dve.tensor_tensor(out=sig[:, 0, :], in0=cT[:, :], in1=sig[:, 2, :], op=ALU.mult))
        pe.wait_ge(s_v.sem, n_v)
        pe.wait_ge(s_in.sem, 16 * 6)
        for j in range(6):
            mm = pe.matmul(p_mod[:, j, :], wmod[:, j * D:(j + 1) * D], sig[:, 0, :], start=True, stop=True)
        mm.then_inc(s_m.sem, 1)
        dve.wait_ge(s_m.sem, 1)
        step(dve.tensor_copy(modT[:, :, :], p_mod[:, :, :]))
        scales, gates = modT[:, 1:5:3, :], modT[:, 2:6:3, :]
        step(dve.tensor_scalar_add(scales, scales, 1.0))
        step(dve.tensor_scalar(tmp[:, 0, :, :], gates, -1.0, None, ALU.mult))
        step(dve.tensor_tensor(out=tmp[:, 0, :, :], in0=gates, in1=tmp[:, 0, :, :], op=ALU.max))
        step(dve.tensor_scalar_max(tmp[:, 0, :, :], tmp[:, 0, :, :], 0.25))
        step(dve.tensor_scalar(tmp[:, 1, :, :], gates, 0.0, 2.0, ALU.is_ge, ALU.mult))
        step(dve.tensor_scalar_add(tmp[:, 1, :, :], tmp[:, 1, :, :], -1.0))
        step(dve.tensor_tensor(out=gates, in0=tmp[:, 0, :, :], in1=tmp[:, 1, :, :], op=ALU.mult))
        for j in range(6):
            for b in range(B):
                dg = dve.tensor_scalar(diag[:, j, b, :], ident[:, :], modT[:, j, b:b + 1], None, ALU.mult)
            dg.then_inc(s_dg.sem, 1)
            s_dg.wait(pe, j)
            pe.matmul(p_bc[:, j, :, :], ones[:, :], diag[:, j, :, :], start=True, stop=True).then_inc(s_bc.sem, 1)
            s_bc.wait(act, j)
            act.activation(mod[:, j, :, :], p_bc[:, j, :, :], ACT.Copy).then_inc(s_mc.sem, 1)
        dve.wait_ge(s_mc.sem, 6)
        dve.tensor_copy(gate_b[:, :, :], mod[:, 5, :, :])
        nc.all_engine_barrier()

    CT = 4
    NC = B * NT // CT
    with ExitStack() as c:
        wT = [sb(c, f"w{n}T", [P, D]) for n in "qkv"]
        bias = sb(c, "bias_qk", [P, 2])
        stats = sb(c, "stats", [P, 2, CT, 6])
        mv = sb(c, "mv", [P, 2, CT, 2])
        power = sb(c, "power", [P, CT])
        rstd = sb(c, "rstd", [P, 2, CT])
        hn = sb(c, "hn", [P, 2, CT, D])
        hT = sb(c, "hT", [P, 2, CT * P])
        full = sb(c, "full", [P, 2, 2, CT * P])
        rest = sb(c, "rest", [P, 2, CT * P])
        parts = sb(c, "parts", [P, 2, 2, NPART, CT * P], BF16)
        p_t = ps(c, "p_t", [P, 2, CT * P])
        p_qk = ps(c, "p_qk", [P, 2, 2, CT * P])
        p_v = ps(c, "p_v", [P, 2, CT, D])
        s_w = count(c, "s_w", 16)
        s_pw = count(c, "s_pw")
        s_ln = count(c, "s_ln", 6)
        s_rs = count(c, "s_rs")
        s_t = count(c, "s_t")
        s_hT = count(c, "s_hT")
        s_qk = count(c, "s_qk", 2)
        s_vp = count(c, "s_vp")
        s_full = count(c, "s_full", 2)
        s_va = count(c, "s_va")
        s_sp = count(c, "s_sp", 10)
        s_pd = [[count(c, f"s_pd{u}{n}", 16) for n in "qk"] for u in range(2)]
        for dst, src in ((wT[0][:, :], ins["wqT"]), (wT[1][:, :], ins["wkT"]), (wT[2][:, :], ins["wvT"]),
                         (bias[:, 0:1], ins["bq"]), (bias[:, 1:2], ins["bk"])):
            sp.dma_start(dst, src).then_inc(s_w.sem, 16)
        pool.memset(power[:, :], -0.5).then_inc(s_pw.sem, 1)
        pool.wait_ge(s_pw.sem, 1)
        pe.wait_ge(s_w.sem, 16 * 5)
        act.wait_ge(s_w.sem, 16 * 5)

        def layernorm(n, b, u, fresh):
            for j in range(CT):
                i = dve.bn_stats(stats[:, u, j, :], X[:, b, CT * u + j, :])
            i.then_inc(s_ln.sem, 1)
            s_ln.wait(dve, n, 1)
            dve.memset(spare[:, :], 0.0)
            for j in range(CT):
                i = dve.bn_aggr(mv[:, u, j, :], stats[:, u, j, :])
            i.then_inc(s_ln.sem, 1)
            s_ln.wait(dve, n, 2)
            dve.tensor_scalar_add(mv[:, u, :, 1:2], mv[:, u, :, 1:2], LN_EPS).then_inc(s_ln.sem, 1)
            s_ln.wait(pool, n, 3)
            pool.tensor_tensor(out=rstd[:, u, :], in0=mv[:, u, :, 1], in1=power[:, :], op=ALU.pow)\
                .then_inc(s_rs.sem, 1)
            s_rs.wait(dve, n)
            if not fresh:
                s_t.wait(dve, (n[0], n[1] - 2))
            for j in range(CT):
                i = dve.tensor_scalar(hn[:, u, j, :], X[:, b, CT * u + j, :], mv[:, u, j, 0:1],
                                      rstd[:, u, j:j + 1], ALU.subtract, ALU.mult)
            i.then_inc(s_ln.sem, 1)
            for m, op in ((1, ALU.mult), (0, ALU.add)):
                s_ln.wait(dve, n, 5 - m)
                dve.tensor_tensor(out=hn[:, u, :, :], in0=hn[:, u, :, :],
                                  in1=mod[:, m, b, :].unsqueeze(1).broadcast_to([P, CT, D]),
                                  op=op).then_inc(s_ln.sem, 1)

        def chunk(n, b, u, fresh, more=True):
            s_ln.wait(pe, n, 6)
            if not fresh:
                s_hT.wait(pe, (n[0], n[1] - 2))
            for j in range(CT):
                mm = pe.transpose(p_t[:, u, j * P:(j + 1) * P], hn[:, u, j, :], ident[:, :])
            mm.then_inc(s_t.sem, 1)
            s_t.wait(act, n)
            if not fresh:
                s_vp.wait(act, (n[0], n[1] - 2))
            act.activation(hT[:, u, :], p_t[:, u, :], ACT.Copy).then_inc(s_hT.sem, 1)
            s_hT.wait(pe, n)
            for i in range(2):
                if not fresh:
                    s_full.wait(pe, (n[0], n[1] - 2), i + 1)
                pe.matmul(p_qk[:, u, i, :], wT[i][:, :], hT[:, u, :], start=True, stop=True).then_inc(s_qk.sem, 1)
            if not fresh:
                s_va.wait(pe, (n[0], n[1] - 2))
            for j in range(CT):
                pe.matmul(p_v[:, u, j, :], hT[:, u, j * P:(j + 1) * P], wT[2][:, :], start=True, stop=False)
                mm = pe.matmul(p_v[:, u, j, :], ones[0:1, :], rows[:, 0, :], start=False, stop=True)
            mm.then_inc(s_vp.sem, 1)
            for i in range(2):
                s_qk.wait(act, n, i + 1)
                if not fresh:
                    s_sp.wait(act, (n[0], n[1] - 2))
                act.activation(full[:, u, i, :], p_qk[:, u, i, :], ACT.Identity,
                               bias=bias[:, i:i + 1]).then_inc(s_full.sem, 1)
            s_vp.wait(act, n)
            act.activation(VA[:, b, CT * u:CT * u + CT, :, 0:DH],
                           p_v[:, u, :, :].rearrange("p t (h d) -> p t h d", d=DH),
                           ACT.Copy).then_inc(s_va.sem, 1)
            if more:
                layernorm((n[0], n[1] + 1), b + u, 1 - u, fresh and u == 0)
            for i in range(2):
                s_full.wait(dve, n, i + 1)
                if not fresh:
                    s_pd[u][i].wait(dve, (b, -1))
                k = 5 * i
                dve.tensor_copy(parts[:, u, i, 0, :], full[:, u, i, :]).then_inc(s_sp.sem, 1)
                s_sp.wait(dve, n, k + 1)
                dve.tensor_tensor(out=rest[:, i, :], in0=full[:, u, i, :], in1=parts[:, u, i, 0, :],
                                  op=ALU.subtract).then_inc(s_sp.sem, 1)
                s_sp.wait(dve, n, k + 2)
                dve.tensor_copy(parts[:, u, i, 1, :], rest[:, i, :]).then_inc(s_sp.sem, 1)
                s_sp.wait(dve, n, k + 3)
                dve.tensor_tensor(out=parts[:, u, i, 2, :], in0=rest[:, i, :], in1=parts[:, u, i, 1, :],
                                  op=ALU.subtract).then_inc(s_sp.sem, 2)
                s_sp.wait(sp, n, k + 5)
                sp.dma_start(parts_d[i][b, :, :, u * CT * P:(u + 1) * CT * P].rearrange("j p n -> p j n"),
                             parts[:, u, i, :, :]).then_inc(s_pd[u][i].sem, 16)

        layernorm((0, 0), 0, 0, True)
        for u in range(2):
            chunk((0, u), 0, u, True)
        with nc.Fori(1, B - 1) as b:
            for u in range(2):
                chunk((b * 2, u), b, u, False)
        for u in range(2):
            chunk((2 * (B - 1), u), B - 1, u, False, more=(u == 0))
        for u in range(2):
            for i in range(2):
                s_pd[u][i].wait(sp, B - 1)
        nc.all_engine_barrier()

    with ExitStack() as c:
        E = sb(c, "E", [P, 4, GH, 512])
        negmax = sb(c, "negmax", [P, 2, GH, 4])
        nm = sb(c, "nm", [GH * 4, 2, P])
        nmb = sb(c, "nmb", [GH * 4, 2, 2, P], BF16)
        OE = sb(c, "OE", [P, 2, 512])
        rsum = sb(c, "rsum", [P, 2, 4, GH])
        p_max = ps(c, "p_max", [P, 2, S])
        p_s = ps(c, "p_s", [P, 2, 512])
        p_o = ps(c, "p_o", [P, 2, 512])
        HU = 16
        s_ld = count(c, "s_ld", 16 * 3 * NPART * NPART)
        s_vg = count(c, "s_vg")
        s_mx = count(c, "s_mx", 2 * HU + 2)
        s_mr = count(c, "s_mr", 2 * HU + 2)
        s_mb = count(c, "s_mb", 4)
        s_md = count(c, "s_md", 64)
        s_st = count(c, "s_st", 64)
        s_ex = count(c, "s_ex", 64)
        s_pv = count(c, "s_pv", 16)
        s_oe = count(c, "s_oe", 2)
        s_ot = count(c, "s_ot", 2)
        s_rc = count(c, "s_rc", 2)
        s_ao = count(c, "s_ao", 2)

        sp.wait_ge(s_z.sem, 4)
        pool.wait_ge(s_z.sem, 4)
        pe.wait_ge(s_z.sem, 4)

        def add(n, d):
            return (n[0], n[1] + d) if isinstance(n, tuple) else n + d

        def heads(hg):
            return slice(hg * GH, hg * GH + GH) if isinstance(hg, int) else bass.ds(hg * GH, GH)

        def load(n, b, hg, p, reuse):
            if reuse:
                s_st.wait(sp, add(n, -2))
            for i in range(NPART):
                for j in range(NPART):
                    r = (i * NPART + j) * DH
                    q = parts_d[0][b, i].rearrange("(h d) n -> d h n", d=DH)
                    k = parts_d[1][b, j].rearrange("(h d) n -> d h n", d=DH)
                    for qh in range(2):
                        sp.dma_start(QA[r:r + DH, p, qh, :, :], q[:, heads(hg), qh * 512:(qh + 1) * 512])\
                            .then_inc(s_ld.sem, 16)
                    sp.dma_start(KA[r:r + DH, p, :, :], k[:, heads(hg), :]).then_inc(s_ld.sem, 16)

        def values(n, b, hg, p, reuse):
            if reuse:
                s_pv.wait(pool, add(n, -2))
            pool.tensor_copy(VG[:, p, :, :, 0:DH + 1], VA[:, b, :, heads(hg), :]).then_inc(s_vg.sem, 1)

        unit_log = {}

        def max_unit(n, p, qh, i, reuse, halves=(0, 1)):
            k = qh * (HU + 1) + i
            c_, qt = divmod(i, 4)
            if 0 in halves and (reuse or k >= 2):
                s_mr.wait(pe, n if k >= 2 else add(n, -1), k - 1 if k >= 2 else 2 * HU + 2 + k - 1)
            if i == 0 and qh == 0:
                s_ld.wait(pe, n)
            slot = k % 2
            for j in halves:
                mm = pe.matmul(p_max[:, slot, j * 512:(j + 1) * 512], QA[0:NPROD, p, qh, c_, qt * P:(qt + 1) * P],
                               KA[0:NPROD, p, c_, j * 512:(j + 1) * 512], start=True, stop=True)
            if 1 not in halves:
                return
            mm.then_inc(s_mx.sem, 1)
            s_mx.wait(dve, n, k + 1)
            dve.tensor_reduce(negmax[:, qh, c_, qt:qt + 1], p_max[:, slot, :], axis=AX.X, op=ALU.max,
                              negate=True).then_inc(s_mr.sem, 1)

        def max_rows(n, p, qh, reuse):
            k = qh * (HU + 1) + HU
            slot = k % 2
            s_mr.wait(pe, n, k)
            pe.transpose(p_max[0:GH * 4, slot, 0:P], negmax[:, qh, :, :].rearrange("p c q -> p (c q)"),
                         ident[:, :]).then_inc(s_mx.sem, 1)
            s_mx.wait(dve, n, k + 1)
            dve.tensor_copy(nm[:, qh, :], p_max[0:GH * 4, slot, 0:P]).then_inc(s_mr.sem, 1)
            s_mr.wait(dve, n, k + 1)
            if reuse:
                s_md.wait(dve, add(n, -1), 32 * (qh + 1))
            dve.tensor_copy(nmb[:, qh, 0, :], nm[:, qh, :]).then_inc(s_mb.sem, 1)
            s_mb.wait(dve, n, 2 * qh + 1)
            dve.tensor_tensor(out=nmb[:, qh, 1, :], in0=nm[:, qh, :], in1=nmb[:, qh, 0, :],
                              op=ALU.subtract).then_inc(s_mb.sem, 1)
            s_mb.wait(sp, n, 2 * qh + 2)
            for j in range(2):
                sp.dma_start(QA[MROW + j:MROW + j + 1, p, qh, :, :],
                             nmb[:, qh, j, :]).then_inc(s_md.sem, 16)

        def score(n, p, s, c_, reuse):
            qh, kb = divmod(s, 8)
            i = 4 * s + c_
            if i >= 2:
                s_ex.wait(pe, n, i - 1)
            elif reuse:
                s_ex.wait(pe, add(n, -1), 64 + i - 1)
            if kb == 0 and c_ == 0:
                s_md.wait(pe, n, 32 * (qh + 1))
            pe.matmul(p_s[:, i % 2, :], KA[:, p, c_, kb * P:(kb + 1) * P], QA[:, p, qh, c_, :],
                      start=True, stop=True).then_inc(s_st.sem, 1)
            s_st.wait(act, n, i + 1)
            if c_ == 0 and (s >= 4 or reuse):
                s_pv.wait(act, n if s >= 4 else add(n, -1), s - 3 if s >= 4 else s + 13)
            act.activation(E[:, s % 4, c_, :], p_s[:, i % 2, :], ACT.Exp, scale=DH ** -0.5)\
                .then_inc(s_ex.sem, 1)

        def weigh(n, p, s, reuse, halves=(0, 1)):
            qh, kb = divmod(s, 8)
            if kb == 0:
                if 0 not in halves:
                    return
                lo, hi = 0, 512
            else:
                lo, hi = 256 * halves[0], 256 * (halves[-1] + 1)
            s_ex.wait(pe, n, 4 * s + 4)
            if s == 0:
                s_vg.wait(pe, n)
            if kb == 0 and reuse:
                s_ao.wait(pe, add(n, -1), qh + 1)
            for c_ in range(GH):
                mm = pe.matmul(p_o[c_ * VW:(c_ + 1) * VW, qh, lo:hi], VG[:, p, kb, c_, :], E[:, s % 4, c_, lo:hi],
                               start=(kb == 0), stop=(kb == 7), skip_group_check=True)
            if hi == 512:
                mm.then_inc(s_pv.sem, 1)

        def result_copy(n, qh, reuse):
            s_pv.wait(dve, n, 8 * (qh + 1))
            if reuse:
                s_ot.wait(dve, add(n, -1), qh + 1)
            dve.tensor_copy(OE[:, qh, :], p_o[:, qh, :]).then_inc(s_oe.sem, 1)

        def result(n, b, hg, qh, reuse):
            s_oe.wait(pe, n, qh + 1)
            for qt in range(4):
                mm = pe.transpose(p_o[:, qh, qt * P:(qt + 1) * P], OE[:, qh, qt * P:(qt + 1) * P], ident[:, :])
            mm.then_inc(s_ot.sem, 1)
            s_ot.wait(dve, n, qh + 1)
            o = p_o[:, qh, :].rearrange("p (q c w) -> p q c w", q=4, w=VW)
            dve.reciprocal(rsum[:, qh, :, :], o[:, :, :, DH]).then_inc(s_rc.sem, 1)
            s_rc.wait(dve, n, qh + 1)
            a = AO[:, b, 4 * qh:4 * qh + 4, :].rearrange("p q (g c d) -> p q g c d", g=H // GH, d=DH)
            a = a[:, :, hg, :, :]
            dve.tensor_tensor(out=a, in0=o[:, :, :, 0:DH],
                              in1=rsum[:, qh, :, :].unsqueeze(3).broadcast_to([P, 4, GH, DH]),
                              op=ALU.mult).then_inc(s_ao.sem, 1)

        def group(n, p, at, nxt, prev, reuse):
            for s in range(16):
                if s == 0 and nxt:
                    load(add(n, 1), *nxt, 1 - p, reuse)
                    values(add(n, 1), *nxt, 1 - p, reuse)
                if s < 6:
                    units = [(n, p, 1, 4 + 2 * s + i, True) for i in range(2)]
                elif s < 14:
                    units = nxt and [(add(n, 1), 1 - p, 0, 2 * (s - 6) + i, True) for i in range(2)]
                else:
                    units = nxt and [(add(n, 1), 1 - p, 1, 2 * (s - 14) + i, True) for i in range(2)]
                w = (n, p, s - 1, reuse) if s > 0 else prev and (add(n, -1), 1 - p, 15, True)
                score(n, p, s, 0, reuse)
                if units and s % 8 != 6:
                    max_unit(*units[0])
                score(n, p, s, 1, reuse)
                if w:
                    weigh(*w, halves=(0,))
                if s == 6:
                    max_rows(n, p, 1, reuse)
                if s == 14 and nxt:
                    max_rows(add(n, 1), 1 - p, 0, True)
                score(n, p, s, 2, reuse)
                if units:
                    max_unit(*units[0 if s % 8 == 6 else 1])
                score(n, p, s, 3, reuse)
                if w:
                    weigh(*w, halves=(1,))
                if units and s % 8 == 6:
                    max_unit(*units[1])
                if s == 2 and prev:
                    result_copy(add(n, -1), 1, True)
                if s == 3 and prev:
                    result(add(n, -1), *prev, 1, True)
                if s == 10:
                    result_copy(n, 0, reuse)
                if s == 11:
                    result(n, *at, 0, reuse)

        load(0, 0, 0, 0, False)
        values(0, 0, 0, 0, False)
        for i in range(HU):
            max_unit(0, 0, 0, i, False)
        max_rows(0, 0, 0, False)
        for i in range(4):
            max_unit(0, 0, 1, i, False)
        HG = H // GH
        where = [(g // HG, g % HG) for g in range(NG)]
        group(0, 0, where[0], where[1], None, False)
        group(1, 1, where[1], where[2], where[0], True)
        with nc.Fori(1, NG // 2 - 1) as it:
            b0, hp = it // 2, it % 2
            g0 = (it * 2, 0)
            nb, nh = (it + 1) // 2, (it + 1) % 2
            pb, ph = (it - 1) // 2, (it - 1) % 2
            group(g0, 0, (b0, hp * 2), (b0, hp * 2 + 1), (pb, ph * 2 + 1), True)
            group((it * 2, 1), 1, (b0, hp * 2 + 1), (nb, nh * 2), (b0, hp * 2), True)
        group(NG - 2, 0, where[-2], where[-1], where[-3], True)
        group(NG - 1, 1, where[-1], None, where[-2], True)
        weigh(NG - 1, 1, 15, True)
        result_copy(NG - 1, 1, True)
        result(NG - 1, *where[-1], 1, True)
        nc.all_engine_barrier()

    with ExitStack() as c:
        ao = sb(c, "ao", [P, B, D])
        aoT = sb(c, "aoT", [P, B, P])
        gated = sb(c, "gated", [P, B, D])
        stats = sb(c, "stats2", [P, B, 6])
        mv = sb(c, "mv2", [P, B, 2])
        power = sb(c, "power2", [P, B])
        rstd = sb(c, "rstd2", [P, B])
        p_t = ps(c, "p_t2", [P, B, P])
        p_w = ps(c, "p_w2", [P, B, D])
        s_pw = count(c, "s_pw2")
        s_c = count(c, "s_c")
        s_t = count(c, "s_t2")
        s_tc = count(c, "s_tc")
        s_w = count(c, "s_w2")
        s_d = count(c, "s_d", 8)
        s_r = count(c, "s_r2")
        s_xm = count(c, "s_xm", 16)
        pool.memset(power[:, :], -0.5).then_inc(s_pw.sem, 1)
        pool.wait_ge(s_pw.sem, 1)
        def add(n, d):
            return (n[0], n[1] + d) if isinstance(n, tuple) else n + d

        def fetch(n, t):
            dve.tensor_scalar_mul(ao[:, :, :], AO[:, :, t, :], 1.0).then_inc(s_c.sem, 1)

        def product(n):
            s_c.wait(pe, n)
            for b in range(B):
                mm = pe.transpose(p_t[:, b, :], ao[:, b, :], ident[:, :])
            mm.then_inc(s_t.sem, 1)
            s_t.wait(act, n)
            act.activation(aoT[:, :, :], p_t[:, :, :], ACT.Copy).then_inc(s_tc.sem, 1)
            s_tc.wait(pe, n)
            for b in range(B):
                pe.matmul(p_w[:, b, :], aoT[:, b, :], woT[:, :], start=True, stop=False)
                mm = pe.matmul(p_w[:, b, :], ones[0:1, :], rows[:, 1, :], start=False, stop=True)
            mm.then_inc(s_w.sem, 1)

        def residual(n, t, more):
            s_w.wait(dve, n)
            dve.tensor_tensor(out=gated[:, :, :], in0=p_w[:, :, :], in1=mod[:, 2, :, :], op=ALU.mult)\
                .then_inc(s_d.sem, 1)
            if more:
                fetch(add(n, 1), t + 1)
                s_d.wait(pe, n, 1)
                product(add(n, 1))
            s_d.wait(dve, n, 1)
            dve.tensor_tensor(out=gated[:, :, :], in0=gated[:, :, :], in1=X[:, :, t, :], op=ALU.add)\
                .then_inc(s_d.sem, 1)
            s_d.wait(dve, n, 2)
            s_d.wait(sp, n, 2)
            sp.dma_start(x_mid[:, :, t, :], gated[:, :, :]).then_inc(s_xm.sem, 16)
            for b in range(B):
                i = dve.bn_stats(stats[:, b, :], gated[:, b, :])
            i.then_inc(s_d.sem, 1)
            s_d.wait(dve, n, 3)
            dve.memset(spare[:, :], 0.0)
            for b in range(B):
                i = dve.bn_aggr(mv[:, b, :], stats[:, b, :])
            i.then_inc(s_d.sem, 1)
            s_d.wait(dve, n, 4)
            dve.tensor_scalar_add(mv[:, :, 1:2], mv[:, :, 1:2], LN_EPS).then_inc(s_d.sem, 1)
            s_d.wait(pool, n, 5)
            pool.tensor_tensor(out=rstd[:, :], in0=mv[:, :, 1], in1=power[:, :], op=ALU.pow)\
                .then_inc(s_r.sem, 1)
            s_r.wait(dve, n)
            for b in range(B):
                i = dve.tensor_scalar(X[:, b, t, :], gated[:, b, :], mv[:, b, 0:1], rstd[:, b:b + 1],
                                      ALU.subtract, ALU.mult)
            i.then_inc(s_d.sem, 1)
            s_d.wait(dve, n, 6)
            dve.tensor_tensor(out=X[:, :, t, :], in0=X[:, :, t, :], in1=mod[:, 4, :, :], op=ALU.mult)\
                .then_inc(s_d.sem, 1)
            s_d.wait(dve, n, 7)
            s_xm.wait(dve, n)
            dve.tensor_tensor(out=X[:, :, t, :], in0=X[:, :, t, :], in1=mod[:, 3, :, :], op=ALU.add)\
                .then_inc(s_d.sem, 1)
            s_d.wait(dve, n, 8)

        fetch(0, 0)
        product(0)
        with nc.Fori(0, NT - 1) as t:
            residual((t, 0), t, True)
        residual(NT - 1, NT - 1, False)
        nc.all_engine_barrier()
    first.close()

    layers(nc, ins, X, ident, ident_b, spare, sb, ps, count)

    with ExitStack() as c:
        XM = sb(c, "XM", [P, B, NT, D])
        s_l = count(c, "s_l", 16)
        s_f = count(c, "s_f", 2)
        s_out = count(c, "s_out", 16)
        for b in range(B):
            sp.dma_start(XM[:, b, :, :], x_mid[:, b, :, :]).then_inc(s_l.sem, 16)
        for b in range(B):
            dve.tensor_tensor(out=X[:, b, :, :], in0=X[:, b, :, :],
                              in1=gate_b[:, b, :].unsqueeze(1).broadcast_to([P, NT, D]),
                              op=ALU.mult).then_inc(s_f.sem, 1)
            dve.wait_ge(s_f.sem, 2 * b + 1)
            dve.wait_ge(s_l.sem, 16 * B)
            dve.tensor_tensor(out=X[:, b, :, :], in0=X[:, b, :, :], in1=XM[:, b, :, :],
                              op=ALU.add).then_inc(s_f.sem, 1)
            s_f.wait(sp, b)
            sp.dma_start(out_dram[:, b, :, :], X[:, b, :, :]).then_inc(s_out.sem, 16)
        sp.wait_ge(s_out.sem, 16 * B)
    whole.close()


def layers(nc, ins, X, ident, ident_b, spare, sb, ps, count):
    pe, act, dve, pool, sp = nc.tensor, nc.scalar, nc.vector, nc.gpsimd, nc.sync
    c = ExitStack()
    Wqkv = sb(c, "Wqkv", [P, 2, 2, 3 * INNER], F32R)
    share = 3 * INNER // NT
    Wraw = sb(c, "Wraw", [P, share])
    Wo = sb(c, "Wo", [P, 2, LH // 2, D])
    qks = sb(c, "qks", [P, 2, 2, 2, LD])
    W1 = sb(c, "W1", [P, 2 * FF])
    W2 = sb(c, "W2", [P, len(CH), D])
    b1 = sb(c, "b1", [P, 2, len(CH)])
    ln = sb(c, "ln", [P, 2])
    rope = sb(c, "rope", [P, NT, 2, 2, LD])
    tab = sb(c, "tab", [P, 2, 2, LD])
    mask = sb(c, "mask", [P, 2, 4 * KB], BF16)
    power = sb(c, "power3", [P, 2 * LH])
    begun = sb(c, "begun", [P, NT])
    xin = sb(c, "xin", [P, B, D])
    XS = sb(c, "XS", [P, B, 2, WIN + P + 1], F32R)
    QK = sb(c, "QK", [P, 2 * INNER])
    SQ = sb(c, "SQ", [P, 2 * INNER])
    T1 = sb(c, "T1", [P, 2, 2 * INNER])
    T2 = sb(c, "T2", [P, 2 * INNER])
    ss = sb(c, "ss", [P, 2, 2 * LH])
    rn = sb(c, "rn", [P, 2, 2 * LH])
    qT = sb(c, "qT", [P, LH // 2, P])
    kT = sb(c, "kT", [P, LH // 2, WIN + P])
    kH = sb(c, "kH", [P, B, LH // 2, WIN])
    E = sb(c, "Ew", [P, 2, LH, KB])
    mx = sb(c, "mx", [P, 2, LH])
    sm = sb(c, "sm", [P, 2, 2, LH])
    V = sb(c, "V", [KB, 2, INNER])
    ET = sb(c, "ET", [KB, LH, P])
    OT = sb(c, "OT", [P, LH // 2, P])
    x1 = sb(c, "x1", [P, B, D])
    FS = sb(c, "FS", [P, B, P + 1])
    fx = sb(c, "fx", [P, B, D])
    fst = sb(c, "fst", [P, B, 6])
    fmv = sb(c, "fmv", [P, B, 2])
    frs = sb(c, "frs", [P, B])
    fnT = sb(c, "fnT", [P, B * P])
    G = sb(c, "G", [P, 2, B * P])
    HH = sb(c, "HH", [P, len(CH), B * P])
    NR = 4
    R = ps(c, "R", [P, NR, 512])
    PS = ps(c, "PS", [P, 4, 512])

    names = dict(xi=1, tab=1, wsp=2, xT=1, hal=1, xs=2, xl=2, qk=4, qke=4, sq=1, t1=1, t2=1, ss=2, pw=1, ad=1, no=1,
                 tq=4, kh=1, te=6, s=2, mx=2, sub=2, ex=2, sum=1, rc=1, pn=1, vp=4, ve=4, pt=4, pe=4,
                 pv=2, oe=2, wo=1, x1=2, f1=1, fc=1, f1e=2, f2=1, f2e=1, fst=3, frs=1, fn=1, f3=1, f3e=1,
                 ff=6, g=3, hh=3, f5=1, fx=1)
    s = {k: count(c, "l_" + k, per) for k, per in names.items()}
    s_wa = count(c, "l_wa", 16 * 6)
    s_wr = count(c, "l_wr", 16)
    s_wf = count(c, "l_wf", 16 * 9)
    s_c = count(c, "l_c", 16 * 2)
    s_one = count(c, "l_one")
    s_w0 = count(c, "l_w0", 16 + 2)

    def load_attention(l, par):
        hf = LD // 2
        for dst, src in (
            (qks[:, par, 0, 0, :], ins["q_scale"][l].partition_broadcast(P)),
            (qks[:, par, 0, 1, :], ins["k_scale"][l].partition_broadcast(P)),
            (qks[:, par, 1, :, 0:hf], ins["qk_scale"][l, :, hf:LD].partition_broadcast(P)),
            (qks[:, par, 1, :, hf:LD], ins["qk_scale"][l, :, 0:hf].partition_broadcast(P)),
            (Wo[:, par, 0:4, :], ins["Wo"][l, 0:4 * P].rearrange("(a p) n -> p a n", p=P)),
            (Wo[:, par, 4:8, :], ins["Wo"][l, 4 * P:8 * P].rearrange("(a p) n -> p a n", p=P)),
        ):
            sp.dma_start(dst, src).then_inc(s_wa.sem, 16)

    def load_ff(l):
        for dst, src in (
            (W1[:, :], ins["W1"][l]),
            (W2[:, 0:2, :], ins["W2"][l, 0:2 * P].rearrange("(a p) n -> p a n", p=P)),
            (W2[0:FF - 2 * P, 2, :], ins["W2"][l, 2 * P:FF]),
            *((b1[0:w, :, i], ins["b1"][l].rearrange("(i f) -> f i", i=2)[lo:lo + w]) for i, (lo, w) in enumerate(CH)),
            (W2[LASTW:LASTW + 1, len(CH) - 1, :], ins["b2"][l].unsqueeze(0)),
            (ln[:, 0:1], ins["ln_g"][l].unsqueeze(1)),
            (ln[:, 1:2], ins["ln_b"][l].unsqueeze(1)),
        ):
            with nc.allow_non_contiguous_dma("small columns"):
                sp.dma_start(dst, src).then_inc(s_wf.sem, 16)

    class At:

        def __init__(self, u, first=False):
            self.u, self.first = u, first
            self.tile = u * B
            self.t, self.t_prev, self.t_next = u % NT, (u + NT - 1) % NT, (u + 1) % NT
            self.layer, self.par = u // NT, u // NT % 2
            self.par_prev = ((u + NT - 1) // NT + 1) % 2

        def time(self, d):
            return self.t if d >= 0 else self.t_prev

        def later(self, d):
            return (self.time(d) + NT - 1) // NT

        def before(self, d):
            return (self.u + NT + d) % NT

        def parity(self, d):
            return self.par if d >= 0 else self.par_prev

    waited = {}

    def wait_once(e, name, base, d, k):
        k = s[name].per if k is None else k
        if waited.get((e.engine, name), (-99, 0)) >= (d, k):
            return
        waited[e.engine, name] = (d, k)
        s[name].wait(e, (base, d), k)

    def wait(e, name, at, d, k=None):
        if not (at.first and d < 0):
            wait_once(e, name, at.tile, d, k)

    def waitf(e, name, at, k=None, d=-1):
        wait_once(e, name, at.u, d, k)

    def inc(i, name, n=1):
        return i.then_inc(s[name].sem, n)

    class Ring:

        def __init__(self):
            self.n, self.last = 0, [None] * NR

        def take(self, at):
            r = self.n % NR
            self.n += 1
            if self.last[r]:
                kind, name, d, k = self.last[r]
                if kind == "tile":
                    wait(pe, name, at, d, k)
                else:
                    waitf(pe, name, at, k, d)
            self.last[r] = None
            return r

        def read(self, r, name, d, k, kind="tile"):
            self.last[r] = (kind, name, d, k)

        def next_step(self):
            self.last = [x and (x[0], x[1], x[2] - (B if x[0] == "tile" else 1), x[3]) for x in self.last]

    ring = Ring()
    hc = D // 2

    def read_input(at, t, prev):
        if prev is not None:
            wait(dve, "xT", at, prev)
        inc(dve.tensor_scalar_mul(xin[:, :, :], X[:, :, t, :], 1.0), "xi")

    def rotary_table(at):
        wait(dve, "t2", at, -1)
        inc(dve.tensor_tensor(out=tab[:, :, :, :], in0=rope[:, at.t, :, :, :], in1=qks[:, at.par, :, :, :],
                              op=ALU.mult), "tab")

    def halo_x(at, d, t):
        b = d % B
        wait(dve, "vp", at, d - B)
        wait(dve, "xl", at, d - B)
        inc(dve.tensor_scalar(XS[:, b, :, 0:WIN + 1], XS[:, b, :, P:P + WIN + 1].bitcast(F32), begun[:, bass.ds(t, 1)], None,
                              ALU.mult), "hal")

    def input_T(at, d):
        b = d % B
        r = ring.take(at)
        waitf(pe, "xi", at, d=d // B)
        inc(pe.transpose(R[:, r, 0:P], xin[:, b, :], ident[:, :]), "xT")
        wait(act, "hal", at, d)
        wait(act, "xT", at, d)
        shifted = ((slice(0, hc), WIN), (slice(hc, D), WIN + 1))
        for c_, o in shifted:
            inc(act.activation(XS[c_, b, 0, o:o + P], R[c_, r, 0:P], ACT.Copy), "xs")
        wait(dve, "xs", at, d)
        for c_, o in shifted:
            inc(dve.tensor_tensor(out=XS[c_, b, 1, o:o + P], in0=R[c_, r, 0:P],
                                  in1=XS[c_, b, 0, o:o + P].bitcast(F32), op=ALU.subtract), "xl")
        ring.read(r, "xl", d, 2)

    def project(at, d, rows, bank, tokens, cols):
        for n, (i, j) in enumerate(((0, 0), (0, 1), (1, 0))):
            mm = pe.matmul(R[0:rows, bank, :], XS[:, d % B, i, tokens:tokens + rows],
                           Wqkv[:, at.parity(d), j, cols:cols + 512], start=(n == 0), stop=(n == 2))
        return mm

    def split_next(at):
        cols = bass.ds(at.t * share, share)
        part = [Wqkv[:, (at.layer + 1) % 2, j, cols] for j in range(2)]
        s_wr.wait(dve, (at.u, 0))
        inc(dve.tensor_scalar_mul(part[0], Wraw[:, :], 1.0), "wsp")
        waitf(dve, "wsp", at, 1, 0)
        inc(dve.tensor_tensor(out=part[1], in0=Wraw[:, :], in1=part[0].bitcast(F32), op=ALU.subtract), "wsp")

    def project_qk(at, d, js):
        b = d % B
        wait(pe, "xl", at, d)
        for j in js:
            r = ring.take(at)
            inc(project(at, d, P, r, WIN, j * 512), "qk")
            wait(act, "qk", at, d, j + 1)
            if j == 0:
                wait(act, "t2", at, d - 1)
                wait(act, "sq", at, d - 1)
            inc(act.activation(QK[:, j * 512:(j + 1) * 512], R[:, r, :], ACT.Copy), "qke")
            ring.read(r, "qke", d, j + 1)

    def view_qk(a):
        return a.rearrange("p (i h e) -> p i h e", i=2, e=LD)

    def square(at, d):
        wait(act, "qke", at, d)
        wait(act, "ss", at, d - 1, 1)
        inc(act.activation(SQ[:, :], QK[:, :], ACT.Square), "sq")

    def rotate_cos(at, d):
        wait(dve, "qke", at, d)
        wait(dve, "tq", at, d - 2)
        waitf(dve, "tab", at, d=0)
        inc(dve.tensor_tensor(out=view_qk(T1[:, d % 2, :]), in0=view_qk(QK[:, :]),
                              in1=tab[:, 0].unsqueeze(2).broadcast_to([P, 2, LH, LD]), op=ALU.mult), "t1")

    def rotate_sin(at, d):
        p, hf = d % 2, LD // 2
        q, t2 = view_qk(QK[:, :]), view_qk(T2[:, :])
        wait(dve, "ad", at, d - 1)
        for j in range(2):
            i = dve.tensor_tensor(out=t2[:, :, :, j * hf:(j + 1) * hf], in0=q[:, :, :, (1 - j) * hf:(2 - j) * hf],
                                  in1=tab[:, 1, :, j * hf:(j + 1) * hf].unsqueeze(2).broadcast_to([P, 2, LH, hf]),
                                  op=ALU.mult)
        inc(i, "t2")
        wait(pool, "t2", at, d)
        inc(pool.tensor_tensor(out=T1[:, p, :], in0=T1[:, p, :], in1=T2[:, :], op=ALU.add), "ad")

    def norms(at, d):
        p = d % 2
        wait(dve, "sq", at, d)
        inc(dve.reduce_sum(ss[:, p, :], SQ[:, :].rearrange("p (h e) -> p h e", e=LD), axis=AX.X), "ss")
        wait(dve, "ss", at, d, 1)
        inc(dve.tensor_scalar_max(ss[:, p, :], ss[:, p, :], 1e-24), "ss")
        wait(pool, "ss", at, d, 2)
        inc(pool.tensor_tensor(out=rn[:, p, :], in0=ss[:, p, :], in1=power[:, :], op=ALU.pow), "pw")

    def normalise(at, d):
        p = d % 2
        wait(dve, "ad", at, d)
        wait(dve, "pw", at, d)
        t1 = T1[:, p, :].rearrange("p (h e) -> p h e", e=LD)
        inc(dve.tensor_tensor(out=t1, in0=t1, in1=rn[:, p, :].unsqueeze(2).broadcast_to([P, 2 * LH, LD]),
                              op=ALU.mult), "no")

    def halo_k(at, d):
        b = d % B
        wait(dve, "s", at, d - 1)
        wait(dve, "te", at, d - B)
        inc(dve.tensor_scalar(kT[:, :, 0:WIN], kH[:, b, :, :], begun[:, bass.ds(at.time(d), 1)], None,
                              ALU.mult), "kh")

    def transpose_qk(at, d):
        b, p = d % B, d % 2
        wait(pe, "no", at, d)
        for j in range(4):
            r = ring.take(at)
            for i in range(4):
                mm = pe.transpose(R[:, r, i * P:(i + 1) * P], T1[:, p, (4 * j + i) * P:(4 * j + i + 1) * P], ident[:, :])
            inc(mm, "tq")
            wait(act, "tq", at, d, j + 1)
            src = R[:, r, :].rearrange("p (i n) -> p i n", i=4)
            if j < 2:
                inc(act.activation(qT[:, 4 * j:4 * j + 4, :], src, ACT.Copy), "te")
                ring.read(r, "te", d, j + 1)
            else:
                wait(act, "kh", at, d)
                h = slice(4 * j - 8, 4 * j - 4)
                inc(act.activation(kT[:, h, WIN:WIN + P], src, ACT.Copy), "te")
                inc(act.activation(kH[:, b, h, :], src[:, :, P - WIN:P], ACT.Copy), "te")
                ring.read(r, "te", d, 2 * j)

    def scores(at, d, hf):
        b, p = d % B, d % 2
        wait(pe, "te", at, d)
        wait(pe, "kh", at, d)
        wait(pe, "sub", at, d - 1, hf + 1)
        for par in range(2):
            bank, o = 2 * hf + par, par * LD
            pe.matmul(PS[:, bank, 0:4 * KB], ident_b[:, :], mask[:, at.later(d), :], start=True, stop=False,
                      skip_group_check=True)
            for g in range(2):
                for j in range(4):
                    pair = 4 * hf + j
                    mm = pe.matmul(PS[g * QB:(g + 1) * QB, bank, j * KB:(j + 1) * KB],
                                   qT[o:o + LD, pair, g * QB:(g + 1) * QB],
                                   kT[o:o + LD, pair, g * QB:g * QB + KB],
                                   start=False, stop=True, skip_group_check=True)
        inc(mm, "s")
        view = PS[:, 2 * hf:2 * hf + 2, 0:4 * KB].rearrange("p a (j k) -> p a j k", k=KB)
        m = mx[:, p, 8 * hf:8 * hf + 8].rearrange("p (a j) -> p a j", a=2)
        e = E[:, p, 8 * hf:8 * hf + 8, :].rearrange("p (a j) k -> p a j k", a=2)
        wait(dve, "s", at, d, hf + 1)
        inc(dve.reduce_max(m, view, axis=AX.X), "mx")
        wait(dve, "mx", at, d, hf + 1)
        if hf == 0:
            wait(dve, "pt", at, d - 2)
        inc(dve.tensor_tensor(out=e, in0=view, in1=m.unsqueeze(3).broadcast_to([P, 2, 4, KB]),
                              op=ALU.subtract), "sub")

    def exponentials(at, d, hf):
        wait(act, "sub", at, d, hf + 1)
        e = E[:, d % 2, 8 * hf:8 * hf + 8, :]
        inc(act.activation(e, e, ACT.Exp), "ex")

    def divide(at, d):
        p = d % 2
        wait(dve, "ex", at, d)
        inc(dve.reduce_sum(sm[:, p, 0, :], E[:, p, :, :], axis=AX.X), "sum")
        wait(dve, "sum", at, d)
        wait(dve, "pn", at, d - 2)
        inc(dve.reciprocal(sm[:, p, 1, :], sm[:, p, 0, :]), "rc")
        wait(pool, "rc", at, d)
        inc(pool.tensor_tensor(out=E[:, p, :, :], in0=E[:, p, :, :],
                               in1=sm[:, p, 1, :].unsqueeze(2).broadcast_to([P, LH, KB]), op=ALU.mult), "pn")

    def project_v(at, d):
        b = d % B
        for j in range(4):
            g, half = divmod(j, 2)
            r = ring.take(at)
            inc(project(at, d, KB, r, g * QB, 2 * INNER + half * 512), "vp")
            wait(act, "vp", at, d, j + 1)
            inc(act.activation(V[:, g, half * 512:(half + 1) * 512], R[0:KB, r, :], ACT.Copy), "ve")
            ring.read(r, "ve", d, j + 1)

    def transpose_e(at, d):
        p = d % 2
        wait(pe, "pn", at, d)
        for j in range(4):
            r = ring.take(at)
            for i in range(4):
                mm = pe.transpose(R[0:KB, r, i * P:(i + 1) * P], E[:, p, 4 * j + i, :], ident[:, :])
            inc(mm, "pt")
            wait(act, "pt", at, d, j + 1)
            inc(act.activation(ET[:, 4 * j:4 * j + 4, :], R[0:KB, r, :].rearrange("p (i n) -> p i n", i=4),
                               ACT.Copy), "pe")
            ring.read(r, "pe", d, j + 1)

    def attend(at, d):
        wait(pe, "ve", at, d)
        for hf in range(2):
            wait(pe, "pe", at, d, 2 * hf + 2)
            r = ring.take(at)
            for j in range(4):
                pair = 4 * hf + j
                for g in range(2):
                    for par in range(2):
                        mm = pe.matmul(R[par * LD:(par + 1) * LD, r, j * P + g * QB:j * P + (g + 1) * QB],
                                       V[:, g, (2 * pair + par) * LD:(2 * pair + par + 1) * LD],
                                       ET[:, 8 * hf + 4 * par + j, g * QB:(g + 1) * QB], start=True, stop=True,
                                       skip_group_check=True)
            inc(mm, "pv")
            wait(act, "pv", at, d, hf + 1)
            inc(act.activation(OT[:, 4 * hf:4 * hf + 4, :], R[:, r, :].rearrange("p (j n) -> p j n", j=4),
                               ACT.Copy), "oe")
            ring.read(r, "oe", d, hf + 1)

    def output(at, d):
        b = d % B
        r = ring.take(at)
        for pair in range(LH // 2):
            wait(pe, "oe", at, d, pair // 4 + 1)
            mm = pe.matmul(R[:, r, 0:D], OT[:, pair, :], Wo[:, at.parity(d), pair, :], start=(pair == 0),
                           stop=(pair == LH // 2 - 1))
        inc(mm, "wo")
        wait(dve, "wo", at, d)
        t = at.time(d)
        inc(dve.tensor_tensor(out=x1[:, b, :], in0=R[:, r, 0:D], in1=X[:, b, t, :], op=ALU.add), "x1")
        ring.read(r, "x1", d, 1)
        wait(dve, "x1", at, d, 1)
        inc(dve.tensor_scalar_mul(X[:, b, t, :], x1[:, b, :], 1.0), "x1")

    def ff_carry(at, d):
        if type(at.u) is not int or at.u + d > 0:
            waitf(dve, "f2", at, None, d - 1)
            waitf(dve, "f1e", at, None, d - 1)
        inc(dve.tensor_scalar(FS[hc:D, :, 0:1], FS[hc:D, :, P:P + 1], begun[hc:D, bass.ds(at.before(d), 1)], None,
                              ALU.mult), "fc")

    def ff_shift(at, d):
        r = ring.take(at)
        wait(pe, "x1", at, B * d + B - 1, 2)
        for b in range(B):
            mm = pe.transpose(R[:, r, b * P:(b + 1) * P], x1[:, b, :], ident[:, :])
        inc(mm, "f1")
        waitf(act, "fc", at, None, d)
        waitf(act, "f1", at, None, d)
        src = R[:, r, :].rearrange("p (b n) -> p b n", b=B)
        inc(act.activation(FS[0:hc, :, 0:P], src[0:hc], ACT.Copy), "f1e")
        inc(act.activation(FS[hc:D, :, 1:P + 1], src[hc:D], ACT.Copy), "f1e")
        ring.read(r, "f1e", d, 2, "step")

    def ff_tokens(at, d):
        waitf(pe, "f1e", at, None, d)
        waitf(pe, "fc", at, None, d)
        r = ring.take(at)
        for b in range(B):
            mm = pe.transpose(R[:, r, b * P:(b + 1) * P], FS[:, b, 0:P], ident[:, :])
        inc(mm, "f2")
        waitf(dve, "f2", at, None, d)
        inc(dve.tensor_copy(fx[:, :, :], R[:, r, :].rearrange("p (b n) -> p b n", b=B)), "f2e")
        ring.read(r, "f2e", d, 1, "step")

    def ff_stats(at, d):
        waitf(dve, "f2e", at, None, d)
        for b in range(B):
            i = dve.bn_stats(fst[:, b, :], fx[:, b, :])
        inc(i, "fst")
        waitf(dve, "fst", at, 1, d)
        dve.memset(spare[:, :], 0.0)
        for b in range(B):
            i = dve.bn_aggr(fmv[:, b, :], fst[:, b, :])
        inc(i, "fst")
        waitf(dve, "fst", at, 2, d)
        inc(dve.tensor_scalar_add(fmv[:, :, 1:2], fmv[:, :, 1:2], LN_EPS), "fst")
        waitf(pool, "fst", at, 3, d)
        inc(pool.tensor_tensor(out=frs[:, :], in0=fmv[:, :, 1], in1=power[:, 0:B], op=ALU.pow), "frs")

    def ff_scale(at, d):
        waitf(dve, "frs", at, None, d)
        for b in range(B):
            i = dve.tensor_scalar(fx[:, b, :], fx[:, b, :], fmv[:, b, 0:1], frs[:, b:b + 1],
                                  ALU.subtract, ALU.mult)
        inc(i, "fn")

    def ff_norm(at, d):
        for e in (pe, act, dve):
            if isinstance(at.u, int):
                s_wf.wait(e, (at.u + d) // NT)
            else:
                s_wf.wait(e, ((at.u + (NT + d)) // NT, -1))
        waitf(pe, "fn", at, None, d)
        r = ring.take(at)
        for b in range(B):
            mm = pe.transpose(R[:, r, b * P:(b + 1) * P], fx[:, b, :], ident[:, :])
        inc(mm, "f3")
        waitf(act, "f3", at, None, d)
        inc(act.activation(fnT[:, :], R[:, r, :], ACT.Identity, bias=ln[:, 1:2], scale=ln[:, 0:1]), "f3e")
        ring.read(r, "f3e", d, 1, "step")

    def ff_up(at, d):
        waitf(pe, "f3e", at, None, d)
        for i, (lo, w) in enumerate(CH):
            rg = ring.take(at)
            inc(pe.matmul(R[0:w, rg, :], W1[:, FF + lo:FF + lo + w], fnT[:, :], start=True, stop=True), "ff")
            ra = ring.take(at)
            inc(pe.matmul(R[0:w, ra, :], W1[:, lo:lo + w], fnT[:, :], start=True, stop=True), "ff")
            waitf(act, "ff", at, 2 * i + 1, d)
            if i > 1:
                waitf(act, "hh", at, i - 1, d)
            inc(act.activation(G[0:w, i % 2, :], R[0:w, rg, :], ACT.Gelu, bias=b1[0:w, 1, i:i + 1]), "g")
            ring.read(rg, "g", d, i + 1, "step")
            waitf(dve, "ff", at, 2 * i + 2, d)
            waitf(dve, "g", at, i + 1, d)
            inc(dve.scalar_tensor_tensor(HH[0:w, i, :], R[0:w, ra, :], b1[0:w, 0, i:i + 1], G[0:w, i % 2, :],
                                         ALU.add, ALU.mult), "hh")
            ring.read(ra, "hh", d, i + 1, "step")

    def ff_down(at, d):
        waitf(pe, "hh", at, None, d)
        r = ring.take(at)
        for b in range(B):
            for i, (lo, w) in enumerate(CH):
                w += (i == len(CH) - 1)
                mm = pe.matmul(R[:, r, b * P:(b + 1) * P], HH[0:w, i, b * P:(b + 1) * P], W2[0:w, i, :],
                               start=(i == 0), stop=(i == len(CH) - 1))
        inc(mm, "f5")
        waitf(dve, "f5", at, None, d)
        xt = X[:, :, at.before(d), :]
        inc(dve.tensor_tensor(out=xt, in0=xt, in1=R[:, r, :].rearrange("p (b n) -> p b n", b=B),
                              op=ALU.add), "fx")
        ring.read(r, "fx", d, 1, "step")
        ring.n += 2

    def step(at, new=True, slots=B, ff=2):
        waited.clear()
        for d in range(slots):
            mid = (d >= 2 or not at.first) and (new or d < 2)
            after = (d >= 1 or not at.first) and (new or d < 1)
            old = (d >= 3 or not at.first) and (new or d < 3)

            def feed_forward(slot, part, before, banks=1):
                if d == slot:
                    if ff >= before:
                        part(at, -before)
                    else:
                        ring.n += banks

            if new and d == B - 1:
                read_input(at, at.t_next, d)
            if old:
                project_v(at, d - 3)
            else:
                ring.n += 4
            feed_forward(3, ff_shift, 1)
            feed_forward(0, ff_norm, 2)
            feed_forward(1, ff_up, 2, 6)
            if mid:
                scores(at, d - 2, 0)
            feed_forward(3, ff_tokens, 1)
            if mid:
                scores(at, d - 2, 1)
                exponentials(at, d - 2, 0)
            feed_forward(3, ff_stats, 1, 0)
            if after:
                normalise(at, d - 1)
            if new and d == 0:
                for e in (pe, dve):
                    s_wa.wait(e, (at.layer, 0))
                if not at.first:
                    waitf(pe, "wsp", at, None, -1)
            if new:
                project_qk(at, d, (0, 1))
            else:
                ring.n += 2
            if mid:
                exponentials(at, d - 2, 1)
                divide(at, d - 2)
            if new:
                project_qk(at, d, (2,))
            else:
                ring.n += 1
            if old:
                transpose_e(at, d - 3)
            else:
                ring.n += 4
            if after:
                halo_k(at, d - 1)
            feed_forward(2, ff_down, 2, 3)
            if new:
                project_qk(at, d, (3,))
                if d == 0:
                    rotary_table(at)
                rotate_cos(at, d)
            else:
                ring.n += 1
            if new:
                rotate_sin(at, d)
                square(at, d)
            feed_forward(3, ff_scale, 1, 0)
            if old:
                attend(at, d - 3)
            else:
                ring.n += 2
            if after:
                transpose_qk(at, d - 1)
            else:
                ring.n += 4
            if new:
                halo_x(at, d + 1, at.t if d < B - 1 else at.t_next)
            if old:
                output(at, d - 3)
            else:
                ring.n += 1
            if new:
                input_T(at, d + 1)
            else:
                ring.n += 1
            feed_forward(2, ff_carry, 1, 0)
            if new:
                norms(at, d)
            if new and d == B - 1:
                split_next(at)
        ring.next_step()

    sp.dma_start(rope[:, :, :, :, :], ins["rope"]).then_inc(s_c.sem, 16)
    sp.dma_start(mask[:, :, :], ins["mask"]).then_inc(s_c.sem, 16)
    first_w = T1[:, :, :].rearrange("p a n -> p (a n)")[:, 0:3 * INNER]
    sp.dma_start(first_w, ins["Wqkv"][0]).then_inc(s_w0.sem, 16)
    load_attention(0, 0)
    load_ff(0)
    pool.memset(power[:, :], -0.5).then_inc(s_one.sem, 1)
    pool.memset(kH[:, :, :, :], 0.0).then_inc(s_one.sem, 1)
    pool.memset(FS[:, :, :], 0.0).then_inc(s_one.sem, 1)
    pool.memset(begun[:, 0:1], 0.0).then_inc(s_one.sem, 1)
    pool.memset(begun[:, 1:NT], 1.0).then_inc(s_one.sem, 1)
    pool.wait_ge(s_one.sem, 5)
    lo = LASTW // 32 * 32
    pool.memset(HH[lo:lo + 32, len(CH) - 1, :], 1.0).then_inc(s_one.sem, 1)
    dve.wait_ge(s_one.sem, 6)
    for j in range(2):
        dve.tensor_scalar_mul(XS[:, :, j, P:P + WIN + 1], FS[:, :, 0:WIN + 1], 1.0).then_inc(s_one.sem, 1)
    for e in (pool, dve, act, pe):
        e.wait_ge(s_one.sem, 8)
    for e in (pe, dve):
        s_c.wait(e, 0)

    steps = NL * NT
    read_input(At(0, True), 0, None)
    s_w0.wait(dve, 0, 16)
    dve.tensor_scalar_mul(Wqkv[:, 0, 0, :], first_w, 1.0).then_inc(s_w0.sem, 1)
    s_w0.wait(dve, 0, 17)
    dve.tensor_tensor(out=Wqkv[:, 0, 1, :], in0=first_w, in1=Wqkv[:, 0, 0, :].bitcast(F32),
                      op=ALU.subtract).then_inc(s_w0.sem, 1)
    for e in (pe, dve):
        s_w0.wait(e, 0)
    halo_x(At(0, True), 0, 0)
    input_T(At(0, True), 0)
    step(At(0, True), ff=0)
    step(At(1), ff=1)
    start = (ring.n % NR, list(ring.last))
    with nc.Fori(2, steps, engines=[e.engine for e in (pe, act, dve, pool)]) as u:
        step(At(u))
        assert start == (ring.n % NR, ring.last), (start, ring.n % NR, ring.last)
    end = At(steps)
    step(end, new=False, slots=3)
    ring.last = [x and (x[0], x[1], x[2] + (B if x[0] == "tile" else 1), x[3]) for x in ring.last]
    for part in (ff_shift, ff_tokens, ff_stats, ff_scale, ff_norm, ff_up, ff_down):
        part(end, -1)

    def reload_ff(l):
        if isinstance(l, int):
            sp.wait_ge(s["f5"].sem, s["f5"].at(l * NT - 1))
        else:
            s["f5"].wait(sp, (l * NT, -1))
        load_ff(l)

    def load_share(l, t, following):
        u = l * NT + t
        if isinstance(u, int):
            if u > 0:
                s["wsp"].wait(sp, u - 1)
        else:
            s["wsp"].wait(sp, (u, -1))
        cols = slice(t * share, (t + 1) * share) if isinstance(t, int) else bass.ds(t * share, share)
        sp.dma_start(Wraw[:, :], ins["Wqkv"][following][:, cols]).then_inc(s_wr.sem, 16)

    def reload(l, following):
        load_share(l, 0, following)
        if isinstance(l, int):
            if l > 0:
                sp.wait_ge(s["wo"].sem, s["wo"].at(l * NT * B - 1))
        else:
            s["wo"].wait(sp, (l * (NT * B), -1))
        s_wa.wait(sp, (l, 0))
        if not (isinstance(l, int) and l == last):
            load_attention(following, (l + 1) % 2)
        load_share(l, 1, following)
        if not (isinstance(l, int) and l == 0):
            reload_ff(l)
        with nc.Fori(2, NT, engines=[sp.engine]) as t:
            load_share(l, t, following)

    last = NL - 1
    reload(0, 1)
    with nc.Fori(1, last, engines=[sp.engine]) as l:
        reload(l, l + 1)
    reload(last, 0)
    s_wr.wait(sp, NL * NT - 1)
    nc.all_engine_barrier()
    c.close()


def tables():
    f32 = np.float32
    half = np.arange(0, LD, 2, dtype=f32)
    inv = (f32(1.0) / np.power(f32(10000.0), half / f32(LD))).astype(f32)
    t = np.arange(S, dtype=f32)
    fr = (t[:, None] * inv[None, :]).astype(f32)
    fr = np.concatenate([fr, fr], -1)
    base = ((half + f32(0.4 * LD)) / f32(1.4 * LD)).astype(f32)
    power = ((t - S // 2) / (WIN // 2)).astype(f32)
    sc = np.power(base[None, :], power[:, None]).astype(f32)
    sc = np.concatenate([sc, sc], -1)
    cos, sin = np.cos(fr).astype(f32), np.sin(fr).astype(f32)
    sign = np.where(np.arange(LD) < LD // 2, f32(-1), f32(1))
    q_k = []
    for scale in (sc * f32(8.0), (f32(1.0) / sc).astype(f32)):
        q_k.append(np.stack([cos * scale, sin * sign * scale]))
    r = np.stack(q_k, 2)
    rope = np.ascontiguousarray(r.reshape(2, NT, P, 2, LD).transpose(2, 1, 0, 3, 4)).astype(f32)
    q = np.arange(P)
    k = np.arange(KB)
    i = q[:, None] % QB
    ok = (k[None, :] >= i) & (k[None, :] <= i + WIN)
    m = np.zeros((P, 2, 4, KB), f32)
    m[~np.broadcast_to(ok[:, None, None, :], m.shape)] = MASKED
    pad = (q[:, None] < QB) & (k[None, :] < WIN)
    m[:, 0][np.broadcast_to(pad[:, None, :], (P, 4, KB))] = MASKED
    return rope, m.reshape(P, 2, 4 * KB)


def kernel(**inputs):
    import concourse.bacc as bacc
    from concourse.bass_utils import run_bass_kernel_spmd

    a = {k: np.asarray(v) for k, v in inputs.items()}
    rope, mask = tables()
    arrays = {
        "X": a["L0_attn_X"], "wqT": a["L0_attn_Wq"].T, "wkT": a["L0_attn_Wk"].T, "wvT": a["L0_attn_Wv"].T,
        "woT": a["L0_attn_Wo"].T, "bq": a["L0_attn_bq"].reshape(D, 1), "bk": a["L0_attn_bk"].reshape(D, 1),
        "bv": a["L0_attn_bv"].reshape(1, D), "bo": a["L0_attn_bo"].reshape(1, D),
        "Wqkv": a["L0_ffn_Wqkv"], "q_scale": a["L0_ffn_q_scale"], "k_scale": a["L0_ffn_k_scale"],
        "qk_scale": np.stack([a["L0_ffn_q_scale"], a["L0_ffn_k_scale"]], 1),
        "Wo": a["L0_ffn_Wo"], "ln_g": a["L0_ffn_ln_g"], "ln_b": a["L0_ffn_ln_b"], "W1": a["L0_ffn_W1"],
        "b1": a["L0_ffn_b1"], "W2": a["L0_ffn_W2"], "b2": a["L0_ffn_b2"], "cT": a["L0_c"].T,
        "wmod": a["L0_wmod"], "rope": rope, "mask": mask.astype(mybir.dt.np(BF16)),
    }
    arrays = {k: np.ascontiguousarray(v) for k, v in arrays.items()}
    nc = bacc.Bacc("TRN2", target_bir_lowering=False, num_devices=1)
    ins = {k: nc.dram_tensor(f"in_{k}", v.shape, mybir.dt.from_np(v.dtype), kind="ExternalInput").ap()
           for k, v in arrays.items()}
    out = nc.dram_tensor("out", (B, S, D), F32, kind="ExternalOutput").ap()
    build(nc, ins, out)
    r = run_bass_kernel_spmd(nc, [{f"in_{k}": v for k, v in arrays.items()}], core_ids=[0])
    return r.results[0]["out"]
```
